# Optimizing a Trainium2 kernel written in Bass

```python
import numpy as np
import jax
import jax.numpy as jnp

def _softmax(x, axis=-1):
    return jax.nn.softmax(x, axis=axis)

def _gelu(x):
    return jax.nn.gelu(x, approximate=True)

def _silu(x):
    return jax.nn.silu(x)

def _sigmoid(x):
    return jax.nn.sigmoid(x)

def _layernorm(x, axis=-1, eps=1e-05):
    m = jnp.mean(x, axis=axis, keepdims=True)
    v = jnp.var(x, axis=axis, keepdims=True)
    return (x - m) / jnp.sqrt(v + eps)

def _scatter_add(tgt, idx, src, axis=0):
    return tgt.at[idx].add(src)

def _segment_sum(src, seg, n):
    return jax.ops.segment_sum(src, seg, n)
kernel_name = 'mk_seq_preln_d1_jaxref_r8_37118f'

def setup_inputs(seed: int=0):
    np.random.seed(seed)
    _w = jnp.asarray

    def _L0_attn_setup():
        import jax, jax.numpy as jnp
        import numpy as np
        B, T, D = (4, 512, 128)
        H, LH, DH, BUCKETS = (16, 4, 64, 64)

        def _merge_heads(v, h):
            b, t, hd = v.shape
            return v.reshape(b, t, h, hd // h).transpose(0, 2, 1, 3)

        def _bucketed(z, nb):
            Bz, Tz, Dz = z.shape
            return z.reshape(Bz, nb, Tz // nb, Dz)

        def _look_around(z, pad_value):
            pad = [(0, 0)] * z.ndim
            pad[1] = (1, 1)
            p = jnp.pad(z, pad, constant_values=pad_value)
            nb = z.shape[1]
            return jnp.concatenate([p[:, i:i + nb] for i in range(3)], axis=2)
        key = jax.random.key(seed)
        ks = jax.random.split(key, 6)
        x = jax.random.normal(ks[0], (B, T, D), jnp.float32)
        w_q = jax.random.normal(ks[1], (D, H * DH), jnp.float32) * 0.02
        w_kv = jax.random.normal(ks[2], (D, 2 * H * DH), jnp.float32) * 0.02
        w_out = jax.random.normal(ks[3], (H * DH, D), jnp.float32) * 0.02
        b_out = jnp.zeros((D,), jnp.float32)
        sort_w = jax.random.normal(ks[4], (1, H - LH, 2 * DH, BUCKETS), jnp.float32)
        return dict(x=x, w_q=w_q, w_kv=w_kv, w_out=w_out, b_out=b_out, sort_w=sort_w)
    _L0_attn_in = _L0_attn_setup()

    def _L0_ffn_setup():
        import math
        import jax, jax.numpy as jnp
        import numpy as np
        HIDDEN = 128
        INTER = 512
        EXPERTS = 8
        B, T = (4, 256)
        EPS = 1e-12
        CAP_FACTOR = 1.0
        MIN_CAP = 4

        def layer_norm(x, g, b, eps=EPS):
            m = jnp.mean(x, axis=-1, keepdims=True)
            v = jnp.var(x, axis=-1, keepdims=True)
            return (x - m) * jax.lax.rsqrt(v + eps) * g + b

        def top1_gate(x, wg, capacity):
            logits = x @ wg
            gates = jax.nn.softmax(logits, axis=-1)
            E = wg.shape[-1]
            idx = jnp.argmax(gates, axis=-1)
            mask1 = jax.nn.one_hot(idx, E, dtype=gates.dtype)
            locations = jnp.cumsum(mask1, axis=0) - mask1
            mask1 = mask1 * (locations < capacity).astype(gates.dtype)
            gates1_s = jnp.sum(gates * mask1, axis=-1)
            loc_s = jnp.sum(locations * mask1, axis=-1).astype(jnp.int32)
            loc_oh = jax.nn.one_hot(loc_s, capacity, dtype=gates.dtype)
            combine = gates1_s[:, None, None] * mask1[:, :, None] * loc_oh[:, None, :]
            dispatch = jax.lax.stop_gradient((combine > 0).astype(x.dtype))
            return (combine, dispatch)
        key = jax.random.key(seed)
        ks = jax.random.split(key, 8)
        s = 0.02
        return {'x': jax.random.normal(ks[0], (B, T, HIDDEN), jnp.float32), 'attn_nw': jnp.ones((HIDDEN,), jnp.float32), 'attn_nb': jnp.zeros((HIDDEN,), jnp.float32), 'wg': jax.random.normal(ks[1], (HIDDEN, EXPERTS), jnp.float32) * s, 'inter_w': jax.random.normal(ks[2], (EXPERTS, HIDDEN, INTER), jnp.float32) * s, 'inter_b': jnp.zeros((EXPERTS, INTER), jnp.float32), 'output_w': jax.random.normal(ks[3], (EXPERTS, INTER, HIDDEN), jnp.float32) * s, 'output_b': jnp.zeros((EXPERTS, HIDDEN), jnp.float32), 'res_inter_w': jax.random.normal(ks[4], (HIDDEN, INTER), jnp.float32) * s, 'res_inter_b': jnp.zeros((INTER,), jnp.float32), 'res_output_w': jax.random.normal(ks[5], (INTER, HIDDEN), jnp.float32) * s, 'res_output_b': jnp.zeros((HIDDEN,), jnp.float32), 'res_coef': jax.random.normal(ks[6], (HIDDEN, 2), jnp.float32) * s}
    _L0_ffn_in = _L0_ffn_setup()
    _d = {'L0_attn_x': _L0_attn_in['x'], 'L0_attn_w_q': _L0_attn_in['w_q'], 'L0_attn_w_kv': _L0_attn_in['w_kv'], 'L0_attn_w_out': _L0_attn_in['w_out'], 'L0_attn_b_out': _L0_attn_in['b_out'], 'L0_attn_sort_w': _L0_attn_in['sort_w'], 'L0_ffn_attn_nw': _L0_ffn_in['attn_nw'], 'L0_ffn_attn_nb': _L0_ffn_in['attn_nb'], 'L0_ffn_wg': _L0_ffn_in['wg'], 'L0_ffn_inter_w': _L0_ffn_in['inter_w'], 'L0_ffn_inter_b': _L0_ffn_in['inter_b'], 'L0_ffn_output_w': _L0_ffn_in['output_w'], 'L0_ffn_output_b': _L0_ffn_in['output_b'], 'L0_ffn_res_inter_w': _L0_ffn_in['res_inter_w'], 'L0_ffn_res_inter_b': _L0_ffn_in['res_inter_b'], 'L0_ffn_res_output_w': _L0_ffn_in['res_output_w'], 'L0_ffn_res_output_b': _L0_ffn_in['res_output_b'], 'L0_ffn_res_coef': _L0_ffn_in['res_coef']}
    _x0 = _d['L0_attn_x']
    _d['L0_attn_x'] = jax.random.normal(jax.random.fold_in(jax.random.key(seed), 1), (8, 512, 128), dtype=_x0.dtype)
    del _x0
    return _d

def reference(L0_attn_x, L0_attn_w_q, L0_attn_w_kv, L0_attn_w_out, L0_attn_b_out, L0_attn_sort_w, L0_ffn_attn_nw, L0_ffn_attn_nb, L0_ffn_wg, L0_ffn_inter_w, L0_ffn_inter_b, L0_ffn_output_w, L0_ffn_output_b, L0_ffn_res_inter_w, L0_ffn_res_inter_b, L0_ffn_res_output_w, L0_ffn_res_output_b, L0_ffn_res_coef):

    def _L0_attn_ref(x, w_q, w_kv, w_out, b_out, sort_w):
        import jax, jax.numpy as jnp
        import numpy as np
        B, T, D = (4, 512, 128)
        H, LH, DH, BUCKETS = (16, 4, 64, 64)

        def _merge_heads(v, h):
            b, t, hd = v.shape
            return v.reshape(b, t, h, hd // h).transpose(0, 2, 1, 3)

        def _bucketed(z, nb):
            Bz, Tz, Dz = z.shape
            return z.reshape(Bz, nb, Tz // nb, Dz)

        def _look_around(z, pad_value):
            pad = [(0, 0)] * z.ndim
            pad[1] = (1, 1)
            p = jnp.pad(z, pad, constant_values=pad_value)
            nb = z.shape[1]
            return jnp.concatenate([p[:, i:i + nb] for i in range(3)], axis=2)
        b, t, d = x.shape
        h, lh, dh, buckets = (H, LH, DH, BUCKETS)
        sh = h - lh
        w = t // buckets
        neg = -jnp.finfo(x.dtype).max
        q = _merge_heads(x @ w_q, h)
        k, v = jnp.split(x @ w_kv, 2, axis=-1)
        k = _merge_heads(k, h)
        v = _merge_heads(v, h)
        lq, sq = (q[:, :lh], q[:, lh:])
        lk, sk = (k[:, :lh], k[:, lh:])
        lv, sv = (v[:, :lh], v[:, lh:])
        B1 = b * lh
        blq = _bucketed(lq.reshape(B1, t, dh), buckets)
        blk = _look_around(_bucketed(lk.reshape(B1, t, dh), buckets), -1.0)
        blv = _look_around(_bucketed(lv.reshape(B1, t, dh), buckets), -1.0)
        ticker = jnp.arange(t, dtype=x.dtype).reshape(1, buckets, w)
        bq_k = _look_around(ticker, -1.0)
        dots = jnp.einsum('bnie,bnje->bnij', blq, blk)
        dots = jnp.where(bq_k[:, :, None, :] == -1.0, neg, dots)
        attn = jax.nn.softmax(dots, axis=-1)
        local_out = jnp.einsum('bnij,bnje->bnie', attn, blv).reshape(b, lh, t, dh)
        B2 = b * sh
        bq = _bucketed(sq.reshape(B2, t, dh), buckets)
        bk = _bucketed(sk.reshape(B2, t, dh), buckets)
        bv = _bucketed(sv.reshape(B2, t, dh), buckets)
        feats = jnp.concatenate([bq.sum(2), bk.sum(2)], axis=-1)
        W = jnp.broadcast_to(sort_w, (b, sh, 2 * dh, buckets)).reshape(B2, 2 * dh, buckets)
        R = jax.nn.relu(jnp.einsum('bud,bdv->buv', feats, W))
        R = jax.nn.softmax(R, axis=-1)
        bk_r = jnp.einsum('buv,bvtd->butd', R, bk)
        bv_r = jnp.einsum('buv,bvtd->butd', R, bv)
        bk2 = jnp.concatenate([bk_r, bk], axis=2)
        bv2 = jnp.concatenate([bv_r, bv], axis=2)
        dots2 = jnp.einsum('buie,buje->buij', bq, bk2) * dh ** (-0.5)
        attn2 = jax.nn.softmax(dots2, axis=-1)
        sink_out = jnp.einsum('buij,buje->buie', attn2, bv2).reshape(b, sh, t, dh)
        out = jnp.concatenate([local_out, sink_out], axis=1)
        out = out.transpose(0, 2, 1, 3).reshape(b, t, h * dh)
        return out @ w_out + b_out

    def _L0_ffn_ref(x, attn_nw, attn_nb, wg, inter_w, inter_b, output_w, output_b, res_inter_w, res_inter_b, res_output_w, res_output_b, res_coef):
        import math
        import jax, jax.numpy as jnp
        import numpy as np
        HIDDEN = 128
        INTER = 512
        EXPERTS = 8
        B, T = (4, 256)
        EPS = 1e-12
        CAP_FACTOR = 1.0
        MIN_CAP = 4

        def layer_norm(x, g, b, eps=EPS):
            m = jnp.mean(x, axis=-1, keepdims=True)
            v = jnp.var(x, axis=-1, keepdims=True)
            return (x - m) * jax.lax.rsqrt(v + eps) * g + b

        def top1_gate(x, wg, capacity):
            logits = x @ wg
            gates = jax.nn.softmax(logits, axis=-1)
            E = wg.shape[-1]
            idx = jnp.argmax(gates, axis=-1)
            mask1 = jax.nn.one_hot(idx, E, dtype=gates.dtype)
            locations = jnp.cumsum(mask1, axis=0) - mask1
            mask1 = mask1 * (locations < capacity).astype(gates.dtype)
            gates1_s = jnp.sum(gates * mask1, axis=-1)
            loc_s = jnp.sum(locations * mask1, axis=-1).astype(jnp.int32)
            loc_oh = jax.nn.one_hot(loc_s, capacity, dtype=gates.dtype)
            combine = gates1_s[:, None, None] * mask1[:, :, None] * loc_oh[:, None, :]
            dispatch = jax.lax.stop_gradient((combine > 0).astype(x.dtype))
            return (combine, dispatch)
        Bx, Tx, M = x.shape
        S = Bx * Tx
        E = wg.shape[-1]
        capacity = max(MIN_CAP, math.ceil(S / E * CAP_FACTOR))
        residual = x.reshape(S, M)
        attn_out = layer_norm(residual, attn_nw, attn_nb)
        combine, dispatch = top1_gate(attn_out, wg, capacity)
        dispatched = jnp.einsum('sec,sm->ecm', dispatch, attn_out)
        h = jax.nn.gelu(jnp.einsum('ecm,emi->eci', dispatched, inter_w) + inter_b[:, None, :], approximate=True)
        expert_out = jnp.einsum('eci,eim->ecm', h, output_w) + output_b[:, None, :]
        moe_out = jnp.einsum('sec,ecm->sm', combine, expert_out)
        rh = jax.nn.gelu(attn_out @ res_inter_w + res_inter_b, approximate=True)
        res_mlp_out = rh @ res_output_w + res_output_b
        coef = jax.nn.softmax(attn_out @ res_coef, axis=-1)
        out = res_mlp_out * coef[:, :1] + moe_out * coef[:, 1:]
        out = out + residual
        return out.reshape(Bx, Tx, M)
    x = L0_attn_x
    x = x + _L0_attn_ref(_layernorm(x, axis=-1), L0_attn_w_q, L0_attn_w_kv, L0_attn_w_out, L0_attn_b_out, L0_attn_sort_w)
    x = x + _L0_ffn_ref(_layernorm(x, axis=-1), L0_ffn_attn_nw, L0_ffn_attn_nb, L0_ffn_wg, L0_ffn_inter_w, L0_ffn_inter_b, L0_ffn_output_w, L0_ffn_output_b, L0_ffn_res_inter_w, L0_ffn_res_inter_b, L0_ffn_res_output_w, L0_ffn_res_output_b, L0_ffn_res_coef)
    return x

_drawn_inputs = setup_inputs


def setup_inputs(seed=0):
    import zlib

    import numpy as np

    out = dict(_drawn_inputs(seed))
    spreads = {'L0_attn_b_out': (0.0, 0.1),
     'L0_ffn_attn_nw': (1.0, 0.6),
     'L0_ffn_attn_nb': (0.0, 0.8),
     'L0_ffn_inter_b': (0.0, 0.8),
     'L0_ffn_output_b': (0.0, 0.8),
     'L0_ffn_res_inter_b': (0.0, 0.8),
     'L0_ffn_res_output_b': (0.0, 0.312)}
    factors = {'L0_attn_w_q': 3.21,
     'L0_attn_sort_w': 3.179,
     'L0_ffn_wg': 8.0,
     'L0_ffn_inter_w': 8.0,
     'L0_ffn_output_w': 8.0,
     'L0_ffn_res_inter_w': 4.0,
     'L0_ffn_res_output_w': 3.697,
     'L0_ffn_res_coef': 8.0}
    for name, (base, spread) in spreads.items():
        noise = np.random.default_rng([zlib.crc32(name.encode()), seed]).standard_normal(out[name].shape)
        drawn = base * np.exp(spread * noise) if base else spread * noise
        out[name] = jnp.asarray(drawn.astype(out[name].dtype))
    for name, factor in factors.items():
        out[name] = (out[name] * factor).astype(out[name].dtype)
    return out
```

```python
from contextlib import ExitStack

import concourse.bass as bass
from concourse import mybir

F32 = mybir.dt.float32
BF16 = mybir.dt.bfloat16
I32 = mybir.dt.int32
ALU = mybir.AluOpType
ACT = mybir.ActivationFunctionType
AX_X = mybir.AxisListType.X

P = 128
TILES = 32
D = 128
DH = 64
HEADS = 16
LOCAL_HEADS = 4
SORT_HEADS = HEADS - LOCAL_HEADS
BUCKETS = 64
W = 8
SEQ = BUCKETS * W
TURNS = 4
TOK = 2 * SEQ
CHUNKS = 4
UNITS = 16
GROUPS = 8
WIN = 10 * W
WIDE = 12 * W
PAD = W + SEQ + 3 * W
EXPERTS = 8
CAP = 512
INTER = 512
OUT_OF_SEQUENCE = -1.0e30


def view(t, part, nparts, offset, dims):
    row = t.shape[1]
    return bass.AP(tensor=t, offset=part * row + offset, ap=[[row, nparts]] + dims)


def layer_norm_steps(nc, link, x, stats, small, n, eps, var_ready, wait_root):
    for t in range(n):
        last = nc.vector.bn_stats(stats[:, 6 * t:6 * t + 6], x(t))
    link(last)
    st = stats[:, 0:6 * n].rearrange("p (t s) -> p s t", s=6)
    mean, rstd, a, b, v = (small[:, i * TILES:i * TILES + n] for i in range(5))
    nc.vector.tensor_tensor(a, st[:, 1, :], st[:, 4, :], ALU.add)
    nc.vector.tensor_tensor(b, st[:, 1, :], st[:, 4, :], ALU.subtract)
    link(nc.vector.tensor_tensor(v, st[:, 2, :], st[:, 5, :], ALU.add))
    nc.vector.tensor_scalar(mean, a, 0.5, None, ALU.mult)
    nc.vector.tensor_scalar(v, v, 1.0 / D, eps, ALU.mult, ALU.add)
    link(nc.vector.tensor_tensor(b, b, b, ALU.mult))
    nc.vector.scalar_tensor_tensor(v, b, 0.25, v, ALU.mult, ALU.add).then_inc(var_ready, 1)
    wait_root()
    link(nc.vector.reciprocal(rstd, a))
    link(nc.vector.tensor_tensor(b, rstd, rstd, ALU.mult))
    link(nc.vector.tensor_tensor(b, b, v, ALU.mult))
    link(nc.vector.tensor_scalar(b, b, -0.5, 1.5, ALU.mult, ALU.add))
    link(nc.vector.tensor_tensor(rstd, rstd, b, ALU.mult))


def evacuations():
    order = [(("feats", g), "act") for g in range(3)] + [(("logits", g), "dve") for g in range(2)]

    def chunk(c):
        order.extend((("v", c, n), "act") for n in range(4))
        order.extend((("k", c, n), "act") for n in range(4))
        if c:
            order.append((("rt", c), "act"))
        order.extend((("q", c, n), "act") for n in range(4))
        if c:
            order.extend((("kn", c, n), "act") for n in range(4))
            order.extend((("vr", c, n), "act") for n in range(4))
            order.extend((("kr", c, n), "act") for n in range(4))

    for i in range(UNITS + 4):
        if i % 4 == 0 and i < UNITS:
            chunk(i // 4)
        if i >= 7 and (i - 7) % 4 == 0:
            order.extend((("out", (i - 7) // 4, n), "dve") for n in range(2))
    count = {"act": 0, "dve": 0}
    jobs = {}
    for n, (name, eng) in enumerate(order):
        jobs[name] = (n, eng, count[eng])
        count[eng] += 1
    return jobs, count


def attention_block(nc, ctx, x_sb, A):
    def sb(name, cols, dt=F32):
        return ctx.enter_context(nc.sbuf_tensor(name, [P, cols], dt))

    def psum(name, cols):
        return ctx.enter_context(nc.psum_tensor(name, [P, cols], F32))

    def sem(name):
        return ctx.enter_context(nc.semaphore(name))

    JOBS, COUNT = evacuations()
    NJOBS = len(JOBS)
    AFTER_PROLOGUE = 1

    w_qkv = sb("w_qkv", 3 * 1024)
    w_out = sb("w_out", 8 * D)
    sort_w = sb("sort_w", SORT_HEADS * BUCKETS)
    bias_out = sb("bias_out", D)
    xn_t = sb("xn_t", TILES * P)
    xn_cur = sb("xn_cur", TOK)
    xsum_cur = sb("xsum_cur", P)
    r_blk = sb("r_blk", SORT_HEADS * P)
    r_t = sb("r_t", 4 * P)
    v_nat = sb("v_nat", W * 256)
    k_nat = sb("k_nat", W * 256)
    v_re = sb("v_re", W * 256)
    feats_t = v_re
    k_t = v_re
    keys_t = sb("keys_t", 2 * 16 * P)
    keys_loc = sb("keys_loc", 4 * PAD)
    q_diag = sb("q_diag", 4 * TOK)
    vals = [sb(f"vals{i}", 16 * 256) for i in range(2)]
    vals_loc = sb("vals_loc", 16 * 256)
    att_t = sb("att_t", 2 * TOK)
    s_masked = sb("s_masked", GROUPS * P)
    r_exp = s_masked[:, 0:SORT_HEADS * BUCKETS]
    p_t = [sb(f"p_t{i}", GROUPS * P) for i in range(2)]
    ident = sb("ident", P)
    mask_sort = sb("mask_sort", 64)
    mask_loc = sb("mask_loc", WIDE)
    edge = sb("edge", GROUPS * 24)
    shifted = [sb(f"shifted{i}", GROUPS * 24) for i in range(2)]
    probs = [sb(f"probs{i}", GROUPS * 24) for i in range(2)]
    p_wide = sb("p_wide", GROUPS * P)
    stat = sb("stat", 64)
    rstat = sb("rstat", 3 * 16)
    bn = sb("bn", 6 * TILES)
    ln_small = sb("ln_small", 5 * TILES)
    xn_nat = vals[0]

    work = psum("work", 1024)
    ps_s = psum("ps_s", 1024)
    ps_e = psum("ps_e", 1024)
    ps_o = psum("ps_o", 512)

    x_loaded = [sem(f"x_loaded{i}") for i in range(2)]
    w_loaded = sem("w_loaded")
    consts_ready = sem("consts_ready")
    zeros_ready = sem("zeros_ready")
    pool_chain = sem("pool_chain")
    var_ready = sem("var_ready")
    root_ready = sem("root_ready")
    xn_ready = sem("xn_ready")
    xt_full = sem("xt_full")
    xt_done = sem("xt_done")
    xsum_ready = sem("xsum_ready")
    x_biased = sem("x_biased")
    cur_ready = sem("cur_ready")
    dve_chain = sem("dve_chain")
    r_link = sem("r_link")
    work_full = sem("work_full")
    work_act = sem("work_act")
    work_dve = sem("work_dve")
    r_exped = sem("r_exped")
    r_ready = sem("r_ready")
    own_loaded = sem("own_loaded")
    mixed_loaded = sem("mixed_loaded")
    loc_loaded = sem("loc_loaded")
    s_full = sem("s_full")
    s_done = sem("s_done")
    picked = sem("picked")
    shifted_ready = sem("shifted_ready")
    exped = sem("exped")
    keys_copied = sem("keys_copied")
    p_spread = sem("p_spread")
    edge_done = sem("edge_done")
    max_done = sem("max_done")
    p_t_ready = sem("p_t_ready")
    sum_done = sem("sum_done")
    inv_done = sem("inv_done")
    p_ready = sem("p_ready")
    e_full = sem("e_full")
    e_done = sem("e_done")
    o_full = sem("o_full")
    o_done = sem("o_done")

    x_flat = x_sb
    xg = x_sb[:, :].rearrange("p (t d) -> p t d", d=D)

    def full(eng, it, name):
        eng.wait_ge(work_full, it * NJOBS + (JOBS[name][0] + 1))

    def emptied(eng, it, name):
        _, who, k = JOBS[name]
        s = work_act if who == "act" else work_dve
        eng.wait_ge(s, it * COUNT[who] + (AFTER_PROLOGUE + k + 1))

    def bank(name, cols=512):
        b = JOBS[name][0] % 2
        return b * 512

    names = list(JOBS)
    prologue_jobs = TILES // 4

    block = ctx.enter_context(nc.Block())

    @block.sync
    def _(sp):
        xd = A["x"].rearrange("b (t p) d -> p (b t) d", p=P)
        for i in range(2):
            sp.dma_start(xg[:, 16 * i:16 * i + 16, :], xd[:, 16 * i:16 * i + 16, :]).then_inc(x_loaded[i], 16)
        sp.dma_start(w_qkv[:, 0:1024], A["w_q"]).then_inc(w_loaded, 16)
        sp.dma_start(w_qkv[:, 1024:3072], A["w_kv"]).then_inc(w_loaded, 16)
        sp.dma_start(sort_w[:, :].rearrange("p (h v) -> p h v", h=SORT_HEADS),
                     A["sort_w"].rearrange("a h d v -> d (a h) v")).then_inc(w_loaded, 16)
        sp.dma_start(w_out[:, :].rearrange("p (n d) -> p n d", n=8),
                     A["w_out"].rearrange("(n p) d -> p n d", p=P)).then_inc(w_loaded, 16)
        sp.dma_start(bias_out[:, :], A["b_out"].rearrange("(a d) -> a d", a=1).to_broadcast([P, D])).then_inc(w_loaded, 16)
        sp.wait_ge(zeros_ready, 1)
        with sp.Fori(0, TURNS) as it:
            for c in range(CHUNKS):
                emptied(sp, it, ("v", c, 3))
                if c == 0:
                    for b in range(2):
                        for g in range(GROUPS):
                            lo = 1 if g == 0 else 0
                            hi = 9 if g == GROUPS - 1 else 10
                            src = BUCKETS * b + GROUPS * g - 1
                            sp.dma_start(view(vals_loc, lo * W, (hi - lo) * W, (b * GROUPS + g) * 256, [[1, 256]]),
                                         view(v_nat, src + lo, hi - lo, 0, [[256, W], [1, 256]])).then_inc(loc_loaded, 16)
                    continue
                dst = vals[(c - 1) % 2]
                for g in range(16):
                    sp.dma_start(view(dst, 0, 64, g * 256, [[1, 256]]),
                                 view(v_nat, 8 * g, 8, 0, [[256, W], [1, 256]])).then_inc(own_loaded, 16)
                emptied(sp, it, ("vr", c, 3))
                for g in range(16):
                    sp.dma_start(view(dst, 64, 64, g * 256, [[1, 256]]),
                                 view(v_re, 8 * g, 8, 0, [[256, W], [1, 256]])).then_inc(mixed_loaded, 16)

    @block.gpsimd
    def _(pool):
        done = [0]

        def link(ins):
            done[0] += 1
            ins.then_inc(pool_chain, 1)
            pool.wait_ge(pool_chain, done[0])

        nc.gpsimd.memset(ident[:, :], 0.0)
        nc.gpsimd.memset(mask_sort[:, :], 1.0)
        nc.gpsimd.memset(mask_loc[:, :], 1.0)
        nc.gpsimd.memset(r_blk[:, :], 0.0)
        nc.gpsimd.memset(keys_loc[:, :], 0.0)
        nc.gpsimd.memset(q_diag[:, :], 0.0)
        link(nc.gpsimd.memset(edge[:, :], 0.0))
        link(nc.gpsimd.affine_select(out=ident[:, :], in_=ident[:, :], compare_op=ALU.not_equal, fill=1.0,
                                     base=0, pattern=[[-1, P]], channel_multiplier=1))
        for p0 in (0, 64):
            v = mask_sort[p0:p0 + 64, :].rearrange("p (u t) -> p u t", t=W)
            link(nc.gpsimd.affine_select(out=v, in_=v, compare_op=ALU.is_ge, fill=0.0, base=0,
                                         pattern=[[-8, 8], [0, 8]], channel_multiplier=1))
            link(nc.gpsimd.affine_select(out=v, in_=v, compare_op=ALU.is_ge, fill=0.0, base=7,
                                         pattern=[[8, 8], [0, 8]], channel_multiplier=-1))
            v = mask_loc[p0:p0 + 64, :].rearrange("p (w t) -> p w t", t=W)
            link(nc.gpsimd.affine_select(out=v, in_=v, compare_op=ALU.is_ge, fill=0.0, base=7,
                                         pattern=[[8, 12], [0, 8]], channel_multiplier=-1))
            link(nc.gpsimd.affine_select(out=v, in_=v, compare_op=ALU.is_ge, fill=0.0, base=16,
                                         pattern=[[-8, 12], [0, 8]], channel_multiplier=1))
            first = edge[p0:p0 + 64, 0:W]
            last = edge[p0:p0 + 64, 7 * 24:7 * 24 + W]
            link(nc.gpsimd.affine_select(out=first, in_=first, compare_op=ALU.is_ge, fill=OUT_OF_SEQUENCE,
                                         base=-8, pattern=[[0, W]], channel_multiplier=1))
            link(nc.gpsimd.affine_select(out=last, in_=last, compare_op=ALU.is_ge, fill=OUT_OF_SEQUENCE,
                                         base=55, pattern=[[0, W]], channel_multiplier=-1))
        nc.gpsimd.memset(vals_loc[:, :], 0.0).then_inc(zeros_ready, 1)
        pool.wait_ge(zeros_ready, 1)
        nc.gpsimd.memset(stat[:, :], 0.0).then_inc(consts_ready, 1)
        pool.wait_ge(xt_done, 2)
        nc.gpsimd.tensor_copy(xn_cur[:, :], xn_t[:, 0:TOK]).then_inc(cur_ready, 1)
        pool.wait_ge(xn_ready, 8)
        pool.wait_ge(w_loaded, 80)
        for i in range(4):
            xv = xg[:, 8 * i:8 * i + 8, :]
            nc.gpsimd.tensor_tensor(xv, xv, view(bias_out, 0, P, 0, [[0, 8], [1, D]]), ALU.add).then_inc(x_biased, 1)
        with pool.Fori(0, TURNS) as it:
            for u in range(UNITS):
                if u == 13:
                    full(pool, it, ("q", 3, 3))
                    nxt = (it + 1) % TURNS
                    nc.gpsimd.tensor_copy(xn_cur[:, :], xn_t[:, bass.ds(nxt * TOK, TOK)]).then_inc(cur_ready, 1)
                pool.wait_ge(p_ready, it * UNITS + (u + 1))
                if u:
                    pool.wait_ge(e_full, it * UNITS + u)
                if u < 4:
                    shape, src, m = (GROUPS, 4, 24), [[24, GROUPS], [0, 4], [1, 24]], (mask_loc, [[0, GROUPS], [24, 4], [1, 24]])
                else:
                    shape, src, m = (2 * GROUPS, W, W), [[W, 2 * GROUPS], [0, W], [1, W]], (mask_sort, [[0, 2 * GROUPS], [W, W], [1, W]])
                n = shape[0] * shape[1] * shape[2]
                nc.gpsimd.tensor_tensor(p_wide[:, 0:n].rearrange("p (a m b) -> p a m b", m=shape[1], b=shape[2]),
                                        view(probs[u % 2], 0, P, 0, src), view(m[0], 0, P, 0, m[1]),
                                        ALU.mult).then_inc(p_spread, 1)

    @block.scalar
    def _(act):
        for i in range(2):
            act.wait_ge(var_ready, i + 1)
            nc.scalar.activation(ln_small[:, 2 * TILES:2 * TILES + 16], ln_small[:, 4 * TILES:4 * TILES + 16],
                                 ACT.Sqrt).then_inc(root_ready, 1)
        for n in range(prologue_jobs):
            act.wait_ge(xt_full, n + 1)
            nc.scalar.copy(xn_t[:, n * 512:n * 512 + 512],
                           work[:, (n % 2) * 512:(n % 2) * 512 + 512]).then_inc(xt_done, 1)
        act.sem_inc(work_act, AFTER_PROLOGUE)
        with act.Fori(0, TURNS) as it:
            def empty(name, dst, src):
                full(act, it, name)
                nc.scalar.copy(dst, src).then_inc(work_act, 1)

            def chunk(c):
                for n in range(4):
                    w = bank(("v", c, n))
                    empty(("v", c, n), v_nat[:, n * 512:n * 512 + 512], work[:, w:w + 512])
                for n in range(4):
                    pp, b = divmod(n, 2)
                    w = bank(("k", c, n))
                    if c == 0:
                        o = (pp * 2 + b) * PAD + W
                        empty(("k", c, n), keys_loc[:, o:o + SEQ], work[:, w:w + 512])
                    else:
                        empty(("k", c, n), k_t[:, n * 512:n * 512 + 512], work[:, w:w + 512])
                if c:
                    w = bank(("rt", c))
                    empty(("rt", c), r_t[:, :], work[:, w:w + 512])
                for n in range(4):
                    w = bank(("q", c, n))
                    full(act, it, ("q", c, n))
                    for j in range(2):
                        ins = nc.scalar.copy(view(q_diag, 64 * j, 64, n * 1024 + j * 64, [[P, GROUPS], [1, 64]]),
                                             work[64 * j:64 * j + 64, w:w + 512].rearrange("p (g q) -> p g q", q=64))
                    ins.then_inc(work_act, 1)
                if c:
                    for n in range(4):
                        w = bank(("kn", c, n))
                        empty(("kn", c, n), k_nat[:, n * 512:n * 512 + 512], work[:, w:w + 512])
                    act.wait_ge(keys_copied, it * 3 + c)
                    for n in range(4):
                        w = bank(("vr", c, n))
                        empty(("vr", c, n), view(v_re, 0, P, n * 64, [[256, W], [1, 64]]),
                              work[:, w:w + 512].rearrange("p (t d) -> p t d", t=W))
                    for n in range(4):
                        pp, half = divmod(n, 2)
                        w = bank(("kr", c, n))
                        empty(("kr", c, n), view(keys_t, 0, P, pp * 16 * P + 64 + half * 4, [[1, 4], [P, 16], [8, 8]]),
                              work[:, w:w + 512].rearrange("p (t g u) -> p t g u", t=4, g=16))

            for g in range(3):
                w = bank(("feats", g))
                empty(("feats", g), feats_t[:, g * 512:g * 512 + 512], work[:, w:w + 512])
            emptied(act, it, ("logits", 1))
            nc.scalar.activation(r_exp, r_exp, ACT.Exp).then_inc(r_exped, 1)
            for i in range(UNITS + 3):
                if i % 4 == 0 and i < UNITS:
                    chunk(i // 4)
                if i < UNITS:
                    u = i
                    n = GROUPS * (24 if u < 4 else 16)
                    act.wait_ge(shifted_ready, it * UNITS + (u + 1))
                    nc.scalar.activation(shifted[u % 2][:, 0:n], shifted[u % 2][:, 0:n], ACT.Exp,
                                         scale=1.0 if u < 4 else DH ** -0.5).then_inc(exped, 1)
                if i >= 2 and i - 2 < UNITS:
                    v = i - 2
                    n = WIDE if v < 4 else P
                    act.wait_ge(e_full, it * UNITS + (v + 1))
                    nc.scalar.copy(p_t[v % 2][0:n, :], ps_e[0:n, :]).then_inc(e_done, 1)
                if i >= 3:
                    u = i - 3
                    c, pp, b = u // 4, u // 2 % 2, u % 2
                    if u % 4 == 0 and c:
                        full(act, it, ("out", c - 1, 1))
                    act.wait_ge(o_full, it * UNITS + (u + 1))
                    nc.scalar.copy(att_t[:, pp * TOK + b * SEQ:pp * TOK + (b + 1) * SEQ], ps_o[:, :]).then_inc(o_done, 1)

    @block.vector
    def _(dve):
        done = [0]

        def link(ins):
            done[0] += 1
            ins.then_inc(dve_chain, 1)
            dve.wait_ge(dve_chain, done[0])

        for i in range(2):
            dve.wait_ge(x_loaded[i], 16)

            layer_norm_steps(nc, link, lambda t: xg[:, 16 * i + t, :], bn, ln_small, 16, 1e-5,
                             var_ready, lambda: dve.wait_ge(root_ready, i + 1))
            for t in range(16):
                T = 16 * i + t
                ins = nc.vector.tensor_scalar(xn_nat[:, T * D:T * D + D], xg[:, T, :], ln_small[:, t:t + 1],
                                              ln_small[:, TILES + t:TILES + t + 1], ALU.subtract, ALU.mult)
                if t % 4 == 3:
                    ins.then_inc(xn_ready, 1)
            dve.wait_ge(xn_ready, 4 * (i + 1))
        dve.wait_ge(consts_ready, 1)
        dve.wait_ge(cur_ready, 1)
        nc.vector.tensor_reduce(xsum_cur[:, :], xn_cur[:, :].rearrange("p (b w) -> p b w", w=W), AX_X,
                                ALU.add).then_inc(xsum_ready, 1)
        dve.wait_ge(x_biased, 4)
        dve.sem_inc(work_dve, AFTER_PROLOGUE)
        with dve.Fori(0, TURNS) as it:
            rmax, rsum, rinv = (rstat[:, 16 * k:16 * k + SORT_HEADS] for k in range(3))
            lw = [work[:, bank(("logits", g)):bank(("logits", g)) + (8, 4)[g] * 64].rearrange(
                "p (h v) -> p h v", v=BUCKETS) for g in range(2)]
            hs = [(0, 8), (8, 12)]
            R_LINKS = 4

            def rlink(k, ins):
                ins.then_inc(r_link, 1)
                dve.wait_ge(r_link, it * R_LINKS + (k + 1))

            full(dve, it, ("logits", 0))
            nc.vector.tensor_reduce(rmax[:, 0:8], lw[0], AX_X, ALU.max)
            full(dve, it, ("logits", 1))
            rlink(0, nc.vector.tensor_reduce(rmax[:, 8:12], lw[1], AX_X, ALU.max))
            rlink(1, nc.vector.tensor_scalar(rmax, rmax, 0.0, None, ALU.max))
            for g, (a, b) in enumerate(hs):
                nc.vector.scalar_tensor_tensor(
                    r_exp[:, a * 64:b * 64].rearrange("p (h v) -> p h v", v=BUCKETS), lw[g], 0.0,
                    view(rstat, 0, P, a, [[1, b - a], [0, BUCKETS]]), ALU.max, ALU.subtract).then_inc(work_dve, 1)
            dve.wait_ge(r_exped, it + 1)
            re3 = r_exp.rearrange("p (h v) -> p h v", v=BUCKETS)
            rlink(2, nc.vector.tensor_reduce(rsum, re3, AX_X, ALU.add))
            rlink(3, nc.vector.reciprocal(rinv, rsum))
            for b in range(2):
                nc.vector.tensor_tensor(
                    view(r_blk, 64 * b, 64, 64 * b, [[P, SORT_HEADS], [1, 64]]),
                    view(s_masked, 64 * b, 64, 0, [[64, SORT_HEADS], [1, 64]]),
                    view(rstat, 64 * b, 64, 32, [[1, SORT_HEADS], [0, 64]]), ALU.mult).then_inc(r_ready, 1)

            for i in range(UNITS + 4):
                if i % 4 == 0 and 0 < i < UNITS:
                    emptied(dve, it, ("k", i // 4, 3))
                    nc.vector.tensor_copy(view(keys_t, 0, P, 0, [[P, 32], [1, 64]]),
                                          k_t[:, :].rearrange("p (g k) -> p g k", k=64)).then_inc(keys_copied, 1)
                if i < UNITS:
                    width, blocks, m = (WIDE, GROUPS, mask_loc) if i < 4 else (64, 2 * GROUPS, mask_sort)
                    if i == 0:
                        dve.wait_ge(r_ready, it * 2 + 2)
                    dve.wait_ge(s_full, it * UNITS + (i + 1))
                    nc.vector.tensor_tensor(s_masked[:, 0:blocks * width].rearrange("p (a k) -> p a k", k=width),
                                            view(ps_s, 0, P, 0, [[1024 // blocks, blocks], [1, width]]),
                                            view(m, 0, P, 0, [[0, blocks], [1, width]]), ALU.mult).then_inc(s_done, 1)
                if 1 <= i <= UNITS:
                    u = i - 1
                    k = 24 if u < 4 else 16
                    sv = shifted[u % 2][:, 0:GROUPS * k].rearrange("p (g k) -> p g k", k=k)
                    o = 16 + 8 * (u % 2)
                    ssum, sinv = stat[:, o:o + 8], stat[:, o + 16:o + 24]
                    dve.wait_ge(exped, it * UNITS + (u + 1))
                    nc.vector.tensor_reduce(ssum, sv, AX_X, ALU.add).then_inc(sum_done, 1)
                    dve.wait_ge(sum_done, it * UNITS + (u + 1))
                    nc.vector.reciprocal(sinv, ssum).then_inc(inv_done, 1)
                    dve.wait_ge(inv_done, it * UNITS + (u + 1))
                    if u >= 2:
                        dve.wait_ge(p_spread, it * UNITS + (u - 1))
                    pv = probs[u % 2][:, 0:GROUPS * k].rearrange("p (g k) -> p g k", k=k)
                    nc.vector.tensor_tensor(pv, sv, view(stat, 0, P, o + 16, [[1, GROUPS], [0, k]]),
                                            ALU.mult).then_inc(p_ready, 1)
                if i < UNITS:
                    k = 24 if i < 4 else 16
                    sv = shifted[i % 2][:, 0:GROUPS * k]
                    sv3 = sv.rearrange("p (g k) -> p g k", k=k)
                    smax = stat[:, 8 * (i % 2):8 * (i % 2) + 8]
                    src = s_masked[:, 0:GROUPS * WIDE].rearrange("p (g m k) -> p g k m", g=GROUPS, m=4) if i < 4 else \
                        s_masked[:, :].rearrange("p (a u t) -> p a t u", u=W, t=W)
                    dst = sv3 if i < 4 else sv.rearrange("p (a t) -> p a t", t=W)
                    dve.wait_ge(s_done, it * UNITS + (i + 1))
                    nc.vector.tensor_reduce(dst, src, AX_X, ALU.add).then_inc(picked, 1)
                    dve.wait_ge(picked, it * UNITS + (i + 1))
                    if i < 4:
                        nc.vector.tensor_tensor(sv, sv, edge[:, :], ALU.add).then_inc(edge_done, 1)
                        dve.wait_ge(edge_done, it * 4 + (i + 1))
                    nc.vector.tensor_reduce(smax, sv3, AX_X, ALU.max).then_inc(max_done, 1)
                    dve.wait_ge(max_done, it * UNITS + (i + 1))
                    nc.vector.tensor_tensor(sv3, sv3, view(stat, 0, P, 8 * (i % 2), [[1, GROUPS], [0, k]]),
                                            ALU.subtract).then_inc(shifted_ready, 1)
                if i == 14:
                    dve.wait_ge(cur_ready, it + 2)
                    nc.vector.tensor_reduce(xsum_cur[:, :], xn_cur[:, :].rearrange("p (b w) -> p b w", w=W), AX_X,
                                            ALU.add).then_inc(xsum_ready, 1)
                if i >= 7 and (i - 7) % 4 == 0:
                    c = (i - 7) // 4
                    for n in range(2):
                        full(dve, it, ("out", c, n))
                        w = bank(("out", c, n))
                        xs = x_flat[:, bass.ds(it * TOK + n * 512, 512)]
                        nc.vector.tensor_tensor(xs, xs, work[:, w:w + 512], ALU.add).then_inc(work_dve, 1)

    @block.tensor
    def _(pe):
        pe.wait_ge(consts_ready, 1)
        for n in range(prologue_jobs):
            pe.wait_ge(xn_ready, n + 1)
            if n >= 2:
                pe.wait_ge(xt_done, n - 1)
            for t in range(4):
                T = 4 * n + t
                last = nc.tensor.transpose(work[:, (n % 2) * 512 + t * P:(n % 2) * 512 + t * P + P],
                                           xn_nat[:, T * D:T * D + D], ident[:, :])
            last.then_inc(xt_full, 1)
        pe.wait_ge(xt_done, prologue_jobs)
        pe.wait_ge(w_loaded, 80)
        with pe.Fori(0, TURNS) as it:
            def free_bank(name):
                n = JOBS[name][0]
                if n >= 2:
                    emptied(pe, it, names[n - 2])
                else:
                    pe.wait_ge(work_dve, it * COUNT["dve"] + AFTER_PROLOGUE)

            def chunk(c):
                if c == 0:
                    pe.wait_ge(cur_ready, it + 1)
                for n in range(4):
                    free_bank(("v", c, n))
                    w = bank(("v", c, n))
                    for h in range(2):
                        last = nc.tensor.matmul(work[:, w + h * 256:w + h * 256 + 256],
                                                view(xn_cur, 0, P, 2 * n + h, [[W, P]]),
                                                w_qkv[:, 2048 + c * 256:2048 + c * 256 + 256], start=True, stop=True)
                    last.then_inc(work_full, 1)

                def project(name, part):
                    for n in range(4):
                        free_bank((name, c, n))
                        w = bank((name, c, n))
                        pp, b = divmod(n, 2)
                        o = part * 1024 + (2 * c + pp) * P
                        nc.tensor.matmul(work[:, w:w + 512], w_qkv[:, o:o + P], xn_cur[:, b * SEQ:(b + 1) * SEQ],
                                         start=True, stop=True).then_inc(work_full, 1)

                project("k", 1)
                if c:
                    if c == 1:
                        pe.wait_ge(r_ready, it * 2 + 2)
                    free_bank(("rt", c))
                    w = bank(("rt", c))
                    for h in range(4):
                        hh = 4 * (c - 1) + h
                        last = nc.tensor.transpose(work[:, w + h * P:w + h * P + P], r_blk[:, hh * P:hh * P + P], ident[:, :])
                    last.then_inc(work_full, 1)
                project("q", 0)
                if not c:
                    return
                emptied(pe, it, ("k", c, 3))
                for n in range(4):
                    free_bank(("kn", c, n))
                    w = bank(("kn", c, n))
                    for t in range(2):
                        for pp in range(2):
                            last = nc.tensor.transpose(work[:, w + t * 256 + pp * P:w + t * 256 + pp * P + P],
                                                       view(k_t, 0, P, pp * TOK + 2 * n + t, [[W, P]]),
                                                       ident[:, :])
                    last.then_inc(work_full, 1)
                emptied(pe, it, ("rt", c))
                for h in range(4):
                    free_bank(("vr", c, h))
                    w = bank(("vr", c, h))
                    nc.tensor.matmul(work[:, w:w + 512], r_t[:, h * P:h * P + P],
                                     view(v_nat, 0, P, h * 64, [[256, W], [1, 64]]),
                                     start=True, stop=True).then_inc(work_full, 1)
                emptied(pe, it, ("kn", c, 3))
                for n in range(4):
                    pp, half = divmod(n, 2)
                    free_bank(("kr", c, n))
                    w = bank(("kr", c, n))
                    for t in range(4):
                        for j in range(2):
                            h = 2 * pp + j
                            o = (4 * half + t) * 256 + h * 64
                            last = nc.tensor.matmul(work[64 * j:64 * j + 64, w + t * P:w + t * P + P],
                                                    k_nat[:, o:o + 64], r_t[:, h * P:h * P + P], start=True, stop=True)
                    last.then_inc(work_full, 1)

            pe.wait_ge(xsum_ready, it + 1)
            for g in range(3):
                free_bank(("feats", g))
                w = bank(("feats", g))
                for h in range(4):
                    for part in range(2):
                        o = part * 1024 + (LOCAL_HEADS + 4 * g + h) * 64
                        last = nc.tensor.matmul(work[64 * part:64 * part + 64, w + h * P:w + h * P + P],
                                                w_qkv[:, o:o + 64], xsum_cur[:, :], start=True, stop=True)
                last.then_inc(work_full, 1)
            for g in range(2):
                free_bank(("logits", g))
                emptied(pe, it, ("feats", 1 + g))
                w = bank(("logits", g))
                for h in range((8, 4)[g]):
                    hh = 8 * g + h
                    last = nc.tensor.matmul(work[:, w + h * 64:w + h * 64 + 64], feats_t[:, hh * P:hh * P + P],
                                            sort_w[:, hh * 64:hh * 64 + 64], start=True, stop=True)
                last.then_inc(work_full, 1)

            for i in range(UNITS + 4):
                if i % 4 == 0 and i < UNITS:
                    chunk(i // 4)
                if i < UNITS:
                    c, pp, b = i // 4, i // 2 % 2, i % 2
                    if i % 4 == 0:
                        emptied(pe, it, ("kr", c, 3) if c else ("q", c, 3))
                        if c:
                            pe.wait_ge(keys_copied, it * 3 + c)
                    if i:
                        pe.wait_ge(s_done, it * UNITS + i)
                    for g in range(GROUPS):
                        if c == 0:
                            keys = view(keys_loc, 0, P, (pp * 2 + b) * PAD + g * 64, [[1, WIDE]])
                        else:
                            keys = view(keys_t, 0, P, (pp * 16 + b * 8 + g) * P, [[1, P]])
                        o = (pp * 16 + b * 8 + g) * P
                        last = nc.tensor.matmul(ps_s[:, g * P:g * P + (P if c else WIDE)], q_diag[:, o:o + P], keys,
                                                start=True, stop=True)
                    last.then_inc(s_full, 1)
                if i >= 7 and (i - 7) % 4 == 0:
                    c = (i - 7) // 4
                    pe.wait_ge(o_done, it * UNITS + (4 * c + 4))
                    for n in range(2):
                        free_bank(("out", c, n))
                        w = bank(("out", c, n))
                        for t in range(4):
                            for pp in range(2):
                                o = pp * TOK + (4 * n + t) * P
                                last = nc.tensor.matmul(work[:, w + t * P:w + t * P + P], att_t[:, o:o + P],
                                                        w_out[:, (2 * c + pp) * D:(2 * c + pp) * D + D],
                                                        start=(pp == 0), stop=(pp == 1))
                        last.then_inc(work_full, 1)
                if 2 <= i <= UNITS + 1:
                    u = i - 2
                    pe.wait_ge(p_spread, it * UNITS + (u + 1))
                    if u:
                        pe.wait_ge(e_done, it * UNITS + u)
                    n = WIDE if u < 4 else P
                    for g in range(GROUPS):
                        last = nc.tensor.transpose(ps_e[0:n, g * P:g * P + P], p_wide[:, g * n:g * n + n], ident[:, :])
                    last.then_inc(e_full, 1)
                if 3 <= i <= UNITS + 2:
                    u = i - 3
                    c, pp, b = u // 4, u // 2 % 2, u % 2
                    if u == 0:
                        pe.wait_ge(loc_loaded, it * 256 + 256)
                    elif u % 4 == 0:
                        pe.wait_ge(own_loaded, it * 768 + 256 * c)
                        pe.wait_ge(mixed_loaded, it * 768 + 256 * c)
                    pe.wait_ge(e_done, it * UNITS + (u + 1))
                    if u:
                        pe.wait_ge(o_done, it * UNITS + u)
                    n = WIN if c == 0 else P
                    v = vals_loc if c == 0 else vals[(c - 1) % 2]
                    for g in range(GROUPS):
                        for j in range(2):
                            o = (b * GROUPS + g) * 256 + (2 * pp + j) * 64
                            q = g * P + j * 64
                            last = nc.tensor.matmul(ps_o[64 * j:64 * j + 64, g * 64:g * 64 + 64], v[0:n, o:o + 64],
                                                    p_t[u % 2][0:n, q:q + 64], start=True, stop=True)
                    last.then_inc(o_full, 1)


def feed_forward_block(nc, ctx, x_sb, A, out):
    def sb(name, cols, dt=F32):
        return ctx.enter_context(nc.sbuf_tensor(name, [P, cols], dt))

    def psum(name, cols):
        return ctx.enter_context(nc.psum_tensor(name, [P, cols], F32))

    def sem(name):
        return ctx.enter_context(nc.semaphore(name))

    E = EXPERTS
    CH = INTER // P
    ROW = D + 4
    SLOTS = E * CAP
    TOKENS = TILES * P
    GRP = TOKENS // 512
    VEC = E * CH + CH + 2

    y = sb("y", TOKENS)
    rows = sb("rows", TILES * ROW)
    a_t = sb("a_t", TOKENS)
    blank = sb("blank", SLOTS // P * ROW)
    w_gate = sb("w_gate", E + 2)
    res_w1 = sb("res_w1", INTER)
    res_w2 = sb("res_w2", CH * D)
    w1 = [sb(f"w1_{i}", INTER) for i in range(2)]
    w2 = [sb(f"w2_{i}", CH * D) for i in range(2)]
    b2 = sb("b2", E * D)
    res_b2 = sb("res_b2", D)
    vecs = sb("vecs", D)
    cols = sb("cols", VEC)
    ident = sb("ident_b", P)
    before = sb("before", P, BF16)
    ones = sb("ones", P, BF16)
    rank = sb("rank", E)
    first_slot = sb("first_slot", E)
    spare = sb("spare", TILES)
    bn = sb("bn_b", 6 * TILES)
    ln_small = sb("ln_small_b", 5 * TILES)
    gates = sb("gates", TILES * (E + 2))
    work1 = sb("work1", TILES * E)
    work2 = sb("work2", TILES * E)
    chosen = sb("chosen", TILES * E)
    chosen_bf = sb("chosen_bf", TILES * E, BF16)
    s = {n: sb(n, TILES) for n in ("gmax", "cmax", "gsum", "csum", "top", "first", "slot", "kept", "lost", "share")}
    slot_i = sb("slot_i", TILES, I32)
    counts_i = sb("counts_i", 2 * E, I32)
    h_t = [sb(f"h_t{i}", CH * 512) for i in range(2)]
    res = [sb(f"res{i}", 512) for i in range(2)]
    xe = [sb(f"xe{i}", CAP // P * ROW) for i in range(2)]
    xe_t = [sb(f"xe_t{i}", CAP) for i in range(2)]
    eo = [sb(f"eo{i}", 512) for i in range(2)]

    disp = nc.dram_tensor("disp", (SLOTS + TOKENS, ROW), F32, kind="Internal").ap()
    moe = nc.dram_tensor("moe", (TOKENS + SLOTS, D), F32, kind="Internal").ap()

    ps_t = psum("ps_t", 1024)
    ps_h = psum("ps_h", 1024)
    ps_o = psum("ps_o_b", 1024)
    ps_g = psum("ps_g", 512)
    ps_l = psum("ps_l", 512)

    weights_in = sem("weights_in")
    gate_in = sem("gate_in")
    blank_ready = sem("blank_ready")
    disp_blank = sem("disp_blank")
    moe_blank = sem("moe_blank")
    consts_ready = sem("consts_ready_b")
    pool_chain = sem("pool_chain_b")
    dve_chain = sem("dve_chain_b")
    var_ready = sem("var_ready_b")
    root_ready = sem("root_ready_b")
    y_ready = sem("y_ready")
    base_ready = sem("base_ready")
    rows_ready = sem("rows_ready")
    vecs_full = sem("vecs_full")
    vecs_done = sem("vecs_done")
    t_full = sem("t_full")
    t_done = sem("t_done")
    g_full = sem("g_full")
    shift_ready = sem("shift_ready")
    exp_ready = sem("exp_ready")
    chosen_ready = sem("chosen_ready")
    l_full = sem("l_full")
    slots_ready = sem("slots_ready")
    scattered = sem("scattered")
    h_full = sem("h_full")
    h_done = sem("h_done")
    o_full = sem("o_full_b")
    o_done = sem("o_done_b")
    res_link = sem("res_link")
    xe_loaded = [sem(f"xe_loaded{i}") for i in range(2)]
    we_loaded = [sem(f"we_loaded{i}") for i in range(2)]
    xt_full = sem("xt_full_b")
    xt_done = sem("xt_done_b")
    sent = [sem(f"sent{i}") for i in range(2)]
    moe_in = [sem(f"moe_in{i}") for i in range(4)]
    res_added = sem("res_added")
    BANKS = 2
    fin = sem("fin")
    stored = sem("stored")

    xg = x_sb[:, :].rearrange("p (t d) -> p t d", d=D)
    yg = y[:, :].rearrange("p (t d) -> p t d", d=D)
    rg = rows[:, :].rearrange("p (t r) -> p t r", r=ROW)
    gt = gates[:, :].rearrange("p (t e) -> p t e", e=E + 2)
    c_b1, c_rb1, c_nw, c_nb = 0, E * CH, E * CH + CH, E * CH + CH + 1
    GELU = ACT.Gelu_apprx_tanh

    def spread(name, n, off=0):
        return view(s[name], 0, P, off, [[1, TILES], [0, n]])

    block = ctx.enter_context(nc.Block())

    @block.sync
    def _(sp):
        sp.dma_start(vecs[0:c_rb1, :], A["inter_b"].rearrange("e (c p) -> (e c) p", p=P)).then_inc(weights_in, 16)
        sp.dma_start(vecs[c_rb1:c_nw, :], A["res_inter_b"].rearrange("(c p) -> c p", p=P)).then_inc(weights_in, 16)
        sp.dma_start(vecs[c_nw:c_nw + 1, :], A["attn_nw"].rearrange("(a p) -> a p", a=1)).then_inc(weights_in, 16)
        sp.dma_start(vecs[c_nb:c_nb + 1, :], A["attn_nb"].rearrange("(a p) -> a p", a=1)).then_inc(weights_in, 16)
        sp.dma_start(w_gate[:, 0:E], A["wg"]).then_inc(gate_in, 16)
        sp.dma_start(w_gate[:, E:E + 2], A["res_coef"]).then_inc(gate_in, 16)
        sp.dma_start(res_w1[:, :], A["res_inter_w"]).then_inc(gate_in, 16)
        sp.dma_start(res_w2[:, :].rearrange("p (c d) -> p c d", d=D),
                     A["res_output_w"].rearrange("(c p) d -> p c d", p=P)).then_inc(gate_in, 16)
        sp.dma_start(res_b2[:, :], A["res_output_b"].rearrange("(a d) -> a d", a=1).to_broadcast([P, D])).then_inc(gate_in, 16)
        sp.dma_start(b2[:, :], A["output_b"].rearrange("(a e) d -> a (e d)", a=1).to_broadcast([P, E * D])).then_inc(gate_in, 16)
        sp.wait_ge(blank_ready, 2)
        sp.dma_start(disp[0:SLOTS, :].rearrange("(e p j) r -> p e (j r)", e=E, p=P),
                     blank[:, :].rearrange("p (e r) -> p e r", e=E)).then_inc(disp_blank, 16)
        sp.dma_start(moe[0:TOKENS, :].rearrange("(t p) d -> p t d", p=P),
                     view(blank, 0, P, 0, [[ROW, TILES], [1, D]])).then_inc(moe_blank, 16)

        def load_weights(e, i):
            sp.dma_start(w1[i][:, :], A["inter_w"][bass.ds(e, 1), :, :].rearrange("a p n -> (a p) n")).then_inc(we_loaded[i], 16)
            sp.dma_start(w2[i][:, :].rearrange("p (c d) -> p c d", d=D),
                         A["output_w"][bass.ds(e, 1), :, :].rearrange("a (c p) d -> p (a c) d", p=P)).then_inc(we_loaded[i], 16)

        def load_rows(e, i):
            sp.dma_start(xe[i][:, :], disp[bass.ds(e * CAP, CAP), :].rearrange("(p j) r -> p (j r)", p=P)).then_inc(xe_loaded[i], 16)

        for i in range(2):
            load_weights(i, i)
        sp.wait_ge(scattered, 16 * TILES)
        for i in range(2):
            load_rows(i, i)
        with sp.Fori(0, E // 2 - 1) as turn:
            for i in range(2):
                sp.wait_ge(o_full, turn * 2 + (GRP + 1 + i))
                load_weights(turn * 2 + (2 + i), i)
                sp.wait_ge(sent[i], turn * 64 + 64)
                load_rows(turn * 2 + (2 + i), i)
        for i in range(2):
            sp.wait_ge(sent[i], 64 * (E // 2))
        for i in range(4):
            t = TILES // 4
            sp.dma_start(yg[:, t * i:t * i + t, :],
                         moe[t * P * i:t * P * (i + 1), :].rearrange("(t p) d -> p t d", p=P)).then_inc(moe_in[i], 16)
        for i in range(4):
            t = TILES // 4
            sp.wait_ge(fin, i + 1)
            sp.dma_start(out.rearrange("b (t p) d -> p (b t) d", p=P)[:, t * i:t * i + t, :],
                         xg[:, t * i:t * i + t, :]).then_inc(stored, 16)
        sp.wait_ge(stored, 64)

    @block.gpsimd
    def _(pool):
        done = [0]

        def link(ins):
            done[0] += 1
            ins.then_inc(pool_chain, 1)
            pool.wait_ge(pool_chain, done[0])

        nc.gpsimd.memset(blank[:, :], 0.0)
        nc.gpsimd.memset(rows[:, :], 0.0)
        nc.gpsimd.memset(before[:, :], 1.0)
        nc.gpsimd.memset(ones[:, :], 1.0)
        link(nc.gpsimd.memset(ident[:, :], 0.0))
        nc.gpsimd.iota(view(blank, 0, P, D, [[ROW * 4, E], [ROW, 4]]).bitcast(I32),
                       pattern=[[CAP, E], [1, 4]], base=TOKENS, channel_multiplier=4).then_inc(blank_ready, 1)
        nc.gpsimd.iota(view(rows, 0, P, D, [[ROW, TILES]]).bitcast(I32), pattern=[[P, TILES]], base=0,
                       channel_multiplier=1).then_inc(blank_ready, 1)
        nc.gpsimd.affine_select(out=ident[:, :], in_=ident[:, :], compare_op=ALU.not_equal, fill=1.0, base=0,
                                pattern=[[-1, P]], channel_multiplier=1)
        nc.gpsimd.affine_select(out=before[:, :], in_=before[:, :], compare_op=ALU.is_gt, fill=0.0, base=0,
                                pattern=[[1, P]], channel_multiplier=-1)
        nc.gpsimd.iota(slot_i[:, :], pattern=[[P, TILES]], base=SLOTS, channel_multiplier=1)
        nc.gpsimd.iota(counts_i[:, 0:E], pattern=[[-1, E]], base=E, channel_multiplier=0)
        link(nc.gpsimd.iota(counts_i[:, E:2 * E], pattern=[[CAP, E]], base=0, channel_multiplier=0))
        nc.gpsimd.tensor_copy(spare[:, :], slot_i[:, :])
        nc.gpsimd.tensor_copy(rank[:, :], counts_i[:, 0:E])
        nc.gpsimd.tensor_copy(first_slot[:, :], counts_i[:, E:2 * E]).then_inc(consts_ready, 1)
        for i in range(4):
            t = TILES // 4
            pool.wait_ge(y_ready, 1)
            nc.gpsimd.tensor_tensor(xg[:, t * i:t * i + t, :], xg[:, t * i:t * i + t, :], yg[:, t * i:t * i + t, :],
                                    ALU.add).then_inc(base_ready, 1)
        pool.wait_ge(slots_ready, 1)
        pool.wait_ge(disp_blank, 16)
        pool.wait_ge(rows_ready, TILES)
        for t in range(TILES):
            nc.gpsimd.indirect_dma_start(out=disp[:, :], out_offset=bass.IndirectOffsetOnAxis(ap=slot_i[:, t:t + 1], axis=0),
                                         in_=rows[:, t * ROW:t * ROW + ROW], in_offset=None).then_inc(scattered, 16)
        pool.wait_ge(moe_blank, 16)
        for e in range(E):
            i = e % 2
            pool.wait_ge(o_done, BANKS + GRP + 1 + e)
            for j in range(4):
                nc.gpsimd.indirect_dma_start(
                    out=moe[:, :],
                    out_offset=bass.IndirectOffsetOnAxis(ap=view(xe[i], 0, P, j * ROW + D, [[1, 1]]).bitcast(I32), axis=0),
                    in_=eo[i][:, j * D:j * D + D], in_offset=None).then_inc(sent[i], 16)

    def gelu_steps(act, base, i, bias):
        for c in range(CH):
            act.wait_ge(h_full, base + (c + 1))
            nc.scalar.activation(h_t[i][:, c * 512:c * 512 + 512], ps_h[:, (c % 2) * 512:(c % 2) * 512 + 512], GELU,
                                 bias=bias(c)).then_inc(h_done, 1)

    @block.scalar
    def _(act):
        act.sem_inc(h_done, BANKS)
        for n in range(2):
            act.wait_ge(var_ready, n + 1)
            nc.scalar.activation(ln_small[:, 2 * TILES:3 * TILES], ln_small[:, 4 * TILES:5 * TILES],
                                 ACT.Sqrt).then_inc(root_ready, 1)
        act.wait_ge(vecs_full, 1)
        nc.scalar.copy(cols[:, :], ps_l[:, 0:VEC]).then_inc(vecs_done, 1)
        act.wait_ge(vecs_done, 1)
        for n in range(GRP):
            act.wait_ge(t_full, n + 1)
            nc.scalar.activation(a_t[:, n * 512:n * 512 + 512], ps_t[:, (n % 2) * 512:(n % 2) * 512 + 512], ACT.Identity,
                                 scale=cols[:, c_nw:c_nw + 1], bias=cols[:, c_nb:c_nb + 1]).then_inc(t_done, 1)
        act.wait_ge(shift_ready, 1)
        nc.scalar.activation(gates[:, :], gates[:, :], ACT.Exp).then_inc(exp_ready, 1)
        with act.Fori(0, GRP // 2) as turn:
            for i in range(2):
                gelu_steps(act, turn * (2 * CH) + CH * i, i, lambda c: cols[:, c_rb1 + c:c_rb1 + c + 1])
        with act.Fori(0, E // 2) as turn:
            for i in range(2):
                act.wait_ge(xt_full, turn * 2 + (i + 1))
                nc.scalar.activation(xe_t[i][:, :], ps_t[:, i * 512:i * 512 + 512], ACT.Identity,
                                     scale=cols[:, c_nw:c_nw + 1], bias=cols[:, c_nb:c_nb + 1]).then_inc(xt_done, 1)
                gelu_steps(act, turn * (2 * CH) + (GRP * CH + CH * i), i,
                           lambda c: cols[:, bass.ds(turn * (2 * CH) + (i * CH + c), 1)])

    @block.vector
    def _(dve):
        done = [0]

        def link(ins):
            done[0] += 1
            ins.then_inc(dve_chain, 1)
            dve.wait_ge(dve_chain, done[0])

        dve.sem_inc(o_done, BANKS)
        layer_norm_steps(nc, link, lambda t: xg[:, t, :], bn, ln_small, TILES, 1e-5, var_ready,
                         lambda: dve.wait_ge(root_ready, 1))
        for t in range(TILES):
            ins = nc.vector.tensor_scalar(yg[:, t, :], xg[:, t, :], ln_small[:, t:t + 1],
                                          ln_small[:, TILES + t:TILES + t + 1], ALU.subtract, ALU.mult)
        ins.then_inc(y_ready, 1)
        dve.wait_ge(y_ready, 1)
        layer_norm_steps(nc, link, lambda t: yg[:, t, :], bn, ln_small, TILES, 1e-12, var_ready,
                         lambda: dve.wait_ge(root_ready, 2))
        dve.wait_ge(blank_ready, 2)
        for t in range(TILES):
            nc.vector.tensor_scalar(rg[:, t, 0:D], yg[:, t, :], ln_small[:, t:t + 1],
                                    ln_small[:, TILES + t:TILES + t + 1], ALU.subtract, ALU.mult).then_inc(rows_ready, 1)
        dve.wait_ge(consts_ready, 1)
        dve.wait_ge(g_full, 1)
        lg = ps_g[:, 0:TILES * (E + 2)].rearrange("p (t e) -> p t e", e=E + 2)
        nc.vector.tensor_reduce(s["gmax"][:, :], lg[:, :, 0:E], AX_X, ALU.max)
        link(nc.vector.tensor_reduce(s["cmax"][:, :], lg[:, :, E:E + 2], AX_X, ALU.max))
        nc.vector.tensor_tensor(gt[:, :, 0:E], lg[:, :, 0:E], spread("gmax", E), ALU.subtract)
        nc.vector.tensor_tensor(gt[:, :, E:E + 2], lg[:, :, E:E + 2], spread("cmax", 2), ALU.subtract).then_inc(shift_ready, 1)
        dve.wait_ge(exp_ready, 1)
        nc.vector.tensor_reduce(s["gsum"][:, :], gt[:, :, 0:E], AX_X, ALU.add)
        link(nc.vector.tensor_reduce(s["csum"][:, :], gt[:, :, E:E + 2], AX_X, ALU.add))
        nc.vector.reciprocal(s["gmax"][:, :], s["gsum"][:, :])
        link(nc.vector.reciprocal(s["cmax"][:, :], s["csum"][:, :]))
        nc.vector.tensor_tensor(gt[:, :, 0:E], gt[:, :, 0:E], spread("gmax", E), ALU.mult)
        link(nc.vector.tensor_tensor(gt[:, :, E:E + 2], gt[:, :, E:E + 2], spread("cmax", 2), ALU.mult))
        w1v = work1[:, :].rearrange("p (t e) -> p t e", e=E)
        w2v = work2[:, :].rearrange("p (t e) -> p t e", e=E)
        chv = chosen[:, :].rearrange("p (t e) -> p t e", e=E)
        link(nc.vector.tensor_reduce(s["top"][:, :], gt[:, :, 0:E], AX_X, ALU.max))
        link(nc.vector.tensor_tensor(w1v, gt[:, :, 0:E], spread("top", E), ALU.is_equal))
        link(nc.vector.tensor_tensor(w1v, w1v, view(rank, 0, P, 0, [[0, TILES], [1, E]]), ALU.mult))
        link(nc.vector.tensor_reduce(s["first"][:, :], w1v, AX_X, ALU.max))
        link(nc.vector.tensor_tensor(chv, w1v, spread("first", E), ALU.is_equal))
        nc.vector.tensor_copy(chosen_bf[:, :], chosen[:, :]).then_inc(chosen_ready, 1)
        dve.wait_ge(l_full, 1)
        loc = ps_l[:, 64:64 + TILES * E]
        locv = loc.rearrange("p (t e) -> p t e", e=E)
        nc.vector.scalar_tensor_tensor(work1[:, :], loc, float(CAP), chosen[:, :], ALU.is_lt, ALU.mult)
        link(nc.vector.tensor_tensor(w2v, locv, view(first_slot, 0, P, 0, [[0, TILES], [1, E]]), ALU.add))
        nc.vector.tensor_reduce(s["kept"][:, :], w1v, AX_X, ALU.add)
        link(nc.vector.tensor_tensor(work2[:, :], work2[:, :], work1[:, :], ALU.mult))
        nc.vector.tensor_reduce(s["slot"][:, :], w2v, AX_X, ALU.add)
        link(nc.vector.tensor_tensor(s["lost"][:, :], s["kept"][:, :], spare[:, :], ALU.mult))
        link(nc.vector.tensor_tensor(s["lost"][:, :], spare[:, :], s["lost"][:, :], ALU.subtract))
        nc.vector.tensor_tensor(slot_i[:, :], s["slot"][:, :], s["lost"][:, :], ALU.add).then_inc(slots_ready, 1)
        link(nc.vector.tensor_tensor(s["share"][:, :], s["top"][:, :], s["kept"][:, :], ALU.mult))
        link(nc.vector.tensor_tensor(s["share"][:, :], s["share"][:, :], gt[:, :, E + 1], ALU.mult))
        link(nc.vector.tensor_copy(s["csum"][:, :], gt[:, :, E]))
        dve.wait_ge(base_ready, 4)
        dve.wait_ge(gate_in, 96)
        with dve.Fori(0, GRP // 2) as turn:
            for i in range(2):
                rv = res[i][:, :].rearrange("p (t d) -> p t d", d=D)
                dve.wait_ge(o_full, turn * 2 + (i + 1))
                nc.vector.tensor_tensor(rv, ps_o[:, i * 512:i * 512 + 512].rearrange("p (t d) -> p t d", d=D),
                                        view(res_b2, 0, P, 0, [[0, 4], [1, D]]), ALU.add).then_inc(o_done, 1)
                dve.wait_ge(o_done, turn * 2 + (BANKS + i + 1))
                c0 = s["csum"][:, bass.ds(turn * 8 + 4 * i, 4)].unsqueeze(2).to_broadcast([P, 4, D])
                nc.vector.tensor_tensor(rv, rv, c0, ALU.mult).then_inc(res_link, 1)
                dve.wait_ge(res_link, turn * 2 + (i + 1))
                xs = x_sb[:, bass.ds(turn * 1024 + 512 * i, 512)]
                nc.vector.tensor_tensor(xs, xs, res[i][:, :], ALU.add).then_inc(res_added, 1)
        with dve.Fori(0, E // 2) as turn:
            for i in range(2):
                dve.wait_ge(o_full, turn * 2 + (GRP + 1 + i))
                be = b2[:, bass.ds(turn * (2 * D) + i * D, D)].unsqueeze(1).to_broadcast([P, 4, D])
                nc.vector.tensor_tensor(eo[i][:, :].rearrange("p (t d) -> p t d", d=D),
                                        ps_o[:, i * 512:i * 512 + 512].rearrange("p (t d) -> p t d", d=D),
                                        be, ALU.add).then_inc(o_done, 1)
        dve.wait_ge(res_added, GRP)
        for i in range(4):
            dve.wait_ge(moe_in[i], 16)
            for t in range(TILES // 4 * i, TILES // 4 * (i + 1)):
                ins = nc.vector.scalar_tensor_tensor(xg[:, t, :], yg[:, t, :], s["share"][:, t:t + 1], xg[:, t, :],
                                                     ALU.mult, ALU.add)
            ins.then_inc(fin, 1)

    @block.tensor
    def _(pe):
        pe.wait_ge(consts_ready, 1)
        pe.wait_ge(weights_in, 64)
        nc.tensor.transpose(ps_l[:, 0:VEC], vecs[0:VEC, :], ident[0:VEC, 0:VEC]).then_inc(vecs_full, 1)
        pe.wait_ge(gate_in, 96)
        for n in range(GRP):
            pe.wait_ge(rows_ready, 4 * n + 4)
            if n >= 2:
                pe.wait_ge(t_done, n - 1)
            for t in range(4):
                T = 4 * n + t
                last = nc.tensor.transpose(ps_t[:, (n % 2) * 512 + t * P:(n % 2) * 512 + t * P + P], rg[:, T, 0:D],
                                           ident[:, :])
            last.then_inc(t_full, 1)
        for n in range(GRP):
            pe.wait_ge(t_done, n + 1)
            for T in range(4 * n, 4 * n + 4):
                last = nc.tensor.matmul(ps_g[:, T * (E + 2):(T + 1) * (E + 2)], a_t[:, T * P:T * P + P], w_gate[:, :],
                                        start=True, stop=True)
        last.then_inc(g_full, 1)
        pe.wait_ge(chosen_ready, 1)
        nc.tensor.matmul(ps_l[:, 64:64 + TILES * E], before[:, :], chosen_bf[:, :], start=True, stop=False)
        for k in range(1, TILES):
            last = nc.tensor.matmul(ps_l[:, 64 + k * E:64 + TILES * E], ones[:, :], chosen_bf[:, 0:(TILES - k) * E],
                                    start=False, stop=(k == TILES - 1))
        last.then_inc(l_full, 1)

        def inner(base, wa, moving):
            for c in range(CH):
                pe.wait_ge(h_done, base + (c + 1))
                nc.tensor.matmul(ps_h[:, (c % 2) * 512:(c % 2) * 512 + 512], wa[:, c * P:c * P + P], moving,
                                 start=True, stop=True).then_inc(h_full, 1)

        def outer(base, passes, i, wb):
            pe.wait_ge(h_done, base + (BANKS + CH))
            pe.wait_ge(o_done, passes + 1)
            for j in range(4):
                for c in range(CH):
                    last = nc.tensor.matmul(ps_o[:, i * 512 + j * D:i * 512 + j * D + D],
                                            h_t[i][:, c * 512 + j * P:c * 512 + j * P + P],
                                            wb[:, c * D:c * D + D], start=(c == 0), stop=(c == CH - 1))
            last.then_inc(o_full, 1)

        with pe.Fori(0, GRP // 2) as turn:
            for i in range(2):
                base = turn * (2 * CH) + CH * i
                inner(base, res_w1, a_t[:, bass.ds(turn * 1024 + 512 * i, 512)])
                outer(base, turn * 2 + i, i, res_w2)
        with pe.Fori(0, E // 2) as turn:
            for i in range(2):
                base = turn * (2 * CH) + (GRP * CH + CH * i)
                pe.wait_ge(xe_loaded[i], turn * 16 + 16)
                for j in range(4):
                    last = nc.tensor.transpose(ps_t[:, i * 512 + j * P:i * 512 + j * P + P],
                                               xe[i][:, j * ROW:j * ROW + D], ident[:, :])
                last.then_inc(xt_full, 1)
                pe.wait_ge(we_loaded[i], turn * 32 + 32)
                pe.wait_ge(xt_done, turn * 2 + (i + 1))
                inner(base, w1[i], xe_t[i][:, :])
                outer(base, turn * 2 + (GRP + i), i, w2[i])


_INS = ['x', 'w_q', 'w_kv', 'w_out', 'b_out', 'sort_w']
_FFN = ['attn_nw', 'attn_nb', 'wg', 'inter_w', 'inter_b', 'output_w', 'output_b', 'res_inter_w', 'res_inter_b',
        'res_output_w', 'res_output_b', 'res_coef']


def program(nc, A, out):
    with ExitStack() as outer:
        x_sb = outer.enter_context(nc.sbuf_tensor("x_sb", [P, TILES * D], F32))
        with ExitStack() as ctx:
            attention_block(nc, ctx, x_sb, A)
        with ExitStack() as ctx:
            feed_forward_block(nc, ctx, x_sb, A, out)


def kernel(**inputs):
    import numpy as _np
    import concourse.bacc as _bacc
    from concourse import mybir as _mybir
    from concourse.bass_utils import run_bass_kernel_spmd as _run

    nc = _bacc.Bacc("TRN2", target_bir_lowering=False, num_devices=1)
    arrays, args = {}, {}
    for prefix, names in (("L0_attn_", _INS), ("L0_ffn_", _FFN)):
        for name in names:
            a = _np.ascontiguousarray(inputs[prefix + name])
            arrays[f"in_{name}_dram"] = a
            args[name] = nc.dram_tensor(f"in_{name}_dram", a.shape, _mybir.dt.from_np(a.dtype), kind="ExternalInput").ap()
    out = nc.dram_tensor("out_0_dram", (8, SEQ, D), _mybir.dt.float32, kind="ExternalOutput").ap()
    program(nc, args, out)
    r = _run(nc, [arrays], core_ids=[0])
    return r.results[0]["out_0_dram"]
```

```python
from contextlib import ExitStack

import concourse.bass as bass
from concourse import mybir

F32 = mybir.dt.float32
BF16 = mybir.dt.bfloat16
I32 = mybir.dt.int32
ALU = mybir.AluOpType
ACT = mybir.ActivationFunctionType
AX_X = mybir.AxisListType.X

P = 128
TILES = 32
D = 128
DH = 64
HEADS = 16
LOCAL_HEADS = 4
SORT_HEADS = HEADS - LOCAL_HEADS
BUCKETS = 64
W = 8
SEQ = BUCKETS * W
TURNS = 4
TOK = 2 * SEQ
CHUNKS = 4
UNITS = 16
GROUPS = 8
WIN = 10 * W
WIDE = 12 * W
PAD = W + SEQ + 3 * W
EXPERTS = 8
CAP = 512
INTER = 512
OUT_OF_SEQUENCE = -1.0e30


def view(t, part, nparts, offset, dims):
    row = t.shape[1]
    return bass.AP(tensor=t, offset=part * row + offset, ap=[[row, nparts]] + dims)


def layer_norm_steps(nc, link, x, stats, small, n, eps, var_ready, wait_root):
    for t in range(n):
        last = nc.vector.bn_stats(stats[:, 6 * t:6 * t + 6], x(t))
    link(last)
    st = stats[:, 0:6 * n].rearrange("p (t s) -> p s t", s=6)
    mean, rstd, a, b, v = (small[:, i * TILES:i * TILES + n] for i in range(5))
    nc.vector.tensor_tensor(a, st[:, 1, :], st[:, 4, :], ALU.add)
    nc.vector.tensor_tensor(b, st[:, 1, :], st[:, 4, :], ALU.subtract)
    link(nc.vector.tensor_tensor(v, st[:, 2, :], st[:, 5, :], ALU.add))
    nc.vector.tensor_scalar(mean, a, 0.5, None, ALU.mult)
    nc.vector.tensor_scalar(v, v, 1.0 / D, eps, ALU.mult, ALU.add)
    link(nc.vector.tensor_tensor(b, b, b, ALU.mult))
    nc.vector.scalar_tensor_tensor(v, b, 0.25, v, ALU.mult, ALU.add).then_inc(var_ready, 1)
    wait_root()
    link(nc.vector.reciprocal(rstd, a))
    link(nc.vector.tensor_tensor(b, rstd, rstd, ALU.mult))
    link(nc.vector.tensor_tensor(b, b, v, ALU.mult))
    link(nc.vector.tensor_scalar(b, b, -0.5, 1.5, ALU.mult, ALU.add))
    link(nc.vector.tensor_tensor(rstd, rstd, b, ALU.mult))


EMPTIED_BY = {"feats": "act", "v": "act", "k": "act", "rt": "act", "q": "act", "kn": "act", "vr": "act",
              "logits": "dve", "kr": "dve", "out": "dve"}


def plan(chunks, following):
    def four(name, c):
        return [(name, c, n) for n in range(4)]

    steps = []
    for c in chunks:
        nxt = c + 1 if c + 1 < CHUNKS else 0
        if nxt:
            early = [four("v", nxt), four("k", nxt) + [("rt", nxt)], four("kn", nxt), four("vr", nxt)]
        elif following:
            early = [four("v", 0), [("feats", g) for g in range(3)], four("k", 0)[:2] + [("logits", 0), ("logits", 1)],
                     four("k", 0)[2:]]
        else:
            early = [[], [], [], []]
        for k in range(4):
            u, jobs = 4 * c + k, early[k]
            steps.append(("scores", u))
            if k:
                steps += jobs[:2] + [("to keys", u - 1)] + jobs[2:3] + [("softmax", u)] + jobs[3:] + [("values", u - 1)]
            elif c:
                steps += [("out", c - 1, 0), ("out", c - 1, 1), ("softmax", u)] + jobs
            else:
                steps += jobs[:2] + [("softmax", u)] + jobs[2:]
            if k == 2 and not nxt and following:
                steps.append(("R",))
        if nxt or following:
            q = four("q", nxt)
            steps += q[:2] + [("to keys", u)] + q[2:]
        else:
            steps.append(("to keys", u))
        if nxt:
            steps += [("own keys", nxt)] + four("kr", nxt)
        if nxt == 3 and following:
            steps.append(("next x",))
        steps.append(("values", u))
    steps += [("out", CHUNKS - 1, 0), ("out", CHUNKS - 1, 1)]
    return steps


def first_plan():
    four = range(4)
    return ([("v", 0, n) for n in four] + [("root",)] + [("feats", g) for g in range(3)] + [("k", 0, n) for n in four] +
            [("logits", 0), ("logits", 1), ("R",)] + [("q", 0, n) for n in four])


class Banks:
    def __init__(self, steps, base, it=None, per_turn=None):
        self.order = [s for s in steps if s[0] in EMPTIED_BY]
        self.base, self.it, self.per_turn = base, it, per_turn
        self.count = {"full": 0, "act": 0, "dve": 0}
        self.nth = {}
        for job in self.order:
            who = EMPTIED_BY[job[0]]
            self.nth[job] = (self.count["full"], self.count[who])
            self.count["full"] += 1
            self.count[who] += 1

    def value(self, which, n):
        v = self.base[which] + n
        return v if self.it is None else self.it * self.per_turn[which] + v

    def total(self):
        return {k: self.base[k] + self.count[k] for k in self.base}


def attention_block(nc, ctx, x_sb, A):
    def sb(name, cols, dt=F32):
        return ctx.enter_context(nc.sbuf_tensor(name, [P, cols], dt))

    def psum(name, cols):
        return ctx.enter_context(nc.psum_tensor(name, [P, cols], F32))

    def sem(name):
        return ctx.enter_context(nc.semaphore(name))

    w_qkv = sb("w_qkv", 3 * 1024)
    w_out = sb("w_out", 8 * D)
    sort_w = sb("sort_w", SORT_HEADS * BUCKETS)
    bias_out = sb("bias_out", D)
    xn_t = sb("xn_t", (TURNS - 1) * TOK)
    xn_cur = sb("xn_cur", TOK)
    xsum_cur = sb("xsum_cur", P)
    r_blk = sb("r_blk", SORT_HEADS * P)
    r_t = sb("r_t", 4 * P)
    v_nat = sb("v_nat", W * 256)
    k_nat = sb("k_nat", W * 256)
    v_re = sb("v_re", W * 256)
    feats_t = v_re
    k_t = sb("k_t", 2 * TOK)
    keys_t = sb("keys_t", 2 * 16 * P)
    keys_loc = sb("keys_loc", 4 * PAD)
    q_diag = sb("q_diag", 4 * TOK)
    vals = [sb(f"vals{i}", 16 * 256) for i in range(2)]
    att_t = sb("att_t", 2 * TOK)
    s_masked = sb("s_masked", GROUPS * P)
    r_exp = sb("r_exp", SORT_HEADS * BUCKETS)
    p_t = [sb(f"p_t{i}", GROUPS * P) for i in range(2)]
    ident = sb("ident", P)
    mask_sort = sb("mask_sort", 64)
    mask_loc = sb("mask_loc", WIDE)
    edge = sb("edge", GROUPS * 24)
    shifted = sb("shifted", GROUPS * 24)
    probs = sb("probs", GROUPS * 24)
    p_wide = sb("p_wide", GROUPS * P)
    stat = sb("stat", 3 * GROUPS)
    rstat = sb("rstat", 3 * 16)
    bn = sb("bn", 6 * TILES)
    ln_small = sb("ln_small", 5 * TILES)
    xn_nat = vals[1]

    work = psum("work", 1024)
    ps_s = psum("ps_s", 1024)
    ps_e = psum("ps_e", 1024)
    ps_o = psum("ps_o", 512)

    x_loaded = [sem(f"x_loaded{i}") for i in range(TURNS)]
    w_qkv_loaded = sem("w_qkv_loaded")
    sort_loaded = sem("sort_loaded")
    out_loaded = sem("out_loaded")
    ident_ready = sem("ident_ready")
    consts_ready = sem("consts_ready")
    pool_chain = sem("pool_chain")
    var_ready = sem("var_ready")
    root_ready = sem("root_ready")
    xn_ready = sem("xn_ready")
    xt_full = sem("xt_full")
    xt_done = sem("xt_done")
    x_biased = sem("x_biased")
    cur_ready = sem("cur_ready")
    xsum_ready = sem("xsum_ready")
    dve_chain = sem("dve_chain")
    work_full = sem("work_full")
    work_act = sem("work_act")
    work_dve = sem("work_dve")
    r_link = sem("r_link")
    r_exped = sem("r_exped")
    r_ready = sem("r_ready")
    own_loaded = sem("own_loaded")
    mixed_loaded = sem("mixed_loaded")
    loc_loaded = sem("loc_loaded")
    keys_copied = sem("keys_copied")
    s_full = sem("s_full")
    s_done = sem("s_done")
    picked = sem("picked")
    edge_done = sem("edge_done")
    max_done = sem("max_done")
    shifted_ready = sem("shifted_ready")
    exped = sem("exped")
    sum_done = sem("sum_done")
    inv_done = sem("inv_done")
    p_ready = sem("p_ready")
    p_spread = sem("p_spread")
    e_full = sem("e_full")
    e_done = sem("e_done")
    o_full = sem("o_full")
    o_done = sem("o_done")

    xg = x_sb[:, :].rearrange("p (t d) -> p t d", d=D)
    PART = TILES // TURNS

    FIRST, TURN, LAST = first_plan(), plan(range(CHUNKS), True), plan(range(CHUNKS), False)
    before_first = {"full": 0, "act": 0, "dve": 0}
    before_turns = Banks(FIRST, before_first).total()
    per_turn = Banks(TURN, before_first).count

    def first_banks():
        return Banks(FIRST, before_first)

    def turn_banks(it):
        return Banks(TURN, before_turns, it, per_turn)

    def last_banks():
        return Banks(LAST, {k: before_turns[k] + (TURNS - 1) * per_turn[k] for k in per_turn})

    def full(eng, banks, job):
        eng.wait_ge(work_full, banks.value("full", banks.nth[job][0] + 1))

    def emptied(eng, banks, job):
        who = EMPTIED_BY[job[0]]
        eng.wait_ge(work_act if who == "act" else work_dve, banks.value(who, banks.nth[job][1] + 1))

    def bank(banks, job):
        o = banks.nth[job][0] % 2 * 512
        return work[:, o:o + 512]

    block = ctx.enter_context(nc.Block())

    @block.sync
    def _(sp):
        xd = A["x"].rearrange("b (t p) d -> p (b t) d", p=P)

        def load_x(i):
            sp.dma_start(xg[:, PART * i:PART * (i + 1), :], xd[:, PART * i:PART * (i + 1), :]).then_inc(x_loaded[i], 16)

        load_x(0)
        sp.dma_start(w_qkv[:, 1024:3072], A["w_kv"]).then_inc(w_qkv_loaded, 16)
        sp.dma_start(w_qkv[:, 0:1024], A["w_q"]).then_inc(w_qkv_loaded, 16)
        load_x(1)
        sp.dma_start(sort_w[:, :].rearrange("p (h v) -> p h v", h=SORT_HEADS),
                     A["sort_w"].rearrange("a h d v -> d (a h) v")).then_inc(sort_loaded, 16)
        load_x(2)
        load_x(3)
        sp.dma_start(bias_out[:, :], A["b_out"].rearrange("(a d) -> a d", a=1).to_broadcast([P, D])).then_inc(out_loaded, 16)
        sp.dma_start(w_out[:, :].rearrange("p (n d) -> p n d", n=8),
                     A["w_out"].rearrange("(n p) d -> p n d", p=P)).then_inc(out_loaded, 16)

        def local_values(banks):
            emptied(sp, banks, ("v", 0, 3))
            for b in range(2):
                for g in range(GROUPS):
                    lo = 1 if g == 0 else 0
                    hi = 9 if g == GROUPS - 1 else 10
                    src = BUCKETS * b + GROUPS * g - 1
                    sp.dma_start(view(vals[0], lo * W, (hi - lo) * W, (b * GROUPS + g) * 256, [[1, 256]]),
                                 view(v_nat, src + lo, hi - lo, 0, [[256, W], [1, 256]])).then_inc(loc_loaded, 16)

        def turn(banks, following):
            for c in range(1, CHUNKS):
                emptied(sp, banks, ("v", c, 3))
                for g in range(16):
                    sp.dma_start(view(vals[c % 2], 0, 64, g * 256, [[1, 256]]),
                                 view(v_nat, 8 * g, 8, 0, [[256, W], [1, 256]])).then_inc(own_loaded, 16)
                emptied(sp, banks, ("vr", c, 3))
                for g in range(16):
                    sp.dma_start(view(vals[c % 2], 64, 64, g * 256, [[1, 256]]),
                                 view(v_re, 8 * g, 8, 0, [[256, W], [1, 256]])).then_inc(mixed_loaded, 16)
            if following:
                local_values(banks)

        sp.wait_ge(consts_ready, 1)
        local_values(first_banks())
        with sp.Fori(0, TURNS - 1) as it:
            turn(turn_banks(it), True)
        turn(last_banks(), False)

    @block.gpsimd
    def _(pool):
        done = [0]

        def link(ins):
            done[0] += 1
            ins.then_inc(pool_chain, 1)
            pool.wait_ge(pool_chain, done[0])

        link(nc.gpsimd.memset(ident[:, :], 0.0))
        nc.gpsimd.affine_select(out=ident[:, :], in_=ident[:, :], compare_op=ALU.not_equal, fill=1.0,
                                base=0, pattern=[[-1, P]], channel_multiplier=1).then_inc(ident_ready, 1)
        nc.gpsimd.memset(vals[0][:, :], 0.0)
        nc.gpsimd.memset(keys_loc[:, :], 0.0)
        nc.gpsimd.memset(r_blk[:, :], 0.0)
        nc.gpsimd.memset(q_diag[:, :], 0.0).then_inc(consts_ready, 1)
        nc.gpsimd.memset(mask_sort[:, :], 1.0)
        nc.gpsimd.memset(mask_loc[:, :], 1.0)
        link(nc.gpsimd.memset(edge[:, :], 0.0))
        for p0 in (0, 64):
            v = mask_sort[p0:p0 + 64, :].rearrange("p (u t) -> p u t", t=W)
            link(nc.gpsimd.affine_select(out=v, in_=v, compare_op=ALU.is_ge, fill=0.0, base=0,
                                         pattern=[[-8, 8], [0, 8]], channel_multiplier=1))
            link(nc.gpsimd.affine_select(out=v, in_=v, compare_op=ALU.is_ge, fill=0.0, base=7,
                                         pattern=[[8, 8], [0, 8]], channel_multiplier=-1))
            v = mask_loc[p0:p0 + 64, :].rearrange("p (w t) -> p w t", t=W)
            link(nc.gpsimd.affine_select(out=v, in_=v, compare_op=ALU.is_ge, fill=0.0, base=7,
                                         pattern=[[8, 12], [0, 8]], channel_multiplier=-1))
            link(nc.gpsimd.affine_select(out=v, in_=v, compare_op=ALU.is_ge, fill=0.0, base=16,
                                         pattern=[[-8, 12], [0, 8]], channel_multiplier=1))
            first = edge[p0:p0 + 64, 0:W]
            last = edge[p0:p0 + 64, 7 * 24:7 * 24 + W]
            link(nc.gpsimd.affine_select(out=first, in_=first, compare_op=ALU.is_ge, fill=OUT_OF_SEQUENCE,
                                         base=-8, pattern=[[0, W]], channel_multiplier=1))
            link(nc.gpsimd.affine_select(out=last, in_=last, compare_op=ALU.is_ge, fill=OUT_OF_SEQUENCE,
                                         base=55, pattern=[[0, W]], channel_multiplier=-1))
        nc.gpsimd.memset(stat[:, :], 0.0).then_inc(consts_ready, 1)
        pool.wait_ge(out_loaded, 32)
        for i in range(TURNS):
            pool.wait_ge(xn_ready, 2 * i + 2)
            xv = xg[:, PART * i:PART * (i + 1), :]
            nc.gpsimd.tensor_tensor(xv, xv, view(bias_out, 0, P, 0, [[0, PART], [1, D]]), ALU.add).then_inc(x_biased, 1)

        def turn(it, steps, banks):
            for step in steps:
                if step[0] == "next x":
                    full(pool, banks, ("q", 3, 3))
                    nc.gpsimd.tensor_copy(xn_cur[:, :], xn_t[:, bass.ds(it * TOK, TOK)]).then_inc(cur_ready, 1)
                elif step[0] == "softmax":
                    u = step[1]
                    pool.wait_ge(p_ready, it * UNITS + (u + 1))
                    if u:
                        pool.wait_ge(e_full, it * UNITS + u)
                    if u < 4:
                        shape, src, m = (GROUPS, 4, 24), [[24, GROUPS], [0, 4], [1, 24]], (mask_loc, [[0, GROUPS], [24, 4], [1, 24]])
                    else:
                        shape, src, m = (2 * GROUPS, W, W), [[W, 2 * GROUPS], [0, W], [1, W]], (mask_sort, [[0, 2 * GROUPS], [W, W], [1, W]])
                    n = shape[0] * shape[1] * shape[2]
                    nc.gpsimd.tensor_tensor(p_wide[:, 0:n].rearrange("p (a m b) -> p a m b", m=shape[1], b=shape[2]),
                                            view(probs, 0, P, 0, src), view(m[0], 0, P, 0, m[1]),
                                            ALU.mult).then_inc(p_spread, 1)

        with pool.Fori(0, TURNS - 1) as it:
            turn(it, TURN, turn_banks(it))
        turn(TURNS - 1, LAST, last_banks())

    @block.scalar
    def _(act):
        def root(i):
            act.wait_ge(var_ready, i + 1)
            nc.scalar.activation(ln_small[:, 2 * TILES:2 * TILES + PART], ln_small[:, 4 * TILES:4 * TILES + PART],
                                 ACT.Sqrt).then_inc(root_ready, 1)

        def transposed(n):
            act.wait_ge(xt_full, n + 1)
            dst = xn_cur[:, n * 512:n * 512 + 512] if n < 2 else xn_t[:, (n - 2) * 512:(n - 1) * 512]
            nc.scalar.copy(dst, work[:, (n % 2) * 512:(n % 2) * 512 + 512]).then_inc(xt_done, 1)

        def turn(it, steps, banks):
            def empty(job, dst, src):
                full(act, banks, job)
                nc.scalar.copy(dst, src).then_inc(work_act, 1)

            for step in steps:
                kind = step[0]
                if kind == "root":
                    root(1)
                elif kind == "feats":
                    if step[1] == 0 and steps is TURN:
                        act.wait_ge(mixed_loaded, it * 768 + 768)
                    g = step[1]
                    empty(step, feats_t[:, g * 512:g * 512 + 512], bank(banks, step))
                elif kind == "R":
                    emptied(act, banks, ("logits", 1))
                    nc.scalar.activation(r_exp[:, :], r_exp[:, :], ACT.Exp).then_inc(r_exped, 1)
                elif kind == "v":
                    c, n = step[1:]
                    if n == 0:
                        if c == 1:
                            act.wait_ge(loc_loaded, it * 256 + 256)
                        elif steps is not FIRST:
                            act.wait_ge(own_loaded, it * 768 + 256 * ((c - 1) % CHUNKS))
                    empty(step, v_nat[:, n * 512:n * 512 + 512], bank(banks, step))
                elif kind == "k":
                    c, n = step[1:]
                    pp, b = divmod(n, 2)
                    o = (pp * 2 + b) * PAD + W
                    if c == 0 and n == 0:
                        act.wait_ge(consts_ready, 1)
                    empty(step, k_t[:, n * 512:n * 512 + 512] if c else keys_loc[:, o:o + SEQ], bank(banks, step))
                elif kind == "rt":
                    empty(step, r_t[:, :], bank(banks, step))
                elif kind == "q":
                    c, n = step[1:]
                    full(act, banks, step)
                    src = bank(banks, step)
                    for j in range(2):
                        ins = nc.scalar.copy(view(q_diag, 64 * j, 64, n * 1024 + j * 64, [[P, GROUPS], [1, 64]]),
                                             src[64 * j:64 * j + 64, :].rearrange("p (g q) -> p g q", q=64))
                    ins.then_inc(work_act, 1)
                elif kind == "kn":
                    c, n = step[1:]
                    empty(step, k_nat[:, n * 512:n * 512 + 512], bank(banks, step))
                elif kind == "vr":
                    c, n = step[1:]
                    if c > 1 and n == 0:
                        act.wait_ge(mixed_loaded, it * 768 + 256 * (c - 1))
                    empty(step, view(v_re, 0, P, n * 64, [[256, W], [1, 64]]),
                          bank(banks, step).rearrange("p (t d) -> p t d", t=W))
                elif kind == "softmax":
                    u = step[1]
                    n = GROUPS * (24 if u < 4 else 16)
                    act.wait_ge(shifted_ready, it * UNITS + (u + 1))
                    nc.scalar.activation(shifted[:, 0:n], shifted[:, 0:n], ACT.Exp,
                                         scale=1.0 if u < 4 else DH ** -0.5).then_inc(exped, 1)
                elif kind == "to keys":
                    u = step[1]
                    n = WIDE if u < 4 else P
                    act.wait_ge(e_full, it * UNITS + (u + 1))
                    nc.scalar.copy(p_t[u % 2][0:n, :], ps_e[0:n, :]).then_inc(e_done, 1)
                elif kind == "values":
                    u = step[1]
                    c, pp, b = u // 4, u // 2 % 2, u % 2
                    if u % 4 == 0 and c:
                        full(act, banks, ("out", c - 1, 1))
                    act.wait_ge(o_full, it * UNITS + (u + 1))
                    nc.scalar.copy(att_t[:, pp * TOK + b * SEQ:pp * TOK + (b + 1) * SEQ], ps_o[:, :]).then_inc(o_done, 1)

        root(0)
        for n in range(2):
            transposed(n)
        turn(-1, FIRST, first_banks())
        for i in (2, 3):
            root(i)
        for n in range(2, TILES // 4):
            transposed(n)
        with act.Fori(0, TURNS - 1) as it:
            turn(it, TURN, turn_banks(it))
        turn(TURNS - 1, LAST, last_banks())

    @block.vector
    def _(dve):
        done = [0]

        def link(ins):
            done[0] += 1
            ins.then_inc(dve_chain, 1)
            dve.wait_ge(dve_chain, done[0])

        def normalise(i):
            dve.wait_ge(x_loaded[i], 16)
            layer_norm_steps(nc, link, lambda t: xg[:, PART * i + t, :], bn, ln_small, PART, 1e-5,
                             var_ready, lambda: dve.wait_ge(root_ready, i + 1))
            for t in range(PART):
                T = PART * i + t
                ins = nc.vector.tensor_scalar(xn_nat[:, T * D:T * D + D], xg[:, T, :], ln_small[:, t:t + 1],
                                              ln_small[:, TILES + t:TILES + t + 1], ALU.subtract, ALU.mult)
                if t % 4 == 3:
                    ins.then_inc(xn_ready, 1)
            dve.wait_ge(xn_ready, 2 * i + 2)

        def bucket_sums():
            nc.vector.tensor_reduce(xsum_cur[:, :], xn_cur[:, :].rearrange("p (b w) -> p b w", w=W), AX_X,
                                    ALU.add).then_inc(xsum_ready, 1)

        def turn(it, steps, banks):
            rmax, rsum, rinv = (rstat[:, 16 * k:16 * k + SORT_HEADS] for k in range(3))
            hs = [(0, 8), (8, 12)]
            R_LINKS = 4

            def rlink(k, ins):
                ins.then_inc(r_link, 1)
                dve.wait_ge(r_link, it * R_LINKS + (R_LINKS + k + 1))

            def sort_matrix():
                lw = [bank(banks, ("logits", g))[:, 0:(b - a) * 64].rearrange("p (h v) -> p h v", v=BUCKETS)
                      for g, (a, b) in enumerate(hs)]
                full(dve, banks, ("logits", 0))
                nc.vector.tensor_reduce(rmax[:, 0:8], lw[0], AX_X, ALU.max)
                full(dve, banks, ("logits", 1))
                rlink(0, nc.vector.tensor_reduce(rmax[:, 8:12], lw[1], AX_X, ALU.max))
                rlink(1, nc.vector.tensor_scalar(rmax, rmax, 0.0, None, ALU.max))
                for g, (a, b) in enumerate(hs):
                    nc.vector.scalar_tensor_tensor(
                        r_exp[:, a * 64:b * 64].rearrange("p (h v) -> p h v", v=BUCKETS), lw[g], 0.0,
                        view(rstat, 0, P, a, [[1, b - a], [0, BUCKETS]]), ALU.max, ALU.subtract).then_inc(work_dve, 1)
                dve.wait_ge(r_exped, it + 2)
                re3 = r_exp[:, :].rearrange("p (h v) -> p h v", v=BUCKETS)
                rlink(2, nc.vector.tensor_reduce(rsum, re3, AX_X, ALU.add))
                rlink(3, nc.vector.reciprocal(rinv, rsum))
                for b in range(2):
                    nc.vector.tensor_tensor(
                        view(r_blk, 64 * b, 64, 64 * b, [[P, SORT_HEADS], [1, 64]]),
                        view(r_exp, 64 * b, 64, 0, [[64, SORT_HEADS], [1, 64]]),
                        view(rstat, 64 * b, 64, 32, [[1, SORT_HEADS], [0, 64]]), ALU.mult).then_inc(r_ready, 1)

            def shifted_scores(u):
                width, blocks, m = (WIDE, GROUPS, mask_loc) if u < 4 else (64, 2 * GROUPS, mask_sort)
                k = 24 if u < 4 else 16
                sv = shifted[:, 0:GROUPS * k]
                sv3 = sv.rearrange("p (g k) -> p g k", k=k)
                dve.wait_ge(s_full, it * UNITS + (u + 1))
                nc.vector.tensor_tensor(s_masked[:, 0:blocks * width].rearrange("p (a k) -> p a k", k=width),
                                        view(ps_s, 0, P, 0, [[1024 // blocks, blocks], [1, width]]),
                                        view(m, 0, P, 0, [[0, blocks], [1, width]]), ALU.mult).then_inc(s_done, 1)
                src = s_masked[:, 0:GROUPS * WIDE].rearrange("p (g m k) -> p g k m", g=GROUPS, m=4) if u < 4 else \
                    s_masked[:, :].rearrange("p (a u t) -> p a t u", u=W, t=W)
                dst = sv3 if u < 4 else sv.rearrange("p (a t) -> p a t", t=W)
                dve.wait_ge(s_done, it * UNITS + (u + 1))
                nc.vector.tensor_reduce(dst, src, AX_X, ALU.add).then_inc(picked, 1)
                dve.wait_ge(picked, it * UNITS + (u + 1))
                if u < 4:
                    nc.vector.tensor_tensor(sv, sv, edge[:, :], ALU.add).then_inc(edge_done, 1)
                    dve.wait_ge(edge_done, it * 4 + (u + 1))
                nc.vector.tensor_reduce(stat[:, 0:GROUPS], sv3, AX_X, ALU.max).then_inc(max_done, 1)
                dve.wait_ge(max_done, it * UNITS + (u + 1))
                nc.vector.tensor_tensor(sv3, sv3, view(stat, 0, P, 0, [[1, GROUPS], [0, k]]),
                                        ALU.subtract).then_inc(shifted_ready, 1)

            def probabilities(u):
                k = 24 if u < 4 else 16
                sv3 = shifted[:, 0:GROUPS * k].rearrange("p (g k) -> p g k", k=k)
                dve.wait_ge(exped, it * UNITS + (u + 1))
                nc.vector.tensor_reduce(stat[:, GROUPS:2 * GROUPS], sv3, AX_X, ALU.add).then_inc(sum_done, 1)
                dve.wait_ge(sum_done, it * UNITS + (u + 1))
                nc.vector.reciprocal(stat[:, 2 * GROUPS:3 * GROUPS], stat[:, GROUPS:2 * GROUPS]).then_inc(inv_done, 1)
                dve.wait_ge(inv_done, it * UNITS + (u + 1))
                if u:
                    dve.wait_ge(p_spread, it * UNITS + u)
                nc.vector.tensor_tensor(probs[:, 0:GROUPS * k].rearrange("p (g k) -> p g k", k=k), sv3,
                                        view(stat, 0, P, 2 * GROUPS, [[1, GROUPS], [0, k]]), ALU.mult).then_inc(p_ready, 1)

            for step in steps:
                if step[0] == "R":
                    sort_matrix()
                elif step[0] == "scores":
                    shifted_scores(step[1])
                elif step[0] == "softmax":
                    probabilities(step[1])
                elif step[0] == "own keys":
                    emptied(dve, banks, ("k", step[1], 3))
                    nc.vector.tensor_copy(view(keys_t, 0, P, 0, [[P, 32], [1, 64]]),
                                          k_t[:, :].rearrange("p (g k) -> p g k", k=64)).then_inc(keys_copied, 1)
                elif step[0] == "kr":
                    c, n = step[1:]
                    pp, half = divmod(n, 2)
                    full(dve, banks, step)
                    nc.vector.tensor_copy(view(keys_t, 0, P, pp * 16 * P + 64 + half * 4, [[1, 4], [P, 16], [8, 8]]),
                                          bank(banks, step).rearrange("p (t g u) -> p t g u", t=4, g=16)).then_inc(work_dve, 1)
                elif step[0] == "next x":
                    dve.wait_ge(cur_ready, it + 1)
                    bucket_sums()
                elif step[0] == "out":
                    n = step[2]
                    full(dve, banks, step)
                    xs = x_sb[:, bass.ds(it * TOK + n * 512, 512)]
                    nc.vector.tensor_tensor(xs, xs, bank(banks, step), ALU.add).then_inc(work_dve, 1)

        normalise(0)
        dve.wait_ge(xt_done, 2)
        bucket_sums()
        normalise(1)
        dve.wait_ge(consts_ready, 1)
        turn(-1, FIRST, first_banks())
        for i in (2, 3):
            normalise(i)
        dve.wait_ge(consts_ready, 2)
        dve.wait_ge(x_biased, TURNS)
        with dve.Fori(0, TURNS - 1) as it:
            turn(it, TURN, turn_banks(it))
        turn(TURNS - 1, LAST, last_banks())

    @block.tensor
    def _(pe):
        def transposed(n):
            pe.wait_ge(xn_ready, n + 1)
            if n > 2:
                pe.wait_ge(xt_done, n - 1)
            for t in range(4):
                T = 4 * n + t
                last = nc.tensor.transpose(work[:, (n % 2) * 512 + t * P:(n % 2) * 512 + t * P + P],
                                           xn_nat[:, T * D:T * D + D], ident[:, :])
            last.then_inc(xt_full, 1)

        def turn(it, steps, banks):
            def free_bank(job):
                n = banks.nth[job][0]
                if n >= 2:
                    emptied(pe, banks, banks.order[n - 2])
                elif n == 0 and steps is not FIRST:
                    pe.wait_ge(work_act, banks.value("act", 0))
                    pe.wait_ge(work_dve, banks.value("dve", 0))
                return bank(banks, job)

            def scores(u):
                c, pp, b = u // 4, u // 2 % 2, u % 2
                if u == 0:
                    pe.wait_ge(work_act, banks.value("act", 0))
                elif u % 4 == 0:
                    emptied(pe, banks, ("q", c, 3))
                    emptied(pe, banks, ("kr", c, 3))
                    pe.wait_ge(keys_copied, it * 3 + c)
                if u:
                    pe.wait_ge(s_done, it * UNITS + u)
                for g in range(GROUPS):
                    if c == 0:
                        keys = view(keys_loc, 0, P, (pp * 2 + b) * PAD + g * 64, [[1, WIDE]])
                    else:
                        keys = view(keys_t, 0, P, (pp * 16 + b * 8 + g) * P, [[1, P]])
                    o = (pp * 16 + b * 8 + g) * P
                    last = nc.tensor.matmul(ps_s[:, g * P:g * P + (P if c else WIDE)], q_diag[:, o:o + P], keys,
                                            start=True, stop=True)
                last.then_inc(s_full, 1)

            def to_keys(u):
                pe.wait_ge(p_spread, it * UNITS + (u + 1))
                if u:
                    pe.wait_ge(e_done, it * UNITS + u)
                n = WIDE if u < 4 else P
                for g in range(GROUPS):
                    last = nc.tensor.transpose(ps_e[0:n, g * P:g * P + P], p_wide[:, g * n:g * n + n], ident[:, :])
                last.then_inc(e_full, 1)

            def values(u):
                c, pp, b = u // 4, u // 2 % 2, u % 2
                if u == 0:
                    pe.wait_ge(loc_loaded, it * 256 + 256)
                elif u % 4 == 0:
                    pe.wait_ge(own_loaded, it * 768 + 256 * c)
                    pe.wait_ge(mixed_loaded, it * 768 + 256 * c)
                pe.wait_ge(e_done, it * UNITS + (u + 1))
                if u:
                    pe.wait_ge(o_done, it * UNITS + u)
                n = P if c else WIN
                for g in range(GROUPS):
                    for j in range(2):
                        o = (b * GROUPS + g) * 256 + (2 * pp + j) * 64
                        q = g * P + j * 64
                        last = nc.tensor.matmul(ps_o[64 * j:64 * j + 64, g * 64:g * 64 + 64], vals[c % 2][0:n, o:o + 64],
                                                p_t[u % 2][0:n, q:q + 64], start=True, stop=True)
                last.then_inc(o_full, 1)

            for step in steps:
                kind = step[0]
                if kind == "scores":
                    scores(step[1])
                elif kind == "to keys":
                    to_keys(step[1])
                elif kind == "values":
                    values(step[1])
                elif kind == "feats":
                    g = step[1]
                    if g == 0:
                        pe.wait_ge(xsum_ready, it + 2)
                    w = free_bank(step)
                    for h in range(4):
                        for part in range(2):
                            o = part * 1024 + (LOCAL_HEADS + 4 * g + h) * 64
                            last = nc.tensor.matmul(w[64 * part:64 * part + 64, h * P:h * P + P],
                                                    w_qkv[:, o:o + 64], xsum_cur[:, :], start=True, stop=True)
                    last.then_inc(work_full, 1)
                elif kind == "logits":
                    g = step[1]
                    if steps is FIRST:
                        pe.wait_ge(sort_loaded, 16)
                    w = free_bank(step)
                    emptied(pe, banks, ("feats", 2))
                    for h in range((8, 4)[g]):
                        hh = 8 * g + h
                        last = nc.tensor.matmul(w[:, h * 64:h * 64 + 64], feats_t[:, hh * P:hh * P + P],
                                                sort_w[:, hh * 64:hh * 64 + 64], start=True, stop=True)
                    last.then_inc(work_full, 1)
                elif kind == "v":
                    c, n = step[1:]
                    if c == 0 and n == 0 and steps is TURN:
                        pe.wait_ge(cur_ready, it + 1)
                    w = free_bank(step)
                    for h in range(2):
                        last = nc.tensor.matmul(w[:, h * 256:h * 256 + 256], view(xn_cur, 0, P, 2 * n + h, [[W, P]]),
                                                w_qkv[:, 2048 + c * 256:2048 + c * 256 + 256], start=True, stop=True)
                    last.then_inc(work_full, 1)
                elif kind in ("q", "k"):
                    c, n = step[1:]
                    pp, b = divmod(n, 2)
                    o = (1024 if kind == "k" else 0) + (2 * c + pp) * P
                    nc.tensor.matmul(free_bank(step), w_qkv[:, o:o + P], xn_cur[:, b * SEQ:(b + 1) * SEQ],
                                     start=True, stop=True).then_inc(work_full, 1)
                elif kind == "rt":
                    c = step[1]
                    if c == 1:
                        pe.wait_ge(r_ready, it * 2 + 2)
                    w = free_bank(step)
                    for h in range(4):
                        hh = 4 * (c - 1) + h
                        last = nc.tensor.transpose(w[:, h * P:h * P + P], r_blk[:, hh * P:hh * P + P], ident[:, :])
                    last.then_inc(work_full, 1)
                elif kind == "kn":
                    c, n = step[1:]
                    if n == 0:
                        emptied(pe, banks, ("k", c, 3))
                    w = free_bank(step)
                    for t in range(2):
                        for pp in range(2):
                            last = nc.tensor.transpose(w[:, t * 256 + pp * P:t * 256 + pp * P + P],
                                                       view(k_t, 0, P, pp * TOK + 2 * n + t, [[W, P]]), ident[:, :])
                    last.then_inc(work_full, 1)
                elif kind == "vr":
                    c, h = step[1:]
                    if h == 0:
                        emptied(pe, banks, ("rt", c))
                    nc.tensor.matmul(free_bank(step), r_t[:, h * P:h * P + P], view(v_nat, 0, P, h * 64, [[256, W], [1, 64]]),
                                     start=True, stop=True).then_inc(work_full, 1)
                elif kind == "kr":
                    c, n = step[1:]
                    pp, half = divmod(n, 2)
                    if n == 0:
                        emptied(pe, banks, ("kn", c, 3))
                    w = free_bank(step)
                    for t in range(4):
                        for j in range(2):
                            h = 2 * pp + j
                            o = (4 * half + t) * 256 + h * 64
                            last = nc.tensor.matmul(w[64 * j:64 * j + 64, t * P:t * P + P], k_nat[:, o:o + 64],
                                                    r_t[:, h * P:h * P + P], start=True, stop=True)
                    last.then_inc(work_full, 1)
                elif kind == "out":
                    c, n = step[1:]
                    if n == 0:
                        pe.wait_ge(o_done, it * UNITS + (4 * c + 4))
                    w = free_bank(step)
                    for t in range(4):
                        for pp in range(2):
                            o = pp * TOK + (4 * n + t) * P
                            last = nc.tensor.matmul(w[:, t * P:t * P + P], att_t[:, o:o + P],
                                                    w_out[:, (2 * c + pp) * D:(2 * c + pp) * D + D],
                                                    start=(pp == 0), stop=(pp == 1))
                    last.then_inc(work_full, 1)

        pe.wait_ge(ident_ready, 1)
        for n in range(2):
            transposed(n)
        pe.wait_ge(w_qkv_loaded, 32)
        pe.wait_ge(xt_done, 2)
        turn(-1, FIRST, first_banks())
        totals = first_banks().total()
        pe.wait_ge(work_act, totals["act"])
        for n in range(2, TILES // 4):
            transposed(n)
        pe.wait_ge(xt_done, TILES // 4)
        pe.wait_ge(out_loaded, 32)
        with pe.Fori(0, TURNS - 1) as it:
            turn(it, TURN, turn_banks(it))
        turn(TURNS - 1, LAST, last_banks())


def feed_forward_block(nc, ctx, x_sb, A, out):
    def sb(name, cols, dt=F32):
        return ctx.enter_context(nc.sbuf_tensor(name, [P, cols], dt))

    def psum(name, cols):
        return ctx.enter_context(nc.psum_tensor(name, [P, cols], F32))

    def sem(name):
        return ctx.enter_context(nc.semaphore(name))

    E = EXPERTS
    CH = INTER // P
    ROW = D + 4
    SLOTS = E * CAP
    TOKENS = TILES * P
    GRP = TOKENS // 512
    VEC = E * CH + CH + 2

    y = sb("y", TOKENS)
    rows = sb("rows", TILES * ROW)
    a_t = sb("a_t", TOKENS)
    blank = sb("blank", SLOTS // P * ROW)
    w_gate = sb("w_gate", E + 2)
    res_w1 = sb("res_w1", INTER)
    res_w2 = sb("res_w2", CH * D)
    w1 = [sb(f"w1_{i}", INTER) for i in range(2)]
    w2 = [sb(f"w2_{i}", CH * D) for i in range(2)]
    b2 = sb("b2", E * D)
    res_b2 = sb("res_b2", D)
    vecs = sb("vecs", D)
    cols = sb("cols", VEC)
    ident = sb("ident_b", P)
    before = sb("before", P, BF16)
    ones = sb("ones", P, BF16)
    rank = sb("rank", E)
    first_slot = sb("first_slot", E)
    spare = sb("spare", TILES)
    bn = sb("bn_b", 6 * TILES)
    ln_small = sb("ln_small_b", 5 * TILES)
    gates = sb("gates", TILES * (E + 2))
    work1 = sb("work1", TILES * E)
    work2 = sb("work2", TILES * E)
    chosen = sb("chosen", TILES * E)
    chosen_bf = sb("chosen_bf", TILES * E, BF16)
    s = {n: sb(n, TILES) for n in ("gmax", "cmax", "gsum", "csum", "top", "first", "slot", "kept", "lost", "share")}
    slot_i = sb("slot_i", TILES, I32)
    counts_i = sb("counts_i", 2 * E, I32)
    h_t = [sb(f"h_t{i}", CH * 512) for i in range(2)]
    res = [sb(f"res{i}", 512) for i in range(2)]
    xe = [sb(f"xe{i}", CAP // P * ROW) for i in range(2)]
    xe_t = [sb(f"xe_t{i}", CAP) for i in range(2)]
    eo = [sb(f"eo{i}", 512) for i in range(2)]

    disp = nc.dram_tensor("disp", (SLOTS + TOKENS, ROW), F32, kind="Internal").ap()
    moe = nc.dram_tensor("moe", (TOKENS + SLOTS, D), F32, kind="Internal").ap()

    ps_t = psum("ps_t", 1024)
    ps_h = psum("ps_h", 1024)
    ps_o = psum("ps_o_b", 1024)
    ps_g = psum("ps_g", 512)
    ps_l = psum("ps_l", 512)

    weights_in = sem("weights_in")
    gate_in = sem("gate_in")
    blank_ready = sem("blank_ready")
    disp_blank = sem("disp_blank")
    moe_blank = sem("moe_blank")
    consts_ready = sem("consts_ready_b")
    pool_chain = sem("pool_chain_b")
    dve_chain = sem("dve_chain_b")
    var_ready = sem("var_ready_b")
    root_ready = sem("root_ready_b")
    y_ready = sem("y_ready")
    base_ready = sem("base_ready")
    rows_ready = sem("rows_ready")
    vecs_full = sem("vecs_full")
    vecs_done = sem("vecs_done")
    t_full = sem("t_full")
    t_done = sem("t_done")
    g_full = sem("g_full")
    shift_ready = sem("shift_ready")
    exp_ready = sem("exp_ready")
    chosen_ready = sem("chosen_ready")
    l_full = sem("l_full")
    slots_ready = sem("slots_ready")
    scattered = sem("scattered")
    h_full = sem("h_full")
    h_done = sem("h_done")
    o_full = sem("o_full_b")
    o_done = sem("o_done_b")
    res_link = sem("res_link")
    xe_loaded = [sem(f"xe_loaded{i}") for i in range(2)]
    we_loaded = [sem(f"we_loaded{i}") for i in range(2)]
    xt_full = sem("xt_full_b")
    xt_done = sem("xt_done_b")
    sent = [sem(f"sent{i}") for i in range(2)]
    moe_in = [sem(f"moe_in{i}") for i in range(4)]
    res_added = sem("res_added")
    BANKS = 2
    fin = sem("fin")
    stored = sem("stored")

    xg = x_sb[:, :].rearrange("p (t d) -> p t d", d=D)
    yg = y[:, :].rearrange("p (t d) -> p t d", d=D)
    rg = rows[:, :].rearrange("p (t r) -> p t r", r=ROW)
    gt = gates[:, :].rearrange("p (t e) -> p t e", e=E + 2)
    c_b1, c_rb1, c_nw, c_nb = 0, E * CH, E * CH + CH, E * CH + CH + 1
    GELU = ACT.Gelu_apprx_tanh

    def spread(name, n, off=0):
        return view(s[name], 0, P, off, [[1, TILES], [0, n]])

    block = ctx.enter_context(nc.Block())

    @block.sync
    def _(sp):
        sp.dma_start(vecs[0:c_rb1, :], A["inter_b"].rearrange("e (c p) -> (e c) p", p=P)).then_inc(weights_in, 16)
        sp.dma_start(vecs[c_rb1:c_nw, :], A["res_inter_b"].rearrange("(c p) -> c p", p=P)).then_inc(weights_in, 16)
        sp.dma_start(vecs[c_nw:c_nw + 1, :], A["attn_nw"].rearrange("(a p) -> a p", a=1)).then_inc(weights_in, 16)
        sp.dma_start(vecs[c_nb:c_nb + 1, :], A["attn_nb"].rearrange("(a p) -> a p", a=1)).then_inc(weights_in, 16)
        sp.dma_start(w_gate[:, 0:E], A["wg"]).then_inc(gate_in, 16)
        sp.dma_start(w_gate[:, E:E + 2], A["res_coef"]).then_inc(gate_in, 16)
        sp.dma_start(res_w1[:, :], A["res_inter_w"]).then_inc(gate_in, 16)
        sp.dma_start(res_w2[:, :].rearrange("p (c d) -> p c d", d=D),
                     A["res_output_w"].rearrange("(c p) d -> p c d", p=P)).then_inc(gate_in, 16)
        sp.dma_start(res_b2[:, :], A["res_output_b"].rearrange("(a d) -> a d", a=1).to_broadcast([P, D])).then_inc(gate_in, 16)
        sp.dma_start(b2[:, :], A["output_b"].rearrange("(a e) d -> a (e d)", a=1).to_broadcast([P, E * D])).then_inc(gate_in, 16)
        sp.wait_ge(blank_ready, 2)
        sp.dma_start(disp[0:SLOTS, :].rearrange("(e p j) r -> p e (j r)", e=E, p=P),
                     blank[:, :].rearrange("p (e r) -> p e r", e=E)).then_inc(disp_blank, 16)
        sp.dma_start(moe[0:TOKENS, :].rearrange("(t p) d -> p t d", p=P),
                     view(blank, 0, P, 0, [[ROW, TILES], [1, D]])).then_inc(moe_blank, 16)

        def load_weights(e, i):
            sp.dma_start(w1[i][:, :], A["inter_w"][bass.ds(e, 1), :, :].rearrange("a p n -> (a p) n")).then_inc(we_loaded[i], 16)
            sp.dma_start(w2[i][:, :].rearrange("p (c d) -> p c d", d=D),
                         A["output_w"][bass.ds(e, 1), :, :].rearrange("a (c p) d -> p (a c) d", p=P)).then_inc(we_loaded[i], 16)

        def load_rows(e, i):
            sp.dma_start(xe[i][:, :], disp[bass.ds(e * CAP, CAP), :].rearrange("(p j) r -> p (j r)", p=P)).then_inc(xe_loaded[i], 16)

        for i in range(2):
            load_weights(i, i)
        sp.wait_ge(scattered, 16 * TILES)
        for i in range(2):
            load_rows(i, i)
        with sp.Fori(0, E // 2 - 1) as turn:
            for i in range(2):
                sp.wait_ge(o_full, turn * 2 + (GRP + 1 + i))
                load_weights(turn * 2 + (2 + i), i)
                sp.wait_ge(sent[i], turn * 64 + 64)
                load_rows(turn * 2 + (2 + i), i)
        for i in range(2):
            sp.wait_ge(sent[i], 64 * (E // 2))
        for i in range(4):
            t = TILES // 4
            sp.dma_start(yg[:, t * i:t * i + t, :],
                         moe[t * P * i:t * P * (i + 1), :].rearrange("(t p) d -> p t d", p=P)).then_inc(moe_in[i], 16)
        for i in range(4):
            t = TILES // 4
            sp.wait_ge(fin, i + 1)
            sp.dma_start(out.rearrange("b (t p) d -> p (b t) d", p=P)[:, t * i:t * i + t, :],
                         xg[:, t * i:t * i + t, :]).then_inc(stored, 16)
        sp.wait_ge(stored, 64)

    @block.gpsimd
    def _(pool):
        done = [0]

        def link(ins):
            done[0] += 1
            ins.then_inc(pool_chain, 1)
            pool.wait_ge(pool_chain, done[0])

        nc.gpsimd.memset(blank[:, :], 0.0)
        nc.gpsimd.memset(rows[:, :], 0.0)
        nc.gpsimd.memset(before[:, :], 1.0)
        nc.gpsimd.memset(ones[:, :], 1.0)
        link(nc.gpsimd.memset(ident[:, :], 0.0))
        nc.gpsimd.iota(view(blank, 0, P, D, [[ROW * 4, E], [ROW, 4]]).bitcast(I32),
                       pattern=[[CAP, E], [1, 4]], base=TOKENS, channel_multiplier=4).then_inc(blank_ready, 1)
        nc.gpsimd.iota(view(rows, 0, P, D, [[ROW, TILES]]).bitcast(I32), pattern=[[P, TILES]], base=0,
                       channel_multiplier=1).then_inc(blank_ready, 1)
        nc.gpsimd.affine_select(out=ident[:, :], in_=ident[:, :], compare_op=ALU.not_equal, fill=1.0, base=0,
                                pattern=[[-1, P]], channel_multiplier=1)
        nc.gpsimd.affine_select(out=before[:, :], in_=before[:, :], compare_op=ALU.is_gt, fill=0.0, base=0,
                                pattern=[[1, P]], channel_multiplier=-1)
        nc.gpsimd.iota(slot_i[:, :], pattern=[[P, TILES]], base=SLOTS, channel_multiplier=1)
        nc.gpsimd.iota(counts_i[:, 0:E], pattern=[[-1, E]], base=E, channel_multiplier=0)
        link(nc.gpsimd.iota(counts_i[:, E:2 * E], pattern=[[CAP, E]], base=0, channel_multiplier=0))
        nc.gpsimd.tensor_copy(spare[:, :], slot_i[:, :])
        nc.gpsimd.tensor_copy(rank[:, :], counts_i[:, 0:E])
        nc.gpsimd.tensor_copy(first_slot[:, :], counts_i[:, E:2 * E]).then_inc(consts_ready, 1)
        for i in range(4):
            t = TILES // 4
            pool.wait_ge(y_ready, 1)
            nc.gpsimd.tensor_tensor(xg[:, t * i:t * i + t, :], xg[:, t * i:t * i + t, :], yg[:, t * i:t * i + t, :],
                                    ALU.add).then_inc(base_ready, 1)
        pool.wait_ge(slots_ready, 1)
        pool.wait_ge(disp_blank, 16)
        pool.wait_ge(rows_ready, TILES)
        for t in range(TILES):
            nc.gpsimd.indirect_dma_start(out=disp[:, :], out_offset=bass.IndirectOffsetOnAxis(ap=slot_i[:, t:t + 1], axis=0),
                                         in_=rows[:, t * ROW:t * ROW + ROW], in_offset=None).then_inc(scattered, 16)
        pool.wait_ge(moe_blank, 16)
        for e in range(E):
            i = e % 2
            pool.wait_ge(o_done, BANKS + GRP + 1 + e)
            for j in range(4):
                nc.gpsimd.indirect_dma_start(
                    out=moe[:, :],
                    out_offset=bass.IndirectOffsetOnAxis(ap=view(xe[i], 0, P, j * ROW + D, [[1, 1]]).bitcast(I32), axis=0),
                    in_=eo[i][:, j * D:j * D + D], in_offset=None).then_inc(sent[i], 16)

    def gelu_steps(act, base, i, bias):
        for c in range(CH):
            act.wait_ge(h_full, base + (c + 1))
            nc.scalar.activation(h_t[i][:, c * 512:c * 512 + 512], ps_h[:, (c % 2) * 512:(c % 2) * 512 + 512], GELU,
                                 bias=bias(c)).then_inc(h_done, 1)

    @block.scalar
    def _(act):
        act.sem_inc(h_done, BANKS)
        for n in range(2):
            act.wait_ge(var_ready, n + 1)
            nc.scalar.activation(ln_small[:, 2 * TILES:3 * TILES], ln_small[:, 4 * TILES:5 * TILES],
                                 ACT.Sqrt).then_inc(root_ready, 1)
        act.wait_ge(vecs_full, 1)
        nc.scalar.copy(cols[:, :], ps_l[:, 0:VEC]).then_inc(vecs_done, 1)
        act.wait_ge(vecs_done, 1)
        for n in range(GRP):
            act.wait_ge(t_full, n + 1)
            nc.scalar.activation(a_t[:, n * 512:n * 512 + 512], ps_t[:, (n % 2) * 512:(n % 2) * 512 + 512], ACT.Identity,
                                 scale=cols[:, c_nw:c_nw + 1], bias=cols[:, c_nb:c_nb + 1]).then_inc(t_done, 1)
        act.wait_ge(shift_ready, 1)
        nc.scalar.activation(gates[:, :], gates[:, :], ACT.Exp).then_inc(exp_ready, 1)
        with act.Fori(0, GRP // 2) as turn:
            for i in range(2):
                gelu_steps(act, turn * (2 * CH) + CH * i, i, lambda c: cols[:, c_rb1 + c:c_rb1 + c + 1])
        with act.Fori(0, E // 2) as turn:
            for i in range(2):
                act.wait_ge(xt_full, turn * 2 + (i + 1))
                nc.scalar.activation(xe_t[i][:, :], ps_t[:, i * 512:i * 512 + 512], ACT.Identity,
                                     scale=cols[:, c_nw:c_nw + 1], bias=cols[:, c_nb:c_nb + 1]).then_inc(xt_done, 1)
                gelu_steps(act, turn * (2 * CH) + (GRP * CH + CH * i), i,
                           lambda c: cols[:, bass.ds(turn * (2 * CH) + (i * CH + c), 1)])

    @block.vector
    def _(dve):
        done = [0]

        def link(ins):
            done[0] += 1
            ins.then_inc(dve_chain, 1)
            dve.wait_ge(dve_chain, done[0])

        dve.sem_inc(o_done, BANKS)
        layer_norm_steps(nc, link, lambda t: xg[:, t, :], bn, ln_small, TILES, 1e-5, var_ready,
                         lambda: dve.wait_ge(root_ready, 1))
        for t in range(TILES):
            ins = nc.vector.tensor_scalar(yg[:, t, :], xg[:, t, :], ln_small[:, t:t + 1],
                                          ln_small[:, TILES + t:TILES + t + 1], ALU.subtract, ALU.mult)
        ins.then_inc(y_ready, 1)
        dve.wait_ge(y_ready, 1)
        layer_norm_steps(nc, link, lambda t: yg[:, t, :], bn, ln_small, TILES, 1e-12, var_ready,
                         lambda: dve.wait_ge(root_ready, 2))
        dve.wait_ge(blank_ready, 2)
        for t in range(TILES):
            nc.vector.tensor_scalar(rg[:, t, 0:D], yg[:, t, :], ln_small[:, t:t + 1],
                                    ln_small[:, TILES + t:TILES + t + 1], ALU.subtract, ALU.mult).then_inc(rows_ready, 1)
        dve.wait_ge(consts_ready, 1)
        dve.wait_ge(g_full, 1)
        lg = ps_g[:, 0:TILES * (E + 2)].rearrange("p (t e) -> p t e", e=E + 2)
        nc.vector.tensor_reduce(s["gmax"][:, :], lg[:, :, 0:E], AX_X, ALU.max)
        link(nc.vector.tensor_reduce(s["cmax"][:, :], lg[:, :, E:E + 2], AX_X, ALU.max))
        nc.vector.tensor_tensor(gt[:, :, 0:E], lg[:, :, 0:E], spread("gmax", E), ALU.subtract)
        nc.vector.tensor_tensor(gt[:, :, E:E + 2], lg[:, :, E:E + 2], spread("cmax", 2), ALU.subtract).then_inc(shift_ready, 1)
        dve.wait_ge(exp_ready, 1)
        nc.vector.tensor_reduce(s["gsum"][:, :], gt[:, :, 0:E], AX_X, ALU.add)
        link(nc.vector.tensor_reduce(s["csum"][:, :], gt[:, :, E:E + 2], AX_X, ALU.add))
        nc.vector.reciprocal(s["gmax"][:, :], s["gsum"][:, :])
        link(nc.vector.reciprocal(s["cmax"][:, :], s["csum"][:, :]))
        nc.vector.tensor_tensor(gt[:, :, 0:E], gt[:, :, 0:E], spread("gmax", E), ALU.mult)
        link(nc.vector.tensor_tensor(gt[:, :, E:E + 2], gt[:, :, E:E + 2], spread("cmax", 2), ALU.mult))
        w1v = work1[:, :].rearrange("p (t e) -> p t e", e=E)
        w2v = work2[:, :].rearrange("p (t e) -> p t e", e=E)
        chv = chosen[:, :].rearrange("p (t e) -> p t e", e=E)
        link(nc.vector.tensor_reduce(s["top"][:, :], gt[:, :, 0:E], AX_X, ALU.max))
        link(nc.vector.tensor_tensor(w1v, gt[:, :, 0:E], spread("top", E), ALU.is_equal))
        link(nc.vector.tensor_tensor(w1v, w1v, view(rank, 0, P, 0, [[0, TILES], [1, E]]), ALU.mult))
        link(nc.vector.tensor_reduce(s["first"][:, :], w1v, AX_X, ALU.max))
        link(nc.vector.tensor_tensor(chv, w1v, spread("first", E), ALU.is_equal))
        nc.vector.tensor_copy(chosen_bf[:, :], chosen[:, :]).then_inc(chosen_ready, 1)
        dve.wait_ge(l_full, 1)
        loc = ps_l[:, 64:64 + TILES * E]
        locv = loc.rearrange("p (t e) -> p t e", e=E)
        nc.vector.scalar_tensor_tensor(work1[:, :], loc, float(CAP), chosen[:, :], ALU.is_lt, ALU.mult)
        link(nc.vector.tensor_tensor(w2v, locv, view(first_slot, 0, P, 0, [[0, TILES], [1, E]]), ALU.add))
        nc.vector.tensor_reduce(s["kept"][:, :], w1v, AX_X, ALU.add)
        link(nc.vector.tensor_tensor(work2[:, :], work2[:, :], work1[:, :], ALU.mult))
        nc.vector.tensor_reduce(s["slot"][:, :], w2v, AX_X, ALU.add)
        link(nc.vector.tensor_tensor(s["lost"][:, :], s["kept"][:, :], spare[:, :], ALU.mult))
        link(nc.vector.tensor_tensor(s["lost"][:, :], spare[:, :], s["lost"][:, :], ALU.subtract))
        nc.vector.tensor_tensor(slot_i[:, :], s["slot"][:, :], s["lost"][:, :], ALU.add).then_inc(slots_ready, 1)
        link(nc.vector.tensor_tensor(s["share"][:, :], s["top"][:, :], s["kept"][:, :], ALU.mult))
        link(nc.vector.tensor_tensor(s["share"][:, :], s["share"][:, :], gt[:, :, E + 1], ALU.mult))
        link(nc.vector.tensor_copy(s["csum"][:, :], gt[:, :, E]))
        dve.wait_ge(base_ready, 4)
        dve.wait_ge(gate_in, 96)
        with dve.Fori(0, GRP // 2) as turn:
            for i in range(2):
                rv = res[i][:, :].rearrange("p (t d) -> p t d", d=D)
                dve.wait_ge(o_full, turn * 2 + (i + 1))
                nc.vector.tensor_tensor(rv, ps_o[:, i * 512:i * 512 + 512].rearrange("p (t d) -> p t d", d=D),
                                        view(res_b2, 0, P, 0, [[0, 4], [1, D]]), ALU.add).then_inc(o_done, 1)
                dve.wait_ge(o_done, turn * 2 + (BANKS + i + 1))
                c0 = s["csum"][:, bass.ds(turn * 8 + 4 * i, 4)].unsqueeze(2).to_broadcast([P, 4, D])
                nc.vector.tensor_tensor(rv, rv, c0, ALU.mult).then_inc(res_link, 1)
                dve.wait_ge(res_link, turn * 2 + (i + 1))
                xs = x_sb[:, bass.ds(turn * 1024 + 512 * i, 512)]
                nc.vector.tensor_tensor(xs, xs, res[i][:, :], ALU.add).then_inc(res_added, 1)
        with dve.Fori(0, E // 2) as turn:
            for i in range(2):
                dve.wait_ge(o_full, turn * 2 + (GRP + 1 + i))
                be = b2[:, bass.ds(turn * (2 * D) + i * D, D)].unsqueeze(1).to_broadcast([P, 4, D])
                nc.vector.tensor_tensor(eo[i][:, :].rearrange("p (t d) -> p t d", d=D),
                                        ps_o[:, i * 512:i * 512 + 512].rearrange("p (t d) -> p t d", d=D),
                                        be, ALU.add).then_inc(o_done, 1)
        dve.wait_ge(res_added, GRP)
        for i in range(4):
            dve.wait_ge(moe_in[i], 16)
            for t in range(TILES // 4 * i, TILES // 4 * (i + 1)):
                ins = nc.vector.scalar_tensor_tensor(xg[:, t, :], yg[:, t, :], s["share"][:, t:t + 1], xg[:, t, :],
                                                     ALU.mult, ALU.add)
            ins.then_inc(fin, 1)

    @block.tensor
    def _(pe):
        pe.wait_ge(consts_ready, 1)
        pe.wait_ge(weights_in, 64)
        nc.tensor.transpose(ps_l[:, 0:VEC], vecs[0:VEC, :], ident[0:VEC, 0:VEC]).then_inc(vecs_full, 1)
        pe.wait_ge(gate_in, 96)
        for n in range(GRP):
            pe.wait_ge(rows_ready, 4 * n + 4)
            if n >= 2:
                pe.wait_ge(t_done, n - 1)
            for t in range(4):
                T = 4 * n + t
                last = nc.tensor.transpose(ps_t[:, (n % 2) * 512 + t * P:(n % 2) * 512 + t * P + P], rg[:, T, 0:D],
                                           ident[:, :])
            last.then_inc(t_full, 1)
        for n in range(GRP):
            pe.wait_ge(t_done, n + 1)
            for T in range(4 * n, 4 * n + 4):
                last = nc.tensor.matmul(ps_g[:, T * (E + 2):(T + 1) * (E + 2)], a_t[:, T * P:T * P + P], w_gate[:, :],
                                        start=True, stop=True)
        last.then_inc(g_full, 1)
        pe.wait_ge(chosen_ready, 1)
        nc.tensor.matmul(ps_l[:, 64:64 + TILES * E], before[:, :], chosen_bf[:, :], start=True, stop=False)
        for k in range(1, TILES):
            last = nc.tensor.matmul(ps_l[:, 64 + k * E:64 + TILES * E], ones[:, :], chosen_bf[:, 0:(TILES - k) * E],
                                    start=False, stop=(k == TILES - 1))
        last.then_inc(l_full, 1)

        def inner(base, wa, moving):
            for c in range(CH):
                pe.wait_ge(h_done, base + (c + 1))
                nc.tensor.matmul(ps_h[:, (c % 2) * 512:(c % 2) * 512 + 512], wa[:, c * P:c * P + P], moving,
                                 start=True, stop=True).then_inc(h_full, 1)

        def outer(base, passes, i, wb):
            pe.wait_ge(h_done, base + (BANKS + CH))
            pe.wait_ge(o_done, passes + 1)
            for j in range(4):
                for c in range(CH):
                    last = nc.tensor.matmul(ps_o[:, i * 512 + j * D:i * 512 + j * D + D],
                                            h_t[i][:, c * 512 + j * P:c * 512 + j * P + P],
                                            wb[:, c * D:c * D + D], start=(c == 0), stop=(c == CH - 1))
            last.then_inc(o_full, 1)

        with pe.Fori(0, GRP // 2) as turn:
            for i in range(2):
                base = turn * (2 * CH) + CH * i
                inner(base, res_w1, a_t[:, bass.ds(turn * 1024 + 512 * i, 512)])
                outer(base, turn * 2 + i, i, res_w2)
        with pe.Fori(0, E // 2) as turn:
            for i in range(2):
                base = turn * (2 * CH) + (GRP * CH + CH * i)
                pe.wait_ge(xe_loaded[i], turn * 16 + 16)
                for j in range(4):
                    last = nc.tensor.transpose(ps_t[:, i * 512 + j * P:i * 512 + j * P + P],
                                               xe[i][:, j * ROW:j * ROW + D], ident[:, :])
                last.then_inc(xt_full, 1)
                pe.wait_ge(we_loaded[i], turn * 32 + 32)
                pe.wait_ge(xt_done, turn * 2 + (i + 1))
                inner(base, w1[i], xe_t[i][:, :])
                outer(base, turn * 2 + (GRP + i), i, w2[i])


_INS = ['x', 'w_q', 'w_kv', 'w_out', 'b_out', 'sort_w']
_FFN = ['attn_nw', 'attn_nb', 'wg', 'inter_w', 'inter_b', 'output_w', 'output_b', 'res_inter_w', 'res_inter_b',
        'res_output_w', 'res_output_b', 'res_coef']


def program(nc, A, out):
    with ExitStack() as outer:
        x_sb = outer.enter_context(nc.sbuf_tensor("x_sb", [P, TILES * D], F32))
        with ExitStack() as ctx:
            attention_block(nc, ctx, x_sb, A)
        with ExitStack() as ctx:
            feed_forward_block(nc, ctx, x_sb, A, out)


def kernel(**inputs):
    import numpy as _np
    import concourse.bacc as _bacc
    from concourse import mybir as _mybir
    from concourse.bass_utils import run_bass_kernel_spmd as _run

    nc = _bacc.Bacc("TRN2", target_bir_lowering=False, num_devices=1)
    arrays, args = {}, {}
    for prefix, names in (("L0_attn_", _INS), ("L0_ffn_", _FFN)):
        for name in names:
            a = _np.ascontiguousarray(inputs[prefix + name])
            arrays[f"in_{name}_dram"] = a
            args[name] = nc.dram_tensor(f"in_{name}_dram", a.shape, _mybir.dt.from_np(a.dtype), kind="ExternalInput").ap()
    out = nc.dram_tensor("out_0_dram", (8, SEQ, D), _mybir.dt.float32, kind="ExternalOutput").ap()
    program(nc, args, out)
    r = _run(nc, [arrays], core_ids=[0])
    return r.results[0]["out_0_dram"]
```

```python
from contextlib import ExitStack

import concourse.bass as bass
from concourse import mybir

F32 = mybir.dt.float32
BF16 = mybir.dt.bfloat16
I32 = mybir.dt.int32
ALU = mybir.AluOpType
ACT = mybir.ActivationFunctionType
AX_X = mybir.AxisListType.X

P = 128
TILES = 32
D = 128
DH = 64
HEADS = 16
LOCAL_HEADS = 4
SORT_HEADS = HEADS - LOCAL_HEADS
BUCKETS = 64
W = 8
SEQ = BUCKETS * W
TURNS = 4
TOK = 2 * SEQ
CHUNKS = 4
UNITS = 16
GROUPS = 8
WIN = 10 * W
WIDE = 12 * W
POOL_GROUPS = 3
HALF = 32
HALF_WIDE = 9 * W
PAD = W + SEQ + 3 * W
EXPERTS = 8
CAP = 512
INTER = 512
ROW_RB1 = EXPERTS * INTER // P
ROW_NW = ROW_RB1 + INTER // P
ROW_NB = ROW_NW + 1
VEC = ROW_NB + 1
OUT_OF_SEQUENCE = -1.0e30
PART = TILES // TURNS
ROW = D + 4
BLOCK = PART * ROW


def view(t, part, nparts, offset, dims):
    row = t.shape[1]
    return bass.AP(tensor=t, offset=part * row + offset, ap=[[row, nparts]] + dims)


def layer_norm_stats(nc, link, x, stats, small, n, eps, var_ready):
    for t in range(n):
        last = nc.vector.bn_stats(stats[:, 6 * t:6 * t + 6], x(t))
    link(last)
    st = stats[:, 0:6 * n].rearrange("p (t s) -> p s t", s=6)
    mean, _, a, b, v = (small[:, i * PART:i * PART + n] for i in range(5))
    nc.vector.tensor_tensor(a, st[:, 1, :], st[:, 4, :], ALU.add)
    nc.vector.tensor_tensor(b, st[:, 1, :], st[:, 4, :], ALU.subtract)
    link(nc.vector.tensor_tensor(v, st[:, 2, :], st[:, 5, :], ALU.add))
    nc.vector.tensor_scalar(mean, a, 0.5, None, ALU.mult)
    nc.vector.tensor_scalar(v, v, 1.0 / D, eps, ALU.mult, ALU.add)
    link(nc.vector.tensor_tensor(b, b, b, ALU.mult))
    nc.vector.scalar_tensor_tensor(v, b, 0.25, v, ALU.mult, ALU.add).then_inc(var_ready, 1)


def layer_norm_scale(nc, link, small, n):
    _, rstd, a, b, v = (small[:, i * PART:i * PART + n] for i in range(5))
    link(nc.vector.reciprocal(rstd, a))
    link(nc.vector.tensor_tensor(b, rstd, rstd, ALU.mult))
    link(nc.vector.tensor_tensor(b, b, v, ALU.mult))
    link(nc.vector.tensor_scalar(b, b, -0.5, 1.5, ALU.mult, ALU.add))
    link(nc.vector.tensor_tensor(rstd, rstd, b, ALU.mult))


def layer_norm_rows(nc, small, out, x, n):
    for t in range(n):
        last = nc.vector.tensor_scalar(out(t), x(t), small[:, t:t + 1], small[:, PART + t:PART + t + 1],
                                       ALU.subtract, ALU.mult)
    return last


EMPTIED_BY = {"feats": "act", "v": "act", "k": "act", "rt": "act", "q": "act", "kn": "act", "vr": "act",
              "logits": "dve", "kr": "dve", "out": "dve"}


NORM_AFTER = {("softmax", 1): ("ffn norm", "x1"), ("values", 1): ("ffn root", 0), ("softmax", 4): ("ffn norm", "scale y"),
              ("values", 4): ("ffn norm", "y"), ("softmax", 5): ("ffn base", 0), ("softmax", 6): ("ffn base", 1),
              ("values", 5): ("ffn norm", "of y"), ("values", 6): ("ffn root", 1), ("softmax", 8): ("ffn norm", "scale rows"),
              ("softmax", 9): ("ffn norm", "rows")}


def plan(chunks, following):
    def four(name, c):
        return [(name, c, n) for n in range(4)]

    steps = []
    for c in chunks:
        if c == CHUNKS - 1 and not following:
            out, u = ("out", c - 1), 4 * c
            steps += [("scores", u), out + (0,), ("softmax", u), ("scores", u + 1), out + (1,), ("to keys", u),
                      ("softmax", u + 1), ("scores", u + 2), ("values", u), ("to keys", u + 1),
                      ("softmax", u + 2), ("scores", u + 3), ("values", u + 1), ("to keys", u + 2),
                      ("softmax", u + 3), ("values", u + 2), ("to keys", u + 3), ("values", u + 3)]
            continue
        nxt = c + 1 if c + 1 < CHUNKS else 0
        if nxt:
            kn, vr = four("kn", nxt), four("vr", nxt)
            early = [four("v", nxt), four("k", nxt) + [("rt", nxt)], kn[:2] + vr[:2], kn[2:] + vr[2:]]
        else:
            early = [four("v", 0), [("feats", g) for g in range(3)] + [("logits", 0), ("logits", 1)], four("k", 0)[:2],
                     four("k", 0)[2:]]
        for k in range(4):
            u, jobs = 4 * c + k, early[k]
            steps.append(("scores", u))
            if k:
                h = len(jobs) // 2
                steps += jobs[:h] + [("to keys", u - 1)] + jobs[h:h + 1] + [("softmax", u)] + jobs[h + 1:]
                steps.append(("values", u - 1))
            elif c:
                steps += [("out", c - 1, 0), ("out", c - 1, 1), ("softmax", u)] + jobs
            else:
                steps += jobs[:2] + [("softmax", u)] + jobs[2:]
            if k == 1 and not nxt:
                steps.append(("R",))
        q = four("q", nxt)
        steps += q[:2] + [("to keys", u)] + q[2:]
        if nxt:
            steps += [("own keys", nxt)] + four("kr", nxt)
        if nxt == 3 and following:
            steps.append(("next x",))
        steps.append(("values", u))
    steps += [("out", CHUNKS - 1, 0), ("out", CHUNKS - 1, 1)]
    return [s for step in steps for s in (step, NORM_AFTER.get(step)) if s]


def first_plan():
    four = range(4)
    return ([("v", 0, n) for n in four] + [("root", 1)] + [("feats", g) for g in range(3)] +
            [("k", 0, n) for n in four] + [("root", 2), ("logits", 0), ("logits", 1), ("R",)] + [("q", 0, n) for n in four])


class Banks:
    def __init__(self, steps, base, it=None, per_turn=None):
        self.order = [s for s in steps if s[0] in EMPTIED_BY]
        self.base, self.it, self.per_turn = base, it, per_turn
        self.count = {"full": 0, "act": 0, "dve": 0}
        self.nth = {}
        for job in self.order:
            who = EMPTIED_BY[job[0]]
            self.nth[job] = (self.count["full"], self.count[who])
            self.count["full"] += 1
            self.count[who] += 1

    def value(self, which, n):
        v = self.base[which] + n
        return v if self.it is None else self.it * self.per_turn[which] + v

    def total(self):
        return {k: self.base[k] + self.count[k] for k in self.base}


def attention_block(nc, ctx, x_sb, ident, vecs, w_gate, base_dram, A):
    def sb(name, cols, dt=F32):
        return ctx.enter_context(nc.sbuf_tensor(name, [P, cols], dt))

    def psum(name, cols):
        return ctx.enter_context(nc.psum_tensor(name, [P, cols], F32))

    def sem(name):
        return ctx.enter_context(nc.semaphore(name))

    w_qkv = sb("w_qkv", 3 * 1024)
    w_out = sb("w_out", 8 * D)
    sort_w = sb("sort_w", SORT_HEADS * BUCKETS)
    bias_out = sb("bias_out", D)
    xn_t = sb("xn_t", (TURNS - 1) * TOK)
    xn_cur = sb("xn_cur", TOK)
    xsum_cur = sb("xsum_cur", P)
    r_blk = sb("r_blk", SORT_HEADS * P)
    r_t = sb("r_t", 4 * P)
    v_nat = sb("v_nat", W * 256)
    k_nat = sb("k_nat", W * 256)
    v_re = sb("v_re", W * 256)
    feats_t = v_re
    k_t = sb("k_t", 2 * TOK)
    keys_t = sb("keys_t", 2 * 16 * P)
    keys_loc = sb("keys_loc", 4 * PAD)
    q_diag = sb("q_diag", 4 * TOK)
    vals = [sb(f"vals{i}", 16 * 256) for i in range(2)]
    att_t = sb("att_t", 2 * TOK)
    s_masked = sb("s_masked", GROUPS * HALF_WIDE)
    r_exp = sb("r_exp", SORT_HEADS * BUCKETS)
    p_t = [sb(f"p_t{i}", GROUPS * P) for i in range(2)]
    mask_half = sb("mask_half", HALF)
    mask_sort = sb("mask_sort", 64)
    mask_half_loc = sb("mask_half_loc", HALF_WIDE)
    mask_loc = sb("mask_loc", WIDE)
    edge = sb("edge", GROUPS * 24)
    shifted = sb("shifted", GROUPS * 24)
    probs = sb("probs", GROUPS * 24)
    p_wide = sb("p_wide", GROUPS * P)
    stat = sb("stat", 3 * GROUPS)
    rstat = sb("rstat", 3 * 16)
    bn = sb("bn", 6 * PART)
    ln_small = sb("ln_small", 5 * PART)
    y_tmp = sb("y_tmp", PART * D)
    base_tmp = sb("base_tmp", PART // 2 * D)
    xn_nat = vals[1]

    work = psum("work", 1024)
    ps_s = psum("ps_s", 1024)
    ps_e = psum("ps_e", 1024)
    ps_o = psum("ps_o", 512)

    x_loaded = [sem(f"x_loaded{i}") for i in range(TURNS)]
    w_qkv_loaded = sem("w_qkv_loaded")
    sort_loaded = sem("sort_loaded")
    out_loaded = sem("out_loaded")
    ffn_loaded = sem("ffn_loaded")
    ident_ready = sem("ident_ready")
    consts_ready = sem("consts_ready")
    pool_chain = sem("pool_chain")
    norm_chain = sem("norm_chain")
    ffn_var = sem("ffn_var")
    ffn_root = sem("ffn_root")
    y_ready = sem("y_ready")
    base_ready = sem("base_ready")
    base_stored = sem("base_stored")
    var_ready = sem("var_ready")
    root_ready = sem("root_ready")
    xn_ready = sem("xn_ready")
    xt_full = sem("xt_full")
    xt_done = sem("xt_done")
    x_biased = sem("x_biased")
    cur_ready = sem("cur_ready")
    xsum_ready = sem("xsum_ready")
    dve_chain = sem("dve_chain")
    work_full = sem("work_full")
    work_act = sem("work_act")
    work_dve = sem("work_dve")
    r_link = sem("r_link")
    r_exped = sem("r_exped")
    r_ready = sem("r_ready")
    own_loaded = sem("own_loaded")
    mixed_loaded = sem("mixed_loaded")
    loc_loaded = sem("loc_loaded")
    keys_copied = sem("keys_copied")
    s_full = sem("s_full")
    s_done = sem("s_done")
    picked = sem("picked")
    edge_done = sem("edge_done")
    max_done = sem("max_done")
    shifted_ready = sem("shifted_ready")
    exped = sem("exped")
    sum_done = sem("sum_done")
    inv_done = sem("inv_done")
    p_ready = sem("p_ready")
    p_spread = sem("p_spread")
    p_spread_dve = sem("p_spread_dve")
    e_full = sem("e_full")
    e_done = sem("e_done")
    o_full = sem("o_full")
    o_done = sem("o_done")

    xg = x_sb[:, :].rearrange("p (t r) -> p t r", r=ROW)[:, PART:, 0:D]

    def x_tiles(block, t, n):
        cols = x_sb[:, bass.ds(block * BLOCK + t * ROW, n * ROW)]
        return cols.rearrange("p (t r) -> p t r", r=ROW)[:, :, 0:D]


    FIRST, TURN, LAST = first_plan(), plan(range(CHUNKS), True), plan(range(CHUNKS), False)
    before_first = {"full": 0, "act": 0, "dve": 0}
    before_turns = Banks(FIRST, before_first).total()
    per_turn = Banks(TURN, before_first).count

    def first_banks():
        return Banks(FIRST, before_first)

    def turn_banks(it):
        return Banks(TURN, before_turns, it, per_turn)

    def last_banks():
        return Banks(LAST, {k: before_turns[k] + (TURNS - 1) * per_turn[k] for k in per_turn})

    def spread(engine, u, g0, g1):
        if u < 4:
            shape, src, m = (g1 - g0, 4, 24), [[24, g1 - g0], [0, 4], [1, 24]], (mask_loc, [[0, g1 - g0], [24, 4], [1, 24]])
            n, k = WIDE, 24
        else:
            a = 2 * (g1 - g0)
            shape, src, m = (a, W, W), [[W, a], [0, W], [1, W]], (mask_sort, [[0, a], [W, W], [1, W]])
            n, k = P, 16
        return engine.tensor_tensor(p_wide[:, g0 * n:g1 * n].rearrange("p (a m b) -> p a m b", m=shape[1], b=shape[2]),
                                    view(probs, 0, P, g0 * k, src), view(m[0], 0, P, 0, m[1]), ALU.mult)

    def full(eng, banks, job):
        eng.wait_ge(work_full, banks.value("full", banks.nth[job][0] + 1))

    def emptied(eng, banks, job):
        who = EMPTIED_BY[job[0]]
        eng.wait_ge(work_act if who == "act" else work_dve, banks.value(who, banks.nth[job][1] + 1))

    def bank(banks, job):
        o = banks.nth[job][0] % 2 * 512
        return work[:, o:o + 512]

    block = ctx.enter_context(nc.Block())

    @block.sync
    def _(sp):
        xd = A["x"].rearrange("b (t p) d -> p (b t) d", p=P)

        def load_x(i):
            sp.dma_start(xg[:, PART * i:PART * (i + 1), :], xd[:, PART * i:PART * (i + 1), :]).then_inc(x_loaded[i], 16)

        load_x(0)
        sp.dma_start(w_qkv[:, 1024:3072], A["w_kv"]).then_inc(w_qkv_loaded, 16)
        sp.dma_start(w_qkv[:, 0:1024], A["w_q"]).then_inc(w_qkv_loaded, 16)
        load_x(1)
        sp.dma_start(sort_w[:, :].rearrange("p (h v) -> p h v", h=SORT_HEADS),
                     A["sort_w"].rearrange("a h d v -> d (a h) v")).then_inc(sort_loaded, 16)
        load_x(2)
        load_x(3)
        sp.dma_start(bias_out[:, :], A["b_out"].rearrange("(a d) -> a d", a=1).to_broadcast([P, D])).then_inc(out_loaded, 16)
        sp.dma_start(w_out[:, :].rearrange("p (n d) -> p n d", n=8),
                     A["w_out"].rearrange("(n p) d -> p n d", p=P)).then_inc(out_loaded, 16)

        sp.dma_start(vecs[0:ROW_RB1, :], A["inter_b"].rearrange("e (c p) -> (e c) p", p=P)).then_inc(ffn_loaded, 16)
        sp.dma_start(vecs[ROW_RB1:ROW_NW, :], A["res_inter_b"].rearrange("(c p) -> c p", p=P)).then_inc(ffn_loaded, 16)
        sp.dma_start(vecs[ROW_NW:ROW_NB, :], A["attn_nw"].rearrange("(a p) -> a p", a=1)).then_inc(ffn_loaded, 16)
        sp.dma_start(vecs[ROW_NB:VEC, :], A["attn_nb"].rearrange("(a p) -> a p", a=1)).then_inc(ffn_loaded, 16)
        sp.dma_start(w_gate[:, 0:EXPERTS], A["wg"]).then_inc(ffn_loaded, 16)
        sp.dma_start(w_gate[:, EXPERTS:EXPERTS + 2], A["res_coef"]).then_inc(ffn_loaded, 16)

        def local_values(banks):
            emptied(sp, banks, ("v", 0, 3))
            for b in range(2):
                for g in range(GROUPS):
                    lo = 1 if g == 0 else 0
                    hi = 9 if g == GROUPS - 1 else 10
                    src = BUCKETS * b + GROUPS * g - 1
                    sp.dma_start(view(vals[0], lo * W, (hi - lo) * W, (b * GROUPS + g) * 256, [[1, 256]]),
                                 view(v_nat, src + lo, hi - lo, 0, [[256, W], [1, 256]])).then_inc(loc_loaded, 16)

        def turn(it, banks, following):
            for c in range(1, CHUNKS):
                emptied(sp, banks, ("v", c, 3))
                for g in range(16):
                    sp.dma_start(view(vals[c % 2], 0, 64, g * 256, [[1, 256]]),
                                 view(v_nat, 8 * g, 8, 0, [[256, W], [1, 256]])).then_inc(own_loaded, 16)
                if c == 2:
                    for h in range(2):
                        sp.wait_ge(base_ready, it * 2 + (h + 1))
                        sp.dma_start(base_dram[bass.ds(it, 1), :, h * 512:h * 512 + 512].rearrange("a p d -> p (a d)"),
                                     base_tmp[:, :]).then_inc(base_stored, 16)
                emptied(sp, banks, ("vr", c, 3))
                for g in range(16):
                    sp.dma_start(view(vals[c % 2], 64, 64, g * 256, [[1, 256]]),
                                 view(v_re, 8 * g, 8, 0, [[256, W], [1, 256]])).then_inc(mixed_loaded, 16)
            if following:
                local_values(banks)

        sp.wait_ge(consts_ready, 1)
        local_values(first_banks())
        with sp.Fori(0, TURNS - 1) as it:
            turn(it, turn_banks(it), True)
        turn(TURNS - 1, last_banks(), False)
        sp.wait_ge(base_stored, 32 * TURNS)
        sp.wait_ge(ffn_loaded, 96)

    @block.gpsimd
    def _(pool):
        done = [0]

        def link(ins):
            done[0] += 1
            ins.then_inc(pool_chain, 1)
            pool.wait_ge(pool_chain, done[0])

        link(nc.gpsimd.memset(ident[:, :], 0.0))
        nc.gpsimd.affine_select(out=ident[:, :], in_=ident[:, :], compare_op=ALU.not_equal, fill=1.0,
                                base=0, pattern=[[-1, P]], channel_multiplier=1).then_inc(ident_ready, 1)
        nc.gpsimd.memset(x_sb[:, 0:BLOCK], 0.0)
        link(nc.gpsimd.memset(view(x_sb, 0, P, BLOCK + D, [[ROW, TILES], [1, ROW - D]]), 0.0))
        nc.gpsimd.iota(view(x_sb, 0, P, BLOCK + D, [[ROW, TILES]]).bitcast(I32), pattern=[[P, TILES]], base=0,
                       channel_multiplier=1)
        nc.gpsimd.memset(vals[0][:, :], 0.0)
        nc.gpsimd.memset(keys_loc[:, :], 0.0)
        nc.gpsimd.memset(r_blk[:, :], 0.0)
        nc.gpsimd.memset(q_diag[:, :], 0.0).then_inc(consts_ready, 1)
        for m in (mask_half, mask_sort, mask_half_loc, mask_loc):
            nc.gpsimd.memset(m[:, :], 1.0)
        link(nc.gpsimd.memset(edge[:, :], 0.0))
        for p0 in range(0, P, HALF):
            half = p0 // (2 * HALF)
            for m, buckets, a in ((mask_half, 1, 0), (mask_sort, 1, 4 * half),
                                         (mask_half_loc, 3, half), (mask_loc, 3, 4 * half)):
                v = m[p0:p0 + HALF, :].rearrange("p (w t) -> p w t", t=W)
                n = v.shape[1]
                link(nc.gpsimd.affine_select(out=v, in_=v, compare_op=ALU.is_ge, fill=0.0, base=W - 1 - W * a,
                                             pattern=[[W, n], [0, W]], channel_multiplier=-1))
                link(nc.gpsimd.affine_select(out=v, in_=v, compare_op=ALU.is_ge, fill=0.0, base=W * (a + buckets - 1),
                                             pattern=[[-W, n], [0, W]], channel_multiplier=1))
            if half == 0:
                v = edge[p0:p0 + HALF, 0:W]
                link(nc.gpsimd.affine_select(out=v, in_=v, compare_op=ALU.is_ge, fill=OUT_OF_SEQUENCE,
                                             base=-W, pattern=[[0, W]], channel_multiplier=1))
            else:
                v = edge[p0:p0 + HALF, 7 * 24:7 * 24 + W]
                link(nc.gpsimd.affine_select(out=v, in_=v, compare_op=ALU.is_ge, fill=OUT_OF_SEQUENCE,
                                             base=HALF - W - 1, pattern=[[0, W]], channel_multiplier=-1))
        nc.gpsimd.memset(stat[:, :], 0.0).then_inc(consts_ready, 1)
        pool.wait_ge(out_loaded, 32)
        for i in range(TURNS):
            pool.wait_ge(xn_ready, 2 * i + 2)
            xv = xg[:, PART * i:PART * (i + 1), :]
            nc.gpsimd.tensor_tensor(xv, xv, view(bias_out, 0, P, 0, [[0, PART], [1, D]]), ALU.add).then_inc(x_biased, 1)

        def turn(it, steps, banks):
            for step in steps:
                if step[0] == "next x":
                    full(pool, banks, ("q", 3, 3))
                    nc.gpsimd.tensor_copy(xn_cur[:, :], xn_t[:, bass.ds(it * TOK, TOK)]).then_inc(cur_ready, 1)
                elif step[0] == "ffn base":
                    h = step[1]
                    pool.wait_ge(y_ready, it + 1)
                    if h:
                        pool.wait_ge(base_stored, it * 32 + 16 * h)
                    nc.gpsimd.tensor_tensor(base_tmp[:, :].rearrange("p (t d) -> p t d", d=D), x_tiles(it, 4 * h, 4),
                                            y_tmp[:, h * 512:h * 512 + 512].rearrange("p (t d) -> p t d", d=D),
                                            ALU.add).then_inc(base_ready, 1)
                elif step[0] == "softmax":
                    u = step[1]
                    pool.wait_ge(p_ready, it * UNITS + (u + 1))
                    if u:
                        pool.wait_ge(e_full, it * UNITS + u)
                    if u == UNITS - 1:
                        pool.wait_ge(base_stored, it * 32 + 32)
                    spread(nc.gpsimd, u, 0, POOL_GROUPS).then_inc(p_spread, 1)

        with pool.Fori(0, TURNS - 1) as it:
            turn(it, TURN, turn_banks(it))
        turn(TURNS - 1, LAST, last_banks())

    @block.scalar
    def _(act):
        def root(i):
            act.wait_ge(var_ready, i + 1)
            nc.scalar.activation(ln_small[:, 2 * PART:3 * PART], ln_small[:, 4 * PART:5 * PART],
                                 ACT.Sqrt).then_inc(root_ready, 1)

        def transposed(n):
            act.wait_ge(xt_full, n + 1)
            dst = xn_cur[:, n * 512:n * 512 + 512] if n < 2 else xn_t[:, (n - 2) * 512:(n - 1) * 512]
            nc.scalar.copy(dst, work[:, (n % 2) * 512:(n % 2) * 512 + 512]).then_inc(xt_done, 1)

        def turn(it, steps, banks):
            def empty(job, dst, src):
                full(act, banks, job)
                nc.scalar.copy(dst, src).then_inc(work_act, 1)

            for step in steps:
                kind = step[0]
                if kind == "root":
                    root(step[1])
                elif kind == "ffn root":
                    act.wait_ge(ffn_var, it * 2 + (step[1] + 1))
                    nc.scalar.activation(ln_small[:, 2 * PART:3 * PART], ln_small[:, 4 * PART:5 * PART],
                                         ACT.Sqrt).then_inc(ffn_root, 1)
                elif kind == "feats":
                    if step[1] == 0 and steps is TURN:
                        act.wait_ge(mixed_loaded, it * 768 + 768)
                    g = step[1]
                    empty(step, feats_t[:, g * 512:g * 512 + 512], bank(banks, step))
                elif kind == "R":
                    emptied(act, banks, ("logits", 1))
                    nc.scalar.activation(r_exp[:, :], r_exp[:, :], ACT.Exp).then_inc(r_exped, 1)
                elif kind == "v":
                    c, n = step[1:]
                    if n == 0:
                        if c == 1:
                            act.wait_ge(loc_loaded, it * 256 + 256)
                        elif steps is not FIRST:
                            act.wait_ge(own_loaded, it * 768 + 256 * ((c - 1) % CHUNKS))
                    empty(step, v_nat[:, n * 512:n * 512 + 512], bank(banks, step))
                elif kind == "k":
                    c, n = step[1:]
                    pp, b = divmod(n, 2)
                    o = (pp * 2 + b) * PAD + W
                    if c == 0 and n == 0:
                        act.wait_ge(consts_ready, 1)
                    empty(step, k_t[:, n * 512:n * 512 + 512] if c else keys_loc[:, o:o + SEQ], bank(banks, step))
                elif kind == "rt":
                    empty(step, r_t[:, :], bank(banks, step))
                elif kind == "q":
                    c, n = step[1:]
                    full(act, banks, step)
                    src = bank(banks, step)
                    for j in range(2):
                        ins = nc.scalar.copy(view(q_diag, 64 * j, 64, n * 1024 + j * HALF, [[64, 2 * GROUPS], [1, HALF]]),
                                             src[64 * j:64 * j + 64, :].rearrange("p (g q) -> p g q", q=HALF))
                    ins.then_inc(work_act, 1)
                elif kind == "kn":
                    c, n = step[1:]
                    empty(step, k_nat[:, n * 512:n * 512 + 512], bank(banks, step))
                elif kind == "vr":
                    c, n = step[1:]
                    if c > 1 and n == 0:
                        act.wait_ge(mixed_loaded, it * 768 + 256 * (c - 1))
                    empty(step, view(v_re, 0, P, n * 64, [[256, W], [1, 64]]),
                          bank(banks, step).rearrange("p (t d) -> p t d", t=W))
                elif kind == "softmax":
                    u = step[1]
                    n = GROUPS * (24 if u < 4 else 16)
                    act.wait_ge(shifted_ready, it * UNITS + (u + 1))
                    nc.scalar.activation(shifted[:, 0:n], shifted[:, 0:n], ACT.Exp,
                                         scale=1.0 if u < 4 else DH ** -0.5).then_inc(exped, 1)
                elif kind == "to keys":
                    u = step[1]
                    n = WIDE if u < 4 else P
                    act.wait_ge(e_full, it * UNITS + (u + 1))
                    nc.scalar.copy(p_t[u % 2][0:n, :], ps_e[0:n, :]).then_inc(e_done, 1)
                elif kind == "values":
                    u = step[1]
                    c, pp, b = u // 4, u // 2 % 2, u % 2
                    if u % 4 == 0 and c:
                        full(act, banks, ("out", c - 1, 1))
                    act.wait_ge(o_full, it * UNITS + (u + 1))
                    nc.scalar.copy(att_t[:, pp * TOK + b * SEQ:pp * TOK + (b + 1) * SEQ], ps_o[:, :]).then_inc(o_done, 1)

        root(0)
        for n in range(2):
            transposed(n)
        turn(-1, FIRST, first_banks())
        root(3)
        for n in range(2, TILES // 4):
            transposed(n)
        with act.Fori(0, TURNS - 1) as it:
            turn(it, TURN, turn_banks(it))
        turn(TURNS - 1, LAST, last_banks())

    @block.vector
    def _(dve):
        done = [0]

        def link(ins):
            done[0] += 1
            ins.then_inc(dve_chain, 1)
            dve.wait_ge(dve_chain, done[0])

        def normalise(i, part=None):
            if part != 1:
                dve.wait_ge(x_loaded[i], 16)
                layer_norm_stats(nc, link, lambda t: xg[:, PART * i + t, :], bn, ln_small, PART, 1e-5, var_ready)
            if part == 0:
                return
            dve.wait_ge(root_ready, i + 1)
            layer_norm_scale(nc, link, ln_small, PART)
            for half in range(2):
                t0 = PART * i + 4 * half
                layer_norm_rows(nc, ln_small[:, 4 * half:], lambda t: xn_nat[:, (t0 + t) * D:(t0 + t + 1) * D],
                                lambda t: xg[:, t0 + t, :], 4).then_inc(xn_ready, 1)
            dve.wait_ge(xn_ready, 2 * i + 2)

        def bucket_sums():
            nc.vector.tensor_reduce(xsum_cur[:, :], xn_cur[:, :].rearrange("p (b w) -> p b w", w=W), AX_X,
                                    ALU.add).then_inc(xsum_ready, 1)

        def turn(it, steps, banks):
            rmax, rsum, rinv = (rstat[:, 16 * k:16 * k + SORT_HEADS] for k in range(3))
            hs = [(0, 8), (8, 12)]
            R_LINKS = 4
            NORM_LINKS = 2 * (3 + 5) + 1

            def rlink(k, ins):
                ins.then_inc(r_link, 1)
                dve.wait_ge(r_link, it * R_LINKS + (R_LINKS + k + 1))

            def sort_matrix():
                lw = [bank(banks, ("logits", g))[:, 0:(b - a) * 64].rearrange("p (h v) -> p h v", v=BUCKETS)
                      for g, (a, b) in enumerate(hs)]
                full(dve, banks, ("logits", 0))
                nc.vector.tensor_reduce(rmax[:, 0:8], lw[0], AX_X, ALU.max)
                full(dve, banks, ("logits", 1))
                rlink(0, nc.vector.tensor_reduce(rmax[:, 8:12], lw[1], AX_X, ALU.max))
                rlink(1, nc.vector.tensor_scalar(rmax, rmax, 0.0, None, ALU.max))
                for g, (a, b) in enumerate(hs):
                    nc.vector.scalar_tensor_tensor(
                        r_exp[:, a * 64:b * 64].rearrange("p (h v) -> p h v", v=BUCKETS), lw[g], 0.0,
                        view(rstat, 0, P, a, [[1, b - a], [0, BUCKETS]]), ALU.max, ALU.subtract).then_inc(work_dve, 1)
                dve.wait_ge(r_exped, it + 2)
                re3 = r_exp[:, :].rearrange("p (h v) -> p h v", v=BUCKETS)
                rlink(2, nc.vector.tensor_reduce(rsum, re3, AX_X, ALU.add))
                rlink(3, nc.vector.reciprocal(rinv, rsum))
                for b in range(2):
                    nc.vector.tensor_tensor(
                        view(r_blk, 64 * b, 64, 64 * b, [[P, SORT_HEADS], [1, 64]]),
                        view(r_exp, 64 * b, 64, 0, [[64, SORT_HEADS], [1, 64]]),
                        view(rstat, 64 * b, 64, 32, [[1, SORT_HEADS], [0, 64]]), ALU.mult).then_inc(r_ready, 1)

            def shifted_scores(u):
                k = 24 if u < 4 else 16
                sv = shifted[:, 0:GROUPS * k]
                sv3 = sv.rearrange("p (g k) -> p g k", k=k)
                if u < 4:
                    wide = s_masked[:, :]
                    masked = wide.rearrange("p (g k) -> p g k", g=GROUPS)
                    scores = view(ps_s, 0, P, 0, [[P, GROUPS], [1, HALF_WIDE]])
                    mask = view(mask_half_loc, 0, P, 0, [[0, GROUPS], [1, HALF_WIDE]])
                    src, dst = wide.rearrange("p (g m k) -> p g k m", g=GROUPS, k=24), sv3
                else:
                    wide = s_masked[:, 0:GROUPS * 64]
                    masked = wide.rearrange("p (g s k) -> p g s k", g=GROUPS, s=2)
                    scores = view(ps_s, 0, P, 0, [[P, GROUPS], [HALF, 2], [1, HALF]])
                    mask = view(mask_half, 0, P, 0, [[0, GROUPS], [0, 2], [1, HALF]])
                    src, dst = wide.rearrange("p (a u t) -> p a t u", u=HALF // W, t=W), sv.rearrange("p (a t) -> p a t", t=W)
                dve.wait_ge(s_full, it * UNITS + (u + 1))
                nc.vector.tensor_tensor(masked, scores, mask, ALU.mult).then_inc(s_done, 1)
                dve.wait_ge(s_done, it * UNITS + (u + 1))
                nc.vector.tensor_reduce(dst, src, AX_X, ALU.add).then_inc(picked, 1)
                dve.wait_ge(picked, it * UNITS + (u + 1))
                if u < 4:
                    nc.vector.tensor_tensor(sv, sv, edge[:, :], ALU.add).then_inc(edge_done, 1)
                    dve.wait_ge(edge_done, it * 4 + (u + 1))
                nc.vector.tensor_reduce(stat[:, 0:GROUPS], sv3, AX_X, ALU.max).then_inc(max_done, 1)
                dve.wait_ge(max_done, it * UNITS + (u + 1))
                nc.vector.tensor_tensor(sv3, sv3, view(stat, 0, P, 0, [[1, GROUPS], [0, k]]),
                                        ALU.subtract).then_inc(shifted_ready, 1)

            def probabilities(u):
                k = 24 if u < 4 else 16
                sv3 = shifted[:, 0:GROUPS * k].rearrange("p (g k) -> p g k", k=k)
                dve.wait_ge(exped, it * UNITS + (u + 1))
                nc.vector.tensor_reduce(stat[:, GROUPS:2 * GROUPS], sv3, AX_X, ALU.add).then_inc(sum_done, 1)
                dve.wait_ge(sum_done, it * UNITS + (u + 1))
                nc.vector.reciprocal(stat[:, 2 * GROUPS:3 * GROUPS], stat[:, GROUPS:2 * GROUPS]).then_inc(inv_done, 1)
                dve.wait_ge(inv_done, it * UNITS + (u + 1))
                if u:
                    dve.wait_ge(p_spread, it * UNITS + u)
                nc.vector.tensor_tensor(probs[:, 0:GROUPS * k].rearrange("p (g k) -> p g k", k=k), sv3,
                                        view(stat, 0, P, 2 * GROUPS, [[1, GROUPS], [0, k]]), ALU.mult).then_inc(p_ready, 1)
                dve.wait_ge(p_ready, it * UNITS + (u + 1))
                if u:
                    dve.wait_ge(e_full, it * UNITS + u)
                spread(nc.vector, u, POOL_GROUPS, GROUPS).then_inc(p_spread_dve, 1)

            norm_links = [0]

            def norm_link(ins):
                norm_links[0] += 1
                ins.then_inc(norm_chain, 1)
                dve.wait_ge(norm_chain, it * NORM_LINKS + norm_links[0])

            def ffn_norm(part):
                def x(t):
                    return x_sb[:, bass.ds(it * BLOCK + t * ROW, D)]

                def y(t):
                    return y_tmp[:, t * D:t * D + D]

                if part == "x1":
                    layer_norm_stats(nc, norm_link, x, bn, ln_small, PART, 1e-5, ffn_var)
                elif part == "scale y":
                    dve.wait_ge(ffn_root, it * 2 + 1)
                    layer_norm_scale(nc, norm_link, ln_small, PART)
                elif part == "y":
                    layer_norm_rows(nc, ln_small, y, x, PART).then_inc(y_ready, 1)
                elif part == "of y":
                    dve.wait_ge(y_ready, it + 1)
                    layer_norm_stats(nc, norm_link, y, bn, ln_small, PART, 1e-12, ffn_var)
                elif part == "scale rows":
                    dve.wait_ge(ffn_root, it * 2 + 2)
                    layer_norm_scale(nc, norm_link, ln_small, PART)
                else:
                    dve.wait_ge(base_ready, it * 2 + 2)
                    norm_link(layer_norm_rows(nc, ln_small, x, y, PART))

            for step in steps:
                if step[0] == "R":
                    sort_matrix()
                elif step[0] == "ffn norm":
                    ffn_norm(step[1])
                elif step[0] == "scores":
                    shifted_scores(step[1])
                elif step[0] == "softmax":
                    probabilities(step[1])
                elif step[0] == "own keys":
                    emptied(dve, banks, ("k", step[1], 3))
                    nc.vector.tensor_copy(view(keys_t, 0, P, 0, [[P, 32], [1, 64]]),
                                          k_t[:, :].rearrange("p (g k) -> p g k", k=64)).then_inc(keys_copied, 1)
                elif step[0] == "kr":
                    c, n = step[1:]
                    pp, half = divmod(n, 2)
                    full(dve, banks, step)
                    nc.vector.tensor_copy(view(keys_t, 0, P, pp * 16 * P + 64 + half * 4, [[1, 4], [P, 16], [8, 8]]),
                                          bank(banks, step).rearrange("p (t g u) -> p t g u", t=4, g=16)).then_inc(work_dve, 1)
                elif step[0] == "next x":
                    dve.wait_ge(cur_ready, it + 1)
                    bucket_sums()
                elif step[0] == "out":
                    n = step[2]
                    full(dve, banks, step)
                    xs = x_tiles(it + 1, 4 * n, 4)
                    nc.vector.tensor_tensor(xs, xs, bank(banks, step).rearrange("p (t d) -> p t d", d=D),
                                            ALU.add).then_inc(work_dve, 1)

        normalise(0)
        dve.wait_ge(xt_done, 2)
        bucket_sums()
        normalise(1)
        normalise(2, 0)
        dve.wait_ge(consts_ready, 1)
        turn(-1, FIRST, first_banks())
        normalise(2, 1)
        normalise(3)
        dve.wait_ge(consts_ready, 2)
        dve.wait_ge(x_biased, TURNS)
        with dve.Fori(0, TURNS - 1) as it:
            turn(it, TURN, turn_banks(it))
        turn(TURNS - 1, LAST, last_banks())

    @block.tensor
    def _(pe):
        def transposed(n):
            pe.wait_ge(xn_ready, n + 1)
            if n > 2:
                pe.wait_ge(xt_done, n - 1)
            for t in range(4):
                T = 4 * n + t
                last = nc.tensor.transpose(work[:, (n % 2) * 512 + t * P:(n % 2) * 512 + t * P + P],
                                           xn_nat[:, T * D:T * D + D], ident[:, :])
            last.then_inc(xt_full, 1)

        def turn(it, steps, banks):
            def free_bank(job):
                n = banks.nth[job][0]
                if n >= 2:
                    emptied(pe, banks, banks.order[n - 2])
                elif n == 0 and steps is not FIRST:
                    pe.wait_ge(work_act, banks.value("act", 0))
                    pe.wait_ge(work_dve, banks.value("dve", 0))
                return bank(banks, job)

            def scores(u):
                c, pp, b = u // 4, u // 2 % 2, u % 2
                if u == 0:
                    pe.wait_ge(work_act, banks.value("act", 0))
                elif u % 4 == 0:
                    emptied(pe, banks, ("q", c, 3))
                    emptied(pe, banks, ("kr", c, 3))
                    pe.wait_ge(keys_copied, it * 3 + c)
                if u:
                    pe.wait_ge(s_done, it * UNITS + u)
                for g in range(GROUPS):
                    for half in range(2):
                        if c == 0:
                            n = HALF_WIDE
                            keys = view(keys_loc, 0, P, (pp * 2 + b) * PAD + g * 64 + half * 3 * W, [[1, n]])
                        else:
                            n = 64
                            keys = view(keys_t, 0, P, (pp * 16 + b * 8 + g) * P + half * HALF, [[64, 2], [1, HALF]])
                        o = (pp * 16 + b * 8 + g) * P + half * 64
                        last = nc.tensor.matmul(ps_s[64 * half:64 * half + 64, g * P:g * P + n], q_diag[:, o:o + 64], keys,
                                                start=True, stop=True)
                last.then_inc(s_full, 1)

            def to_keys(u):
                pe.wait_ge(p_spread, it * UNITS + (u + 1))
                pe.wait_ge(p_spread_dve, it * UNITS + (u + 1))
                if u:
                    pe.wait_ge(e_done, it * UNITS + u)
                n = WIDE if u < 4 else P
                for g in range(GROUPS):
                    last = nc.tensor.transpose(ps_e[0:n, g * P:g * P + P], p_wide[:, g * n:g * n + n], ident[:, :])
                last.then_inc(e_full, 1)

            def values(u):
                c, pp, b = u // 4, u // 2 % 2, u % 2
                if u == 0:
                    pe.wait_ge(loc_loaded, it * 256 + 256)
                elif u % 4 == 0:
                    pe.wait_ge(own_loaded, it * 768 + 256 * c)
                    pe.wait_ge(mixed_loaded, it * 768 + 256 * c)
                pe.wait_ge(e_done, it * UNITS + (u + 1))
                if u:
                    pe.wait_ge(o_done, it * UNITS + u)
                n = P if c else WIN
                for g in range(GROUPS):
                    for j in range(2):
                        o = (b * GROUPS + g) * 256 + (2 * pp + j) * 64
                        p = p_t[u % 2][0:n, g * P:(g + 1) * P].rearrange("k (h j q) -> k j h q", h=2, j=2)
                        last = nc.tensor.matmul(ps_o[64 * j:64 * j + 64, g * 64:g * 64 + 64], vals[c % 2][0:n, o:o + 64],
                                                p[:, j], start=True, stop=True)
                last.then_inc(o_full, 1)

            for step in steps:
                kind = step[0]
                if kind == "scores":
                    scores(step[1])
                elif kind == "to keys":
                    to_keys(step[1])
                elif kind == "values":
                    values(step[1])
                elif kind == "feats":
                    g = step[1]
                    if g == 0:
                        pe.wait_ge(xsum_ready, it + 2)
                    w = free_bank(step)
                    for h in range(4):
                        for part in range(2):
                            o = part * 1024 + (LOCAL_HEADS + 4 * g + h) * 64
                            last = nc.tensor.matmul(w[64 * part:64 * part + 64, h * P:h * P + P],
                                                    w_qkv[:, o:o + 64], xsum_cur[:, :], start=True, stop=True)
                    last.then_inc(work_full, 1)
                elif kind == "logits":
                    g = step[1]
                    if steps is FIRST:
                        pe.wait_ge(sort_loaded, 16)
                    w = free_bank(step)
                    emptied(pe, banks, ("feats", 2))
                    for h in range((8, 4)[g]):
                        hh = 8 * g + h
                        last = nc.tensor.matmul(w[:, h * 64:h * 64 + 64], feats_t[:, hh * P:hh * P + P],
                                                sort_w[:, hh * 64:hh * 64 + 64], start=True, stop=True)
                    last.then_inc(work_full, 1)
                elif kind == "v":
                    c, n = step[1:]
                    if c == 0 and n == 0 and steps is TURN:
                        pe.wait_ge(cur_ready, it + 1)
                    w = free_bank(step)
                    for h in range(2):
                        last = nc.tensor.matmul(w[:, h * 256:h * 256 + 256], view(xn_cur, 0, P, 2 * n + h, [[W, P]]),
                                                w_qkv[:, 2048 + c * 256:2048 + c * 256 + 256], start=True, stop=True)
                    last.then_inc(work_full, 1)
                elif kind in ("q", "k"):
                    c, n = step[1:]
                    pp, b = divmod(n, 2)
                    o = (1024 if kind == "k" else 0) + (2 * c + pp) * P
                    nc.tensor.matmul(free_bank(step), w_qkv[:, o:o + P], xn_cur[:, b * SEQ:(b + 1) * SEQ],
                                     start=True, stop=True).then_inc(work_full, 1)
                elif kind == "rt":
                    c = step[1]
                    if c == 1:
                        pe.wait_ge(r_ready, it * 2 + 2)
                    w = free_bank(step)
                    for h in range(4):
                        hh = 4 * (c - 1) + h
                        last = nc.tensor.transpose(w[:, h * P:h * P + P], r_blk[:, hh * P:hh * P + P], ident[:, :])
                    last.then_inc(work_full, 1)
                elif kind == "kn":
                    c, n = step[1:]
                    if n == 0:
                        emptied(pe, banks, ("k", c, 3))
                    w = free_bank(step)
                    for t in range(2):
                        for pp in range(2):
                            last = nc.tensor.transpose(w[:, t * 256 + pp * P:t * 256 + pp * P + P],
                                                       view(k_t, 0, P, pp * TOK + 2 * n + t, [[W, P]]), ident[:, :])
                    last.then_inc(work_full, 1)
                elif kind == "vr":
                    c, h = step[1:]
                    if h == 0:
                        emptied(pe, banks, ("rt", c))
                    nc.tensor.matmul(free_bank(step), r_t[:, h * P:h * P + P], view(v_nat, 0, P, h * 64, [[256, W], [1, 64]]),
                                     start=True, stop=True).then_inc(work_full, 1)
                elif kind == "kr":
                    c, n = step[1:]
                    pp, half = divmod(n, 2)
                    if n == 0:
                        emptied(pe, banks, ("kn", c, 3))
                    w = free_bank(step)
                    for t in range(4):
                        for j in range(2):
                            h = 2 * pp + j
                            o = (4 * half + t) * 256 + h * 64
                            last = nc.tensor.matmul(w[64 * j:64 * j + 64, t * P:t * P + P], k_nat[:, o:o + 64],
                                                    r_t[:, h * P:h * P + P], start=True, stop=True)
                    last.then_inc(work_full, 1)
                elif kind == "out":
                    c, n = step[1:]
                    if n == 0:
                        pe.wait_ge(o_done, it * UNITS + (4 * c + 4))
                    w = free_bank(step)
                    for t in range(4):
                        for pp in range(2):
                            o = pp * TOK + (4 * n + t) * P
                            last = nc.tensor.matmul(w[:, t * P:t * P + P], att_t[:, o:o + P],
                                                    w_out[:, (2 * c + pp) * D:(2 * c + pp) * D + D],
                                                    start=(pp == 0), stop=(pp == 1))
                    last.then_inc(work_full, 1)

        pe.wait_ge(ident_ready, 1)
        for n in range(2):
            transposed(n)
        pe.wait_ge(w_qkv_loaded, 32)
        pe.wait_ge(xt_done, 2)
        turn(-1, FIRST, first_banks())
        totals = first_banks().total()
        pe.wait_ge(work_act, totals["act"])
        for n in range(2, TILES // 4):
            transposed(n)
        pe.wait_ge(xt_done, TILES // 4)
        pe.wait_ge(out_loaded, 32)
        with pe.Fori(0, TURNS - 1) as it:
            turn(it, TURN, turn_banks(it))
        turn(TURNS - 1, LAST, last_banks())


def feed_forward_block(nc, ctx, x_sb, ident, vecs, w_gate, base_dram, A, out):
    def sb(name, cols, dt=F32):
        return ctx.enter_context(nc.sbuf_tensor(name, [P, cols], dt))

    def psum(name, cols):
        return ctx.enter_context(nc.psum_tensor(name, [P, cols], F32))

    def sem(name):
        return ctx.enter_context(nc.semaphore(name))

    E = EXPERTS
    CH = INTER // P
    SLOTS = E * CAP
    TOKENS = TILES * P
    GRP = TOKENS // 512

    acc = sb("acc", TOKENS)
    moe_sb = sb("moe_sb", TOKENS)
    y = sb("y", PART * D)
    a_t = sb("a_t", TOKENS)
    blank = sb("blank", SLOTS // P * ROW)
    res_w1 = sb("res_w1", INTER)
    res_w2 = sb("res_w2", CH * D)
    w1 = [sb(f"w1_{i}", INTER) for i in range(2)]
    w2 = [sb(f"w2_{i}", CH * D) for i in range(2)]
    b2 = sb("b2", E * D)
    res_b2 = sb("res_b2", D)
    cols = sb("cols", VEC)
    before = sb("before", P, BF16)
    ones = sb("ones", P, BF16)
    rank = sb("rank", E)
    first_slot = sb("first_slot", E)
    spare = sb("spare", TILES)
    bn = sb("bn_b", 6 * PART)
    ln_small = sb("ln_small_b", 5 * PART)
    gates = sb("gates", TILES * (E + 2))
    work1 = sb("work1", TILES * E)
    work2 = sb("work2", TILES * E)
    chosen = sb("chosen", TILES * E)
    chosen_bf = sb("chosen_bf", TILES * E, BF16)
    s = {n: sb(n, TILES) for n in ("gmax", "cmax", "gsum", "csum", "top", "first", "slot", "kept", "lost", "share")}
    slot_i = sb("slot_i", TILES, I32)
    counts_i = sb("counts_i", 2 * E, I32)
    h_t = [sb(f"h_t{i}", CH * 512) for i in range(2)]
    res = [sb(f"res{i}", 512) for i in range(2)]
    xe_all = sb("xe_all", E * CAP // P * ROW)
    xe = [sb(f"xe{i}", CAP) for i in range(2)]
    xe_t = [sb(f"xe_t{i}", CAP) for i in range(2)]
    eo = [sb(f"eo{i}", 512) for i in range(2)]

    disp = nc.dram_tensor("disp", (SLOTS + TOKENS, ROW), F32, kind="Internal").ap()
    moe = nc.dram_tensor("moe", (TOKENS + SLOTS, D), F32, kind="Internal").ap()

    ps_t = psum("ps_t", 1024)
    ps_h = psum("ps_h", 1024)
    ps_o = psum("ps_o_b", 1024)
    ps_g = psum("ps_g", 512)
    ps_l = psum("ps_l", 512)

    mlp_in = sem("mlp_in")
    blank_ready = sem("blank_ready")
    disp_blank = sem("disp_blank")
    moe_blank = sem("moe_blank")
    consts_ready = sem("consts_ready_b")
    eo_ready = sem("eo_ready")
    pool_chain = sem("pool_chain_b")
    dve_chain = sem("dve_chain_b")
    var_ready = sem("var_ready_b")
    root_ready = sem("root_ready_b")
    y_ready = sem("y_ready")
    base_ready = sem("base_ready")
    rows_ready = sem("rows_ready")
    vecs_full = sem("vecs_full")
    vecs_done = sem("vecs_done")
    t_full = sem("t_full")
    t_done = sem("t_done")
    g_full = sem("g_full")
    shift_ready = sem("shift_ready")
    exp_ready = sem("exp_ready")
    chosen_ready = sem("chosen_ready")
    l_full = sem("l_full")
    slots_ready = sem("slots_ready")
    scattered = sem("scattered")
    h_full = sem("h_full")
    h_done = sem("h_done")
    o_full = sem("o_full_b")
    o_done = sem("o_done_b")
    res_link = sem("res_link")
    base_in = sem("base_in")
    xe_loaded = [sem(f"xe_loaded{i}") for i in range(E)]
    w1_loaded = [sem(f"w1_loaded{i}") for i in range(2)]
    w2_loaded = [sem(f"w2_loaded{i}") for i in range(2)]
    xe_ready = sem("xe_ready")
    xt_full = sem("xt_full_b")
    xt_done = sem("xt_done_b")
    sent = [sem(f"sent{i}") for i in range(2)]
    moe_in = [sem(f"moe_in{i}") for i in range(4)]
    res_added = sem("res_added")
    BANKS = 2
    fin = sem("fin")
    stored = sem("stored")

    rg = x_sb[:, :].rearrange("p (t r) -> p t r", r=ROW)[:, PART:, :]
    x1g = rg[:, TILES - PART:, 0:D]
    yg = y[:, :].rearrange("p (t d) -> p t d", d=D)
    ag = acc[:, :].rearrange("p (t d) -> p t d", d=D)
    mg = moe_sb[:, :].rearrange("p (t d) -> p t d", d=D)
    gt = gates[:, :].rearrange("p (t e) -> p t e", e=E + 2)
    c_b1, c_rb1, c_nw, c_nb = 0, ROW_RB1, ROW_NW, ROW_NB
    GELU = ACT.Gelu_apprx_tanh

    def spread(name, n, off=0):
        return view(s[name], 0, P, off, [[1, TILES], [0, n]])

    block = ctx.enter_context(nc.Block())

    @block.sync
    def _(sp):
        sp.dma_start(res_w1[:, :], A["res_inter_w"]).then_inc(mlp_in, 16)
        sp.dma_start(res_w2[:, :].rearrange("p (c d) -> p c d", d=D),
                     A["res_output_w"].rearrange("(c p) d -> p c d", p=P)).then_inc(mlp_in, 16)
        sp.dma_start(res_b2[:, :], A["res_output_b"].rearrange("(a d) -> a d", a=1).to_broadcast([P, D])).then_inc(mlp_in, 16)
        sp.dma_start(b2[:, :], A["output_b"].rearrange("(a e) d -> a (e d)", a=1).to_broadcast([P, E * D])).then_inc(mlp_in, 16)
        sp.wait_ge(blank_ready, 1)
        sp.dma_start(disp[0:SLOTS, :].rearrange("(e p j) r -> p e (j r)", e=E, p=P),
                     blank[:, :].rearrange("p (e r) -> p e r", e=E)).then_inc(disp_blank, 16)
        sp.dma_start(moe[0:TOKENS, :].rearrange("(t p) d -> p t d", p=P),
                     view(blank, 0, P, 0, [[ROW, TILES], [1, D]])).then_inc(moe_blank, 16)
        sp.dma_start(acc[:, 0:(TURNS - 1) * TOK].rearrange("p (a d) -> p a d", d=TOK),
                     base_dram[1:TURNS].rearrange("a p d -> p a d")).then_inc(base_in, 16)

        def load_w1(e, i):
            sp.dma_start(w1[i][:, :], A["inter_w"][bass.ds(e, 1), :, :].rearrange("a p n -> (a p) n")).then_inc(w1_loaded[i], 16)

        def load_w2(e, i):
            sp.dma_start(w2[i][:, :].rearrange("p (c d) -> p c d", d=D),
                         A["output_w"][bass.ds(e, 1), :, :].rearrange("a (c p) d -> p (a c) d", p=P)).then_inc(w2_loaded[i], 16)

        for i in range(2):
            load_w1(i, i)
            load_w2(i, i)
        sp.wait_ge(scattered, 16 * TILES)
        for e in range(E):
            sp.dma_start(xe_all[:, e * CAP // P * ROW:(e + 1) * CAP // P * ROW],
                         disp[e * CAP:(e + 1) * CAP, :].rearrange("(p j) r -> p (j r)", p=P)).then_inc(xe_loaded[e], 16)
        with sp.Fori(0, E // 2 - 1) as turn:
            for i in range(2):
                sp.wait_ge(h_full, turn * (2 * CH) + (GRP * CH + CH * (i + 1)))
                load_w1(turn * 2 + (2 + i), i)
                sp.wait_ge(o_full, turn * 2 + (GRP + 1 + i))
                load_w2(turn * 2 + (2 + i), i)
        for i in range(2):
            sp.wait_ge(sent[i], 64 * (E // 2))
        for i in range(4):
            t = TILES // 4
            sp.dma_start(mg[:, t * i:t * i + t, :],
                         moe[t * P * i:t * P * (i + 1), :].rearrange("(t p) d -> p t d", p=P)).then_inc(moe_in[i], 16)
        for i in range(4):
            t = TILES // 4
            sp.wait_ge(fin, i + 1)
            sp.dma_start(out.rearrange("b (t p) d -> p (b t) d", p=P)[:, t * i:t * i + t, :],
                         ag[:, t * i:t * i + t, :]).then_inc(stored, 16)
        sp.wait_ge(stored, 64)

    @block.gpsimd
    def _(pool):
        done = [0]

        def link(ins):
            done[0] += 1
            ins.then_inc(pool_chain, 1)
            pool.wait_ge(pool_chain, done[0])

        nc.gpsimd.memset(before[:, :], 1.0)
        nc.gpsimd.memset(ones[:, :], 1.0)
        link(nc.gpsimd.memset(blank[:, :], 0.0))
        nc.gpsimd.iota(view(blank, 0, P, D, [[ROW * 4, E], [ROW, 4]]).bitcast(I32),
                       pattern=[[CAP, E], [1, 4]], base=TOKENS, channel_multiplier=4).then_inc(blank_ready, 1)
        nc.gpsimd.affine_select(out=before[:, :], in_=before[:, :], compare_op=ALU.is_gt, fill=0.0, base=0,
                                pattern=[[1, P]], channel_multiplier=-1)
        nc.gpsimd.iota(slot_i[:, :], pattern=[[P, TILES]], base=SLOTS, channel_multiplier=1)
        nc.gpsimd.iota(counts_i[:, 0:E], pattern=[[-1, E]], base=E, channel_multiplier=0)
        link(nc.gpsimd.iota(counts_i[:, E:2 * E], pattern=[[CAP, E]], base=0, channel_multiplier=0))
        nc.gpsimd.tensor_copy(spare[:, :], slot_i[:, :])
        nc.gpsimd.tensor_copy(rank[:, :], counts_i[:, 0:E])
        nc.gpsimd.tensor_copy(first_slot[:, :], counts_i[:, E:2 * E]).then_inc(consts_ready, 1)
        pool.wait_ge(slots_ready, 1)
        pool.wait_ge(disp_blank, 16)
        pool.wait_ge(rows_ready, 1)
        for t in range(TILES):
            nc.gpsimd.indirect_dma_start(out=disp[:, :], out_offset=bass.IndirectOffsetOnAxis(ap=slot_i[:, t:t + 1], axis=0),
                                         in_=rg[:, t, :], in_offset=None).then_inc(scattered, 16)
        pool.wait_ge(moe_blank, 16)
        for e in range(E):
            i = e % 2
            pool.wait_ge(eo_ready, e + 1)
            for j in range(4):
                nc.gpsimd.indirect_dma_start(
                    out=moe[:, :],
                    out_offset=bass.IndirectOffsetOnAxis(ap=view(xe_all, 0, P, (4 * e + j) * ROW + D, [[1, 1]]).bitcast(I32), axis=0),
                    in_=eo[i][:, j * D:j * D + D], in_offset=None).then_inc(sent[i], 16)

    def gelu_steps(act, base, i, bias, chunks=range(CH)):
        for c in chunks:
            act.wait_ge(h_full, base + (c + 1))
            nc.scalar.activation(h_t[i][:, c * 512:c * 512 + 512], ps_h[:, (c % 2) * 512:(c % 2) * 512 + 512], GELU,
                                 bias=bias(c)).then_inc(h_done, 1)

    @block.scalar
    def _(act):
        act.sem_inc(h_done, BANKS)

        def columns(groups):
            for n in groups:
                act.wait_ge(t_full, n + 1)
                nc.scalar.activation(a_t[:, n * 512:n * 512 + 512], ps_t[:, (n % 2) * 512:(n % 2) * 512 + 512],
                                     ACT.Identity, scale=cols[:, c_nw:c_nw + 1],
                                     bias=cols[:, c_nb:c_nb + 1]).then_inc(t_done, 1)

        act.wait_ge(vecs_full, 1)
        nc.scalar.copy(cols[:, :], ps_l[:, 0:VEC]).then_inc(vecs_done, 1)
        act.wait_ge(vecs_done, 1)
        columns(range(0, 2))
        for n in range(2):
            act.wait_ge(var_ready, n + 1)
            nc.scalar.activation(ln_small[:, 2 * PART:3 * PART], ln_small[:, 4 * PART:5 * PART],
                                 ACT.Sqrt).then_inc(root_ready, 1)
            if n == 0:
                columns(range(2, 6))

        def res_gelu(turn, i, chunks=range(CH)):
            gelu_steps(act, turn * (2 * CH) + CH * i, i, lambda c: cols[:, c_rb1 + c:c_rb1 + c + 1], chunks)

        res_gelu(0, 0, range(CH - 1))
        columns(range(6, GRP))
        res_gelu(0, 0, [CH - 1])
        res_gelu(0, 1)
        act.wait_ge(shift_ready, 1)
        nc.scalar.activation(gates[:, :], gates[:, :], ACT.Exp).then_inc(exp_ready, 1)
        with act.Fori(0, GRP // 2 - 1) as turn:
            for i in range(2):
                res_gelu(turn + 1, i)
        with act.Fori(0, E // 2) as turn:
            for i in range(2):
                act.wait_ge(xt_full, turn * 2 + (i + 1))
                nc.scalar.activation(xe_t[i][:, :], ps_t[:, i * 512:i * 512 + 512], ACT.Identity,
                                     scale=cols[:, c_nw:c_nw + 1], bias=cols[:, c_nb:c_nb + 1]).then_inc(xt_done, 1)
                gelu_steps(act, turn * (2 * CH) + (GRP * CH + CH * i), i,
                           lambda c: cols[:, bass.ds(turn * (2 * CH) + (i * CH + c), 1)])

    @block.vector
    def _(dve):
        done = [0]

        def link(ins):
            done[0] += 1
            ins.then_inc(dve_chain, 1)
            dve.wait_ge(dve_chain, done[0])

        dve.sem_inc(o_done, BANKS)
        layer_norm_stats(nc, link, lambda t: x1g[:, t, :], bn, ln_small, PART, 1e-5, var_ready)
        dve.wait_ge(root_ready, 1)
        layer_norm_scale(nc, link, ln_small, PART)
        link(layer_norm_rows(nc, ln_small, lambda t: yg[:, t, :], lambda t: x1g[:, t, :], PART))
        layer_norm_stats(nc, link, lambda t: yg[:, t, :], bn, ln_small, PART, 1e-12, var_ready)
        nc.vector.tensor_tensor(ag[:, TILES - PART:, :], x1g, yg, ALU.add).then_inc(base_ready, 1)
        dve.wait_ge(root_ready, 2)
        layer_norm_scale(nc, link, ln_small, PART)
        dve.wait_ge(base_ready, 1)
        layer_norm_rows(nc, ln_small, lambda t: x1g[:, t, :], lambda t: yg[:, t, :], PART).then_inc(rows_ready, 1)
        dve.wait_ge(consts_ready, 1)
        dve.wait_ge(g_full, 1)
        lg = ps_g[:, 0:TILES * (E + 2)].rearrange("p (t e) -> p t e", e=E + 2)
        nc.vector.tensor_reduce(s["gmax"][:, :], lg[:, :, 0:E], AX_X, ALU.max)
        link(nc.vector.tensor_reduce(s["cmax"][:, :], lg[:, :, E:E + 2], AX_X, ALU.max))
        nc.vector.tensor_tensor(gt[:, :, 0:E], lg[:, :, 0:E], spread("gmax", E), ALU.subtract)
        nc.vector.tensor_tensor(gt[:, :, E:E + 2], lg[:, :, E:E + 2], spread("cmax", 2), ALU.subtract).then_inc(shift_ready, 1)
        dve.wait_ge(exp_ready, 1)
        nc.vector.tensor_reduce(s["gsum"][:, :], gt[:, :, 0:E], AX_X, ALU.add)
        link(nc.vector.tensor_reduce(s["csum"][:, :], gt[:, :, E:E + 2], AX_X, ALU.add))
        nc.vector.reciprocal(s["gmax"][:, :], s["gsum"][:, :])
        link(nc.vector.reciprocal(s["cmax"][:, :], s["csum"][:, :]))
        nc.vector.tensor_tensor(gt[:, :, 0:E], gt[:, :, 0:E], spread("gmax", E), ALU.mult)
        link(nc.vector.tensor_tensor(gt[:, :, E:E + 2], gt[:, :, E:E + 2], spread("cmax", 2), ALU.mult))
        w1v = work1[:, :].rearrange("p (t e) -> p t e", e=E)
        w2v = work2[:, :].rearrange("p (t e) -> p t e", e=E)
        chv = chosen[:, :].rearrange("p (t e) -> p t e", e=E)
        link(nc.vector.tensor_reduce(s["top"][:, :], gt[:, :, 0:E], AX_X, ALU.max))
        link(nc.vector.tensor_tensor(w1v, gt[:, :, 0:E], spread("top", E), ALU.is_equal))
        link(nc.vector.tensor_tensor(w1v, w1v, view(rank, 0, P, 0, [[0, TILES], [1, E]]), ALU.mult))
        link(nc.vector.tensor_reduce(s["first"][:, :], w1v, AX_X, ALU.max))
        link(nc.vector.tensor_tensor(chv, w1v, spread("first", E), ALU.is_equal))
        nc.vector.tensor_copy(chosen_bf[:, :], chosen[:, :]).then_inc(chosen_ready, 1)
        dve.wait_ge(l_full, 1)
        loc = ps_l[:, 64:64 + TILES * E]
        locv = loc.rearrange("p (t e) -> p t e", e=E)
        nc.vector.scalar_tensor_tensor(work1[:, :], loc, float(CAP), chosen[:, :], ALU.is_lt, ALU.mult)
        link(nc.vector.tensor_tensor(w2v, locv, view(first_slot, 0, P, 0, [[0, TILES], [1, E]]), ALU.add))
        nc.vector.tensor_reduce(s["kept"][:, :], w1v, AX_X, ALU.add)
        link(nc.vector.tensor_tensor(work2[:, :], work2[:, :], work1[:, :], ALU.mult))
        nc.vector.tensor_reduce(s["slot"][:, :], w2v, AX_X, ALU.add)
        link(nc.vector.tensor_tensor(s["lost"][:, :], s["kept"][:, :], spare[:, :], ALU.mult))
        link(nc.vector.tensor_tensor(s["lost"][:, :], spare[:, :], s["lost"][:, :], ALU.subtract))
        nc.vector.tensor_tensor(slot_i[:, :], s["slot"][:, :], s["lost"][:, :], ALU.add)
        link(nc.vector.tensor_tensor(s["share"][:, :], s["top"][:, :], s["kept"][:, :], ALU.mult))
        nc.vector.tensor_tensor(rg[:, :, D + 1], s["share"][:, :], gt[:, :, E + 1], ALU.mult).then_inc(slots_ready, 1)
        link(nc.vector.tensor_copy(s["csum"][:, :], gt[:, :, E]))
        dve.wait_ge(base_in, 16)
        dve.wait_ge(mlp_in, 64)

        def add_residual(turn, i):
            rv = res[i][:, :].rearrange("p (t d) -> p t d", d=D)
            dve.wait_ge(o_full, turn * 2 + (i + 1))
            nc.vector.tensor_tensor(rv, ps_o[:, i * 512:i * 512 + 512].rearrange("p (t d) -> p t d", d=D),
                                    view(res_b2, 0, P, 0, [[0, 4], [1, D]]), ALU.add).then_inc(o_done, 1)
            dve.wait_ge(o_done, turn * 2 + (BANKS + i + 1))
            c0 = s["csum"][:, bass.ds(turn * 8 + 4 * i, 4)].unsqueeze(2).to_broadcast([P, 4, D])
            nc.vector.tensor_tensor(rv, rv, c0, ALU.mult).then_inc(res_link, 1)
            dve.wait_ge(res_link, turn * 2 + (i + 1))
            xs = acc[:, bass.ds(turn * 1024 + 512 * i, 512)]
            nc.vector.tensor_tensor(xs, xs, res[i][:, :], ALU.add).then_inc(res_added, 1)

        def stage(e, i):
            src = xe_all[:, bass.ds(e * (CAP // P * ROW), CAP // P * ROW)].rearrange("p (j r) -> p j r", r=ROW)
            nc.vector.tensor_copy(xe[i][:, :].rearrange("p (j d) -> p j d", d=D), src[:, :, 0:D]).then_inc(xe_ready, 1)

        def finish_rows(turn, i):
            ev = eo[i][:, :].rearrange("p (t d) -> p t d", d=D)
            dve.wait_ge(o_full, turn * 2 + (GRP + 1 + i))
            be = b2[:, bass.ds(turn * (2 * D) + i * D, D)].unsqueeze(1).to_broadcast([P, 4, D])
            nc.vector.tensor_tensor(ev, ps_o[:, i * 512:i * 512 + 512].rearrange("p (t d) -> p t d", d=D),
                                    be, ALU.add).then_inc(o_done, 1)
            dve.wait_ge(o_done, turn * 2 + (BANKS + GRP + i + 1))
            cols_e = xe_all[:, bass.ds(turn * (2 * CAP // P * ROW) + i * (CAP // P * ROW), CAP // P * ROW)]
            share = cols_e.rearrange("p (j r) -> p j r", r=ROW)[:, :, D + 1:D + 2].to_broadcast([P, CAP // P, D])
            nc.vector.tensor_tensor(ev, ev, share, ALU.mult).then_inc(eo_ready, 1)

        with dve.Fori(0, GRP // 2 - 1) as turn:
            for i in range(2):
                add_residual(turn, i)
        for i in range(2):
            dve.wait_ge(xe_loaded[i], 16)
            stage(i, i)
            add_residual(GRP // 2 - 1, i)
        for e in range(2, E):
            dve.wait_ge(xe_loaded[e], 16)

        def stage_after_next(turn, i):
            dve.wait_ge(xt_full, turn * 2 + (i + 1))
            stage(turn * 2 + (2 + i), i)

        for i in range(2):
            stage_after_next(0, i)
            finish_rows(0, i)
        with dve.Fori(0, E // 2 - 2) as turn:
            for i in range(2):
                stage_after_next(turn + 1, i)
                dve.wait_ge(sent[i], turn * 64 + 64)
                finish_rows(turn + 1, i)
        for i in range(2):
            dve.wait_ge(sent[i], 64 * (E // 2 - 1))
            finish_rows(E // 2 - 1, i)
        dve.wait_ge(res_added, GRP)
        for i in range(4):
            dve.wait_ge(moe_in[i], 16)
            part = acc[:, i * 1024:(i + 1) * 1024]
            nc.vector.tensor_tensor(part, part, moe_sb[:, i * 1024:(i + 1) * 1024], ALU.add).then_inc(fin, 1)

    @block.tensor
    def _(pe):
        def columns(groups):
            for n in groups:
                if n >= 2:
                    pe.wait_ge(t_done, n - 1)
                for t in range(4):
                    T = 4 * n + t
                    last = nc.tensor.transpose(ps_t[:, (n % 2) * 512 + t * P:(n % 2) * 512 + t * P + P], rg[:, T, 0:D],
                                               ident[:, :])
                last.then_inc(t_full, 1)

        def gate_logits(groups):
            for n in groups:
                pe.wait_ge(t_done, n + 1)
                for T in range(4 * n, 4 * n + 4):
                    last = nc.tensor.matmul(ps_g[:, T * (E + 2):(T + 1) * (E + 2)], a_t[:, T * P:T * P + P],
                                            w_gate[:, :], start=True, stop=True)
            return last

        nc.tensor.transpose(ps_l[:, 0:VEC], vecs[0:VEC, :], ident[0:VEC, 0:VEC]).then_inc(vecs_full, 1)
        columns(range(6))
        def inner(base, wa, moving, chunks=range(CH)):
            for c in chunks:
                pe.wait_ge(h_done, base + (c + 1))
                nc.tensor.matmul(ps_h[:, (c % 2) * 512:(c % 2) * 512 + 512], wa[:, c * P:c * P + P], moving,
                                 start=True, stop=True).then_inc(h_full, 1)

        def outer(base, passes, i, wb):
            pe.wait_ge(h_done, base + (BANKS + CH))
            pe.wait_ge(o_done, passes + 1)
            for j in range(4):
                for c in range(CH):
                    last = nc.tensor.matmul(ps_o[:, i * 512 + j * D:i * 512 + j * D + D],
                                            h_t[i][:, c * 512 + j * P:c * 512 + j * P + P],
                                            wb[:, c * D:c * D + D], start=(c == 0), stop=(c == CH - 1))
            last.then_inc(o_full, 1)

        def res_inner(turn, i):
            inner(turn * (2 * CH) + CH * i, res_w1, a_t[:, bass.ds(turn * 1024 + 512 * i, 512)])

        def res_outer(turn, i):
            outer(turn * (2 * CH) + CH * i, turn * 2 + i, i, res_w2)

        def expert_inner(turn, i):
            pe.wait_ge(w1_loaded[i], turn * 16 + 16)
            pe.wait_ge(xt_done, turn * 2 + (i + 1))
            inner(turn * (2 * CH) + (GRP * CH + CH * i), w1[i], xe_t[i][:, :])

        def expert_columns(turn, i):
            pe.wait_ge(xe_ready, turn * 2 + (i + 1))
            for j in range(4):
                last = nc.tensor.transpose(ps_t[:, i * 512 + j * P:i * 512 + j * P + P], xe[i][:, j * D:j * D + D],
                                           ident[:, :])
            last.then_inc(xt_full, 1)

        def expert_outer(turn, i):
            pe.wait_ge(w2_loaded[i], turn * 16 + 16)
            outer(turn * (2 * CH) + (GRP * CH + CH * i), turn * 2 + (GRP + i), i, w2[i])

        pe.wait_ge(mlp_in, 64)
        for c in range(CH):
            if c == CH - 1:
                pe.wait_ge(rows_ready, 1)
                columns(range(6, 8))
            inner(0, res_w1, a_t[:, 0:512], [c])
            last = gate_logits(range(2 * c, 2 * c + 2))
        last.then_inc(g_full, 1)
        inner(CH, res_w1, a_t[:, 512:1024])
        res_outer(0, 0)
        res_inner(1, 0)
        pe.wait_ge(chosen_ready, 1)
        nc.tensor.matmul(ps_l[:, 64:64 + TILES * E], before[:, :], chosen_bf[:, :], start=True, stop=False)
        for k in range(1, TILES):
            last = nc.tensor.matmul(ps_l[:, 64 + k * E:64 + TILES * E], ones[:, :], chosen_bf[:, 0:(TILES - k) * E],
                                    start=False, stop=(k == TILES - 1))
        last.then_inc(l_full, 1)
        res_outer(0, 1)
        with pe.Fori(0, GRP // 2 - 2) as turn:
            res_inner(turn + 1, 1)
            res_outer(turn + 1, 0)
            res_inner(turn + 2, 0)
            res_outer(turn + 1, 1)
        last_turn = GRP // 2 - 1
        res_inner(last_turn, 1)
        res_outer(last_turn, 0)
        expert_columns(0, 0)
        res_outer(last_turn, 1)
        expert_inner(0, 0)
        expert_columns(0, 1)
        with pe.Fori(0, E // 2 - 1) as turn:
            expert_inner(turn, 1)
            expert_columns(turn + 1, 0)
            expert_outer(turn, 0)
            expert_inner(turn + 1, 0)
            expert_columns(turn + 1, 1)
            expert_outer(turn, 1)
        last_turn = E // 2 - 1
        expert_inner(last_turn, 1)
        expert_outer(last_turn, 0)
        expert_outer(last_turn, 1)


_INS = ['x', 'w_q', 'w_kv', 'w_out', 'b_out', 'sort_w']
_FFN = ['attn_nw', 'attn_nb', 'wg', 'inter_w', 'inter_b', 'output_w', 'output_b', 'res_inter_w', 'res_inter_b',
        'res_output_w', 'res_output_b', 'res_coef']


def program(nc, A, out):
    with ExitStack() as outer:
        x_sb = outer.enter_context(nc.sbuf_tensor("x_sb", [P, (TURNS + 1) * BLOCK], F32))
        ident = outer.enter_context(nc.sbuf_tensor("ident", [P, P], F32))
        vecs = outer.enter_context(nc.sbuf_tensor("vecs", [P, D], F32))
        w_gate = outer.enter_context(nc.sbuf_tensor("w_gate", [P, EXPERTS + 2], F32))
        base_dram = nc.dram_tensor("base", (TURNS, P, PART * D), F32, kind="Internal").ap()
        with ExitStack() as ctx:
            attention_block(nc, ctx, x_sb, ident, vecs, w_gate, base_dram, A)
        with ExitStack() as ctx:
            feed_forward_block(nc, ctx, x_sb, ident, vecs, w_gate, base_dram, A, out)


def kernel(**inputs):
    import numpy as _np
    import concourse.bacc as _bacc
    from concourse import mybir as _mybir
    from concourse.bass_utils import run_bass_kernel_spmd as _run

    nc = _bacc.Bacc("TRN2", target_bir_lowering=False, num_devices=1)
    arrays, args = {}, {}
    for prefix, names in (("L0_attn_", _INS), ("L0_ffn_", _FFN)):
        for name in names:
            a = _np.ascontiguousarray(inputs[prefix + name])
            arrays[f"in_{name}_dram"] = a
            args[name] = nc.dram_tensor(f"in_{name}_dram", a.shape, _mybir.dt.from_np(a.dtype), kind="ExternalInput").ap()
    out = nc.dram_tensor("out_0_dram", (8, SEQ, D), _mybir.dt.float32, kind="ExternalOutput").ap()
    program(nc, args, out)
    r = _run(nc, [arrays], core_ids=[0])
    return r.results[0]["out_0_dram"]
```
